# Optimizing a Trainium2 kernel written in Bass

```python
import numpy as np
import jax
import jax.numpy as jnp

def _softmax(x, axis=-1):
    return jax.nn.softmax(x, axis=axis)

def _gelu(x):
    return jax.nn.gelu(x, approximate=True)

def _silu(x):
    return jax.nn.silu(x)

def _sigmoid(x):
    return jax.nn.sigmoid(x)

def _layernorm(x, axis=-1, eps=1e-05):
    m = jnp.mean(x, axis=axis, keepdims=True)
    v = jnp.var(x, axis=axis, keepdims=True)
    return (x - m) / jnp.sqrt(v + eps)

def _scatter_add(tgt, idx, src, axis=0):
    return tgt.at[idx].add(src)

def _segment_sum(src, seg, n):
    return jax.ops.segment_sum(src, seg, n)
kernel_name = 'mk_perceiver_d1_seqx_r4_2c4d3d'

def setup_inputs(seed: int=0):
    np.random.seed(seed)
    _w = jnp.asarray

    def _rec_inputs():
        import jax
        import jax.numpy as jnp
        _rk = jax.random.key(seed)
        x = 7.22e-05 + 1 * jax.random.normal(jax.random.fold_in(_rk, 1), (32, 64, 256), jnp.float32)
        _lenS = 64 - jax.random.randint(jax.random.fold_in(_rk, 7), (32,), 0, max(1, 64 // 4) + 1, jnp.int32)
        _lenS2 = 1601 - jax.random.randint(jax.random.fold_in(_rk, 8), (32,), 0, max(1, 1601 // 4) + 1, jnp.int32)
        _ctx_1024P = jax.random.normal(jax.random.fold_in(_rk, 11), (32, 16, 256), jnp.float32)
        _ctx_1024c = jax.random.dirichlet(jax.random.fold_in(_rk, 511), 0.3 * jnp.ones((16,), jnp.float32), (32, 1601))
        _ctx_1024t = jnp.einsum('bsk,bkd->bsd', _ctx_1024c, _ctx_1024P)
        _ctx_1024t = _ctx_1024t * jax.lax.rsqrt(jnp.mean(jnp.square(_ctx_1024t)) + 1e-12) * 0.953939
        ctx_1024 = 4.13588e-05 + 0.999923 * (_ctx_1024t + 0.3 * jax.random.normal(jax.random.fold_in(_rk, 611), (32, 1601, 256), jnp.float32))
        fside_1x16xSxS2_0 = 8.74812e-05 + 1.00005 * jax.random.normal(jax.random.fold_in(_rk, 12), (1, 16, 64, 1601), jnp.float32)
        return (x, ctx_1024, fside_1x16xSxS2_0)
    x, ctx_1024, fside_1x16xSxS2_0 = _rec_inputs()

    def _L0_xattn_setup():
        import jax, jax.numpy as jnp
        import numpy as np
        D_MODEL = 256
        N_HEADS = 16
        HEAD_DIM = D_MODEL // N_HEADS
        key = jax.random.key(seed)
        ks = jax.random.split(key, 12)
        b, lq, lk = (4, 512, 512)
        inputs_q = jax.random.normal(ks[0], (b, lq, D_MODEL), dtype=jnp.float32)
        inputs_kv = jax.random.normal(ks[1], (b, lk, D_MODEL), dtype=jnp.float32)
        bias = jax.random.normal(ks[2], (1, N_HEADS, lq, lk), dtype=jnp.float32)
        s_in = 1.0 / np.sqrt(D_MODEL)
        wq = jax.random.normal(ks[3], (D_MODEL, N_HEADS, HEAD_DIM), dtype=jnp.float32) * s_in
        wk = jax.random.normal(ks[4], (D_MODEL, N_HEADS, HEAD_DIM), dtype=jnp.float32) * s_in
        wv = jax.random.normal(ks[5], (D_MODEL, N_HEADS, HEAD_DIM), dtype=jnp.float32) * s_in
        bq = jnp.zeros((N_HEADS, HEAD_DIM), dtype=jnp.float32)
        bk = jnp.zeros((N_HEADS, HEAD_DIM), dtype=jnp.float32)
        bv = jnp.zeros((N_HEADS, HEAD_DIM), dtype=jnp.float32)
        wo = jax.random.normal(ks[6], (N_HEADS, HEAD_DIM, D_MODEL), dtype=jnp.float32) * s_in
        bo = jnp.zeros((D_MODEL,), dtype=jnp.float32)
        return {'inputs_q': inputs_q, 'inputs_kv': inputs_kv, 'bias': bias, 'wq': wq, 'bq': bq, 'wk': wk, 'bk': bk, 'wv': wv, 'bv': bv, 'wo': wo, 'bo': bo}
    _L0_xattn_all = _L0_xattn_setup()
    _L0_xattn_in = {k: v for k, v in _L0_xattn_all.items() if k in ('wq', 'bq', 'wk', 'bk', 'wv', 'bv', 'wo', 'bo')}
    del _L0_xattn_all

    def _L0_attn_setup():
        import jax, jax.numpy as jnp
        import numpy as np
        H, HKV, D = (32, 4, 64)
        BS, WS, NB = (64, 128, 16)
        HID = 256
        B, T = (1, 512)

        def masked_softmax(s, mask):
            s = jnp.where(mask, s, -jnp.inf)
            m = jnp.max(s, axis=-1, keepdims=True)
            m = jnp.where(jnp.isfinite(m), m, 0.0)
            e = jnp.where(mask, jnp.exp(s - m), 0.0)
            d = e.sum(-1, keepdims=True)
            return e / jnp.where(d > 0, d, 1.0)
        key = jax.random.key(seed)
        ks = jax.random.split(key, 6)
        sc = 0.02
        x = jax.random.normal(ks[0], (B, T, HID), jnp.float32)
        Wq = jax.random.normal(ks[1], (HID, H * D), jnp.float32) * sc
        Wk = jax.random.normal(ks[2], (HID, HKV * D), jnp.float32) * sc
        Wv = jax.random.normal(ks[3], (HID, HKV * D), jnp.float32) * sc
        Wg = jax.random.normal(ks[4], (HID, H * 3), jnp.float32) * sc
        Wo = jax.random.normal(ks[5], (H * D, HID), jnp.float32) * sc
        return {'x': x, 'Wq': Wq, 'Wk': Wk, 'Wv': Wv, 'Wg': Wg, 'Wo': Wo}
    _L0_attn_all = _L0_attn_setup()
    _L0_attn_in = {k: v for k, v in _L0_attn_all.items() if k in ('Wq', 'Wk', 'Wv', 'Wg', 'Wo')}
    del _L0_attn_all

    def _L0_ffn_setup():
        import jax, jax.numpy as jnp
        import numpy as np
        N_EMBD = 256
        NUM_EXPERTS = 8
        TOP_K = 2
        D_FF = 4 * N_EMBD
        B, S = (4, 512)
        key = jax.random.key(seed)
        ks = jax.random.split(key, 7)
        scale = lambda fan_in: 1.0 / np.sqrt(fan_in)
        x = jax.random.normal(ks[0], (B, S, N_EMBD), dtype=jnp.float32)
        W_router = jax.random.normal(ks[1], (N_EMBD, NUM_EXPERTS), dtype=jnp.float32) * scale(N_EMBD)
        b_router = jnp.zeros((NUM_EXPERTS,), dtype=jnp.float32)
        W1 = jax.random.normal(ks[2], (NUM_EXPERTS, N_EMBD, D_FF), dtype=jnp.float32) * scale(N_EMBD)
        b1 = jnp.zeros((NUM_EXPERTS, D_FF), dtype=jnp.float32)
        W2 = jax.random.normal(ks[3], (NUM_EXPERTS, D_FF, N_EMBD), dtype=jnp.float32) * scale(D_FF)
        b2 = jnpp = jnp.zeros((NUM_EXPERTS, N_EMBD), dtype=jnp.float32)
        return {'x': x, 'W_router': W_router, 'b_router': b_router, 'W1': W1, 'b1': b1, 'W2': W2, 'b2': b2}
    _L0_ffn_all = _L0_ffn_setup()
    _L0_ffn_in = {k: v for k, v in _L0_ffn_all.items() if k in ('W_router', 'b_router', 'W1', 'b1', 'W2', 'b2')}
    del _L0_ffn_all
    return {'x': x, 'ctx_1024': ctx_1024, 'fside_1x16xSxS2_0': fside_1x16xSxS2_0, 'L0_xattn_wq': _L0_xattn_in['wq'], 'L0_xattn_bq': _L0_xattn_in['bq'], 'L0_xattn_wk': _L0_xattn_in['wk'], 'L0_xattn_bk': _L0_xattn_in['bk'], 'L0_xattn_wv': _L0_xattn_in['wv'], 'L0_xattn_bv': _L0_xattn_in['bv'], 'L0_xattn_wo': _L0_xattn_in['wo'], 'L0_xattn_bo': _L0_xattn_in['bo'], 'L0_attn_Wq': _L0_attn_in['Wq'], 'L0_attn_Wk': _L0_attn_in['Wk'], 'L0_attn_Wv': _L0_attn_in['Wv'], 'L0_attn_Wg': _L0_attn_in['Wg'], 'L0_attn_Wo': _L0_attn_in['Wo'], 'L0_ffn_W_router': _L0_ffn_in['W_router'], 'L0_ffn_b_router': _L0_ffn_in['b_router'], 'L0_ffn_W1': _L0_ffn_in['W1'], 'L0_ffn_b1': _L0_ffn_in['b1'], 'L0_ffn_W2': _L0_ffn_in['W2'], 'L0_ffn_b2': _L0_ffn_in['b2']}

def reference(x, ctx_1024, fside_1x16xSxS2_0, L0_xattn_wq, L0_xattn_bq, L0_xattn_wk, L0_xattn_bk, L0_xattn_wv, L0_xattn_bv, L0_xattn_wo, L0_xattn_bo, L0_attn_Wq, L0_attn_Wk, L0_attn_Wv, L0_attn_Wg, L0_attn_Wo, L0_ffn_W_router, L0_ffn_b_router, L0_ffn_W1, L0_ffn_b1, L0_ffn_W2, L0_ffn_b2):
    import jax
    import jax.numpy as jnp

    def _L0_xattn_ref(inputs_q, inputs_kv, bias, wq, bq, wk, bk, wv, bv, wo, bo):
        import jax, jax.numpy as jnp
        import numpy as np
        D_MODEL = 256
        N_HEADS = 16
        HEAD_DIM = D_MODEL // N_HEADS
        q = jnp.einsum('bld,dhk->blhk', inputs_q, wq) + bq
        k = jnp.einsum('bld,dhk->blhk', inputs_kv, wk) + bk
        v = jnp.einsum('bld,dhk->blhk', inputs_kv, wv) + bv
        q = q / jnp.sqrt(jnp.asarray(HEAD_DIM, dtype=q.dtype))
        logits = jnp.einsum('bqhd,bkhd->bhqk', q, k)
        logits = logits + bias.astype(logits.dtype)
        attn = jax.nn.softmax(logits, axis=-1)
        ctx = jnp.einsum('bhqk,bkhd->bqhd', attn, v)
        out = jnp.einsum('bqhd,hdf->bqf', ctx, wo) + bo
        return out

    def _L0_attn_ref(x, Wq, Wk, Wv, Wg, Wo):
        import jax, jax.numpy as jnp
        import numpy as np
        H, HKV, D = (32, 4, 64)
        BS, WS, NB = (64, 128, 16)
        HID = 256
        B, T = (1, 512)

        def masked_softmax(s, mask):
            s = jnp.where(mask, s, -jnp.inf)
            m = jnp.max(s, axis=-1, keepdims=True)
            m = jnp.where(jnp.isfinite(m), m, 0.0)
            e = jnp.where(mask, jnp.exp(s - m), 0.0)
            d = e.sum(-1, keepdims=True)
            return e / jnp.where(d > 0, d, 1.0)
        Bx, Tx, _ = x.shape
        G = H // HKV
        scale = D ** (-0.5)
        q = (x @ Wq).reshape(Bx, Tx, H, D).transpose(0, 2, 1, 3)
        k = (x @ Wk).reshape(Bx, Tx, HKV, D).transpose(0, 2, 1, 3)
        v = (x @ Wv).reshape(Bx, Tx, HKV, D).transpose(0, 2, 1, 3)
        g = jax.nn.sigmoid((x @ Wg).reshape(Bx, Tx, H, 3))
        g_cmp, g_slc, g_swa = (g[..., 0], g[..., 1], g[..., 2])
        k = jnp.repeat(k, G, axis=1)
        v = jnp.repeat(v, G, axis=1)
        scores = jnp.einsum('bhtd,bhsd->bhts', q, k) * scale
        t_idx = jnp.arange(Tx)
        causal = t_idx[:, None] >= t_idx[None, :]
        swa_mask = causal & (t_idx[:, None] - t_idx[None, :] < WS)
        o_swa = jnp.einsum('bhts,bhsd->bhtd', masked_softmax(scores, swa_mask), v)
        TC = (Tx + BS - 1) // BS
        pad = TC * BS - Tx
        k_pad = jnp.pad(k, ((0, 0), (0, 0), (0, pad), (0, 0)))
        v_pad = jnp.pad(v, ((0, 0), (0, 0), (0, pad), (0, 0)))
        k_cmp = k_pad.reshape(Bx, H, TC, BS, D).mean(axis=3)
        v_cmp = v_pad.reshape(Bx, H, TC, BS, D).mean(axis=3)
        scores_cmp = jnp.einsum('bhtd,bhcd->bhtc', q, k_cmp) * scale
        cmp_mask = t_idx[:, None] >= jnp.arange(TC) * BS + BS - 1
        o_cmp = jnp.einsum('bhtc,bhcd->bhtd', masked_softmax(scores_cmp, cmp_mask), v_cmp)
        K = min(NB, TC)
        masked_cmp = jnp.where(cmp_mask, scores_cmp, -jnp.inf)
        _, top_idx = jax.lax.top_k(masked_cmp, K)
        blocks_sel = (top_idx[..., None] == jnp.arange(TC)).any(axis=-2)
        tok_sel = jnp.repeat(blocks_sel, BS, axis=-1)[..., :Tx]
        slc_mask = tok_sel & causal
        o_slc = jnp.einsum('bhts,bhsd->bhtd', masked_softmax(scores, slc_mask), v)
        gate = lambda a: a.transpose(0, 2, 1)[..., None]
        o = o_swa * gate(g_swa) + o_cmp * gate(g_cmp) + o_slc * gate(g_slc)
        o = o.transpose(0, 2, 1, 3).reshape(Bx, Tx, H * D)
        return o @ Wo

    def _L0_ffn_ref(x, W_router, b_router, W1, b1, W2, b2):
        import jax, jax.numpy as jnp
        import numpy as np
        N_EMBD = 256
        NUM_EXPERTS = 8
        TOP_K = 2
        D_FF = 4 * N_EMBD
        B, S = (4, 512)
        Bv, Sv, D = x.shape
        flat_x = x.reshape(-1, D)
        T = flat_x.shape[0]
        logits = flat_x @ W_router + b_router
        top_vals, top_idx = jax.lax.top_k(logits, TOP_K)
        neg_inf = jnp.full_like(logits, -jnp.inf)
        sparse_logits = neg_inf.at[jnp.arange(T)[:, None], top_idx].set(top_vals)
        router_weights = jax.nn.softmax(sparse_logits, axis=-1)
        final_output = jnp.zeros_like(flat_x)
        for e in range(NUM_EXPERTS):
            expert_mask = jnp.any(top_idx == e, axis=-1)
            h = jax.nn.relu(flat_x @ W1[e] + b1[e])
            y = h @ W2[e] + b2[e]
            w = router_weights[:, e] * expert_mask.astype(x.dtype)
            final_output = final_output + y * w[:, None]
        return final_output.reshape(Bv, Sv, D)
    x = x + _L0_xattn_ref(_layernorm(x, axis=-1), ctx_1024, fside_1x16xSxS2_0, L0_xattn_wq, L0_xattn_bq, L0_xattn_wk, L0_xattn_bk, L0_xattn_wv, L0_xattn_bv, L0_xattn_wo, L0_xattn_bo)
    x = x + _L0_attn_ref(_layernorm(x, axis=-1), L0_attn_Wq, L0_attn_Wk, L0_attn_Wv, L0_attn_Wg, L0_attn_Wo)
    x = x + _L0_ffn_ref(_layernorm(x, axis=-1), L0_ffn_W_router, L0_ffn_b_router, L0_ffn_W1, L0_ffn_b1, L0_ffn_W2, L0_ffn_b2)
    return x

_drawn_inputs = setup_inputs


def setup_inputs(seed=0):
    import zlib

    import numpy as np

    out = dict(_drawn_inputs(seed))
    spreads = {'L0_xattn_bq': (0.0, 0.1),
     'L0_xattn_bk': (0.0, 0.8),
     'L0_xattn_bv': (0.0, 0.1),
     'L0_xattn_bo': (0.0, 0.1),
     'L0_ffn_b_router': (0.0, 0.1),
     'L0_ffn_b1': (0.0, 0.1),
     'L0_ffn_b2': (0.0, 0.1)}
    factors = {'L0_attn_Wq': 3.705, 'L0_attn_Wk': 2.914}
    for name, (base, spread) in spreads.items():
        noise = np.random.default_rng([zlib.crc32(name.encode()), seed]).standard_normal(out[name].shape)
        drawn = base * np.exp(spread * noise) if base else spread * noise
        out[name] = jnp.asarray(drawn.astype(out[name].dtype))
    for name, factor in factors.items():
        out[name] = (out[name] * factor).astype(out[name].dtype)
    return out
```

```python
from contextlib import ExitStack

import numpy as np

import concourse.bass as bass
from concourse import mybir

F32 = mybir.dt.float32
ALU = mybir.AluOpType
ACT = mybir.ActivationFunctionType
AX = mybir.AxisListType

P = 128
B, LQ, D = 32, 64, 256
S = 1601
TOK = B * LQ
NT = TOK // P
KC = D // P
H, HD = 16, 16
HG = P // HD
PAIRS = HG // 2
COLS = [(0, 401), (401, 400), (801, 400), (1201, 400)]
NCOL = len(COLS)
ST = -(-S // P)
LAST = S - (ST - 1) * P
GT = 4
GTOK = GT * P
NG = TOK // GTOK
EPS = 1e-5
LOWEST = -3.0e38

NH, KV, DH = 32, 4, 64
GH = NH // KV
QC = NH * DH // P
CH = GH // 2
GB = GTOK // LQ
UNITS = GT * KV
AHEAD, RING = 3, 4
NP = QC + KV + GB // 2 + 1
NPR = [-(-NP // 2), NP // 2]
MASKED = -1.0e30

NE, FF = 8, 1024
FC = FF // P


def rows_of(t):
    return P if t < ST - 1 else LAST


def stand(eng, passed):
    eng.sem_inc(passed, 1)


def layer_norm(dve, nc, x_of, step, stats, mv, std, xn, chain, std_ready, passed):
    at = step * LN_STEPS
    stand(dve, passed)
    for j in range(GT):
        nc.vector.bn_stats(stats[:, j, :], x_of(j)).then_inc(chain, 1)
    for j in range(GT):
        dve.wait_ge(chain, at + j + 1)
        stand(dve, passed)
        nc.vector.bn_aggr(mv[:, j, :], stats[:, j, :]).then_inc(chain, 1)
    dve.wait_ge(chain, at + 2 * GT)
    nc.vector.tensor_scalar(std[:, :], mv[:, :, 1], EPS, None, ALU.add).then_inc(chain, 1)
    dve.wait_ge(std_ready, step + 1)
    nc.vector.reciprocal(std[:, :], std[:, :]).then_inc(chain, 1)
    dve.wait_ge(chain, at + LN_STEPS)
    for j in range(GT):
        last = nc.vector.tensor_scalar(xn[:, j, :], x_of(j), mv[:, j, 0:1], std[:, j:j + 1],
                                       ALU.subtract, ALU.mult)
    return last


LN_STEPS = 2 * GT + 2


def layer_norm_root(act, nc, step, std, chain, std_ready):
    act.wait_ge(chain, step * LN_STEPS + 2 * GT + 1)
    nc.scalar.activation(std[:, :], std[:, :], ACT.Sqrt).then_inc(std_ready, 1)


def project_queries(nc, dram, keep):
    with ExitStack() as ctx:
        sb = lambda name, shape: ctx.enter_context(nc.sbuf_tensor(name, shape, F32))
        sem = lambda name: ctx.enter_context(nc.semaphore(name))
        wq = sb("wq", [P, KC, D])
        bq = sb("bq", [P, KC])
        stats, mv, std = sb("q_stats", [P, GT, 6]), sb("q_mv", [P, GT, 2]), sb("q_std", [P, GT])
        xn = sb("q_xn", [P, GT, D])
        xnT = sb("q_xnT", [P, KC, GTOK])
        turned = [ctx.enter_context(nc.psum_tensor(f"q_turned{k}", [P, GTOK], F32)) for k in range(KC)]
        proj = [ctx.enter_context(nc.psum_tensor(f"q_proj{c}", [P, GTOK], F32)) for c in range(KC)]
        loaded, chain, std_ready, normed = sem("q_loaded"), sem("q_chain"), sem("q_std_ready"), sem("q_normed")
        xT_filled, xT_kept = sem("q_xT_filled"), sem("q_xT_kept")
        q_filled, q_kept = sem("q_filled"), sem("q_kept")
        passed = sem("q_passed")
        x_all, QT, ident = keep["x_all"], keep["QT"], keep["ident"]
        block = ctx.enter_context(nc.Block())

        @block.sync
        def _(sp):
            sp.dma_start(x_all[:, :, :], dram["x"].rearrange("(t p) d -> p t d", p=P)).then_inc(loaded, 16)
            sp.dma_start(ident[:, :], dram["ident"]).then_inc(loaded, 16)
            sp.dma_start(wq[:, :, :], dram["wq"].rearrange("(k p) n -> p k n", p=P)).then_inc(loaded, 16)
            sp.dma_start(bq[:, :], dram["bq"]).then_inc(loaded, 16)
            sp.dma_start(keep["headmask"][:, :], dram["headmask"]).then_inc(loaded, 16)

        @block.vector
        def _(dve):
            dve.wait_ge(loaded, 80)
            with dve.Fori(0, NG) as g:
                dve.wait_ge(xT_filled, KC * g)
                layer_norm(dve, nc, lambda j: x_all[:, bass.ds(g * GT + j, 1), :].rearrange("p a d -> p (a d)"),
                           g, stats, mv, std, xn, chain, std_ready, passed).then_inc(normed, 1)
                for c in range(KC):
                    dve.wait_ge(q_filled, KC * g + c + 1)
                    nc.vector.tensor_scalar(QT[:, c, bass.ds(g * GTOK, GTOK)], proj[c][:, :], bq[:, c:c + 1],
                                            float(HD) ** -0.5, ALU.add, ALU.mult).then_inc(q_kept, 1)

        @block.scalar
        def _(act):
            with act.Fori(0, NG) as g:
                layer_norm_root(act, nc, g, std, chain, std_ready)
                for k in range(KC):
                    act.wait_ge(xT_filled, KC * g + k + 1)
                    act.wait_ge(q_filled, KC * g)
                    nc.scalar.copy(xnT[:, k, :], turned[k][:, :]).then_inc(xT_kept, 1)

        @block.tensor
        def _(pe):
            pe.wait_ge(loaded, 80)
            with pe.Fori(0, NG) as g:
                pe.wait_ge(normed, g + 1)
                for k in range(KC):
                    pe.wait_ge(xT_kept, KC * g)
                    for j in range(GT):
                        last = nc.tensor.transpose(turned[k][:, j * P:(j + 1) * P], xn[:, j, k * P:(k + 1) * P], ident[:, :])
                    last.then_inc(xT_filled, 1)
                pe.wait_ge(xT_kept, KC * (g + 1))
                for c in range(KC):
                    pe.wait_ge(q_kept, KC * g)
                    for k in range(KC):
                        last = nc.tensor.matmul(proj[c][:, :], wq[:, k, c * P:(c + 1) * P], xnT[:, k, :],
                                                start=(k == 0), stop=(k == KC - 1))
                    last.then_inc(q_filled, 1)


def cross_attention(nc, dram, keep):
    with ExitStack() as ctx:
        sb = lambda name, shape: ctx.enter_context(nc.sbuf_tensor(name, shape, F32))
        bank = lambda name: ctx.enter_context(nc.psum_tensor(name, [P, 512], F32))
        sem = lambda name: ctx.enter_context(nc.semaphore(name))
        wk, wv = sb("wk", [P, KC, D]), sb("wv", [P, KC, D])
        bk, bv = sb("bk", [P, KC]), sb("bv", [P, D])
        bias = sb("bias", [P, KC * PAIRS, S])
        ctxT = sb("ctxT", [P, KC, S])
        KT = sb("KT", [P, KC, S])
        V = sb("V", [P, ST, D])
        QB = [sb(f"QB{g}", [P, HG * LQ]) for g in range(KC)]
        probs = [sb(f"probs{g}", [P, PAIRS, S]) for g in range(KC)]
        PT = [sb(f"PT{r}", [P, HG * LQ]) for r in range(2)]
        picked = sb("picked", [P, HG * LQ])
        top = [sb(f"top{g}", [P, PAIRS, NCOL]) for g in range(KC)]
        neg_max = [sb(f"neg_max{g}", [P, PAIRS]) for g in range(KC)]
        total = [sb(f"total{g}", [P, PAIRS]) for g in range(KC)]
        score_bank = [bank(f"score_bank{r}") for r in range(2)]
        turn_bank = [bank(f"turn_bank{r}") for r in range(2)]
        proj_bank = [bank(f"proj_bank{r}") for r in range(2)]
        out_bank = [bank(f"out_bank{g}") for g in range(KC)]

        w_loaded, ctx_loaded = sem("w_loaded"), sem("ctx_loaded")
        k_filled, k_kept, v_filled, v_kept = sem("k_filled"), sem("k_kept"), sem("v_filled"), sem("v_kept")
        qb_ready = [sem(f"qb_ready{g}") for g in range(KC)]
        s_filled, s_read = sem("s_filled"), sem("s_read")
        max_ready, exp_done, scale_ready, probs_ready = sem("max_ready"), sem("exp_done"), sem("scale_ready"), sem("probs_ready")
        t_filled = [sem(f"t_filled{r}") for r in range(2)]
        t_kept = [sem(f"t_kept{r}") for r in range(2)]
        t_used = [sem(f"t_used{r}") for r in range(2)]
        out_read, ct_ready = sem("out_read"), sem("ct_ready")
        passed, passed_pool = sem("passed"), sem("passed_pool")
        QT, CT, ident, headmask = keep["QT"], keep["CT"], keep["ident"], keep["headmask"]
        VF = -(-ST // 2)
        nk = KC * NCOL
        block = ctx.enter_context(nc.Block())

        def turn_of(b, g, t):
            r = (g + t) % 2
            before = 0 if g == 0 else (-(-ST // 2) if r == 0 else ST // 2)
            return r, b * ST + before + t // 2

        @block.sync
        def _(sp):
            sp.dma_start(wk[:, :, :], dram["wk"].rearrange("(k p) n -> p k n", p=P)).then_inc(w_loaded, 16)
            sp.dma_start(bk[:, :], dram["bk"]).then_inc(w_loaded, 16)
            sp.dma_start(wv[:, :, :], dram["wv"].rearrange("(k p) n -> p k n", p=P)).then_inc(w_loaded, 16)
            sp.dma_start(bv[:, :], dram["bv"]).then_inc(w_loaded, 16)
            sp.dma_start(ctxT[:, :, :], dram["ctxT"][0].rearrange("k p s -> p k s")).then_inc(ctx_loaded, 16)
            sp.dma_start(bias[:, :, :], dram["bias"].rearrange("r p s -> p r s")).then_inc(w_loaded, 16)
            with sp.Fori(1, B) as b:
                sp.wait_ge(v_filled, VF * b)
                sp.dma_start(ctxT[:, :, :], dram["ctxT"][bass.ds(b, 1)].rearrange("a k p s -> p (a k) s")).then_inc(ctx_loaded, 16)

        @block.tensor
        def _(pe):
            def project_k(b):
                pe.wait_ge(ctx_loaded, 16 * b + 16)
                pe.wait_ge(v_kept, VF * b)
                for c in range(KC):
                    for j, (at, n) in enumerate(COLS):
                        i = c * NCOL + j
                        if i >= 2:
                            pe.wait_ge(k_kept, nk * b + i - 1)
                        for k in range(KC):
                            last = nc.tensor.matmul(proj_bank[i % 2][:, 0:n], wk[:, k, c * P:(c + 1) * P],
                                                    ctxT[:, k, at:at + n], start=(k == 0), stop=(k == KC - 1))
                        last.then_inc(k_filled, 1)

            def project_v(b):
                pe.wait_ge(k_kept, nk * b + nk)
                for f in range(VF):
                    if f >= 2:
                        pe.wait_ge(v_kept, VF * b + f - 1)
                    for t in range(2 * f, min(2 * f + 2, ST)):
                        n = rows_of(t)
                        for k in range(KC):
                            last = nc.tensor.matmul(proj_bank[f % 2][0:n, (t % 2) * D:(t % 2 + 1) * D],
                                                    ctxT[:, k, t * P:t * P + n], wv[:, k, :],
                                                    start=(k == 0), stop=(k == KC - 1))
                    last.then_inc(v_filled, 1)

            def scores(b, g):
                pe.wait_ge(qb_ready[g], b + 1)
                pe.wait_ge(k_kept, nk * b + (g + 1) * NCOL)
                for i in range(PAIRS):
                    for j, (at, n) in enumerate(COLS):
                        m = (2 * b + g) * PAIRS * NCOL + i * NCOL + j
                        if g == 1 or i or j >= 2:
                            pe.wait_ge(s_read, m - 1)
                        elif j == 0:
                            pe.wait_ge(s_read, m)
                        nc.tensor.matmul(score_bank[j % 2][:, 0:n], QB[g][:, i * P:(i + 1) * P],
                                         KT[:, g, at:at + n], start=True, stop=True).then_inc(s_filled, 1)

            def turn(b, g, t):
                r, before = turn_of(b, g, t)
                n = rows_of(t)
                pe.wait_ge(t_kept[r], before)
                for i in range(PAIRS):
                    last = nc.tensor.transpose(turn_bank[r][0:n, i * P:(i + 1) * P],
                                               probs[g][:, i, t * P:t * P + n], ident[:, :])
                last.then_inc(t_filled[r], 1)

            def weigh(b, g, t):
                r, before = turn_of(b, g, t)
                n = rows_of(t)
                pe.wait_ge(t_kept[r], before + 1)
                nc.tensor.matmul(out_bank[g][:, :], V[0:n, t, g * P:(g + 1) * P], PT[r][0:n, :],
                                 start=(t == 0), stop=(t == ST - 1)).then_inc(t_used[r], 1)

            def mix(b, g):
                pe.wait_ge(probs_ready, PAIRS * (2 * b + g + 1))
                pe.wait_ge(v_kept, VF * b + VF)
                pe.wait_ge(out_read, 2 * b)
                turn(b, g, 0)
                for t in range(ST):
                    if t + 1 < ST:
                        turn(b, g, t + 1)
                    weigh(b, g, t)

            pe.wait_ge(w_loaded, 80)
            project_k(0)
            scores(0, 0)
            project_v(0)
            with pe.Fori(0, B - 1) as b:
                scores(b, 1)
                mix(b, 0)
                project_k(b + 1)
                scores(b + 1, 0)
                mix(b, 1)
                project_v(b + 1)
            scores(B - 1, 1)
            mix(B - 1, 0)
            mix(B - 1, 1)

        @block.vector
        def _(dve):
            def logits(b, g, again=True):
                r, before = turn_of(b, g, ST - 1)
                for i in range(PAIRS):
                    for j, (at, n) in enumerate(COLS):
                        m = (2 * b + g) * PAIRS * NCOL + i * NCOL + j
                        dve.wait_ge(s_filled, m + 1)
                        if again and i == 0 and j == 0:
                            dve.wait_ge(t_used[r], before + 1 - ST)
                        stand(dve, passed)
                        nc.vector.tensor_tensor_reduce(probs[g][:, i, at:at + n], score_bank[j % 2][:, 0:n],
                                                       bias[:, g * PAIRS + i, at:at + n], 1.0, LOWEST,
                                                       ALU.add, ALU.max, top[g][:, i, j:j + 1]).then_inc(s_read, 1)
                    dve.wait_ge(s_read, (2 * b + g) * PAIRS * NCOL + (i + 1) * NCOL)
                    nc.vector.tensor_reduce(neg_max[g][:, i:i + 1], top[g][:, i, :], AX.X, ALU.max,
                                            negate=True).then_inc(max_ready, 1)

            def invert_totals(b, g):
                dve.wait_ge(exp_done, PAIRS * (2 * b + g + 1))
                nc.vector.reciprocal(total[g][:, :], total[g][:, :]).then_inc(scale_ready, 1)

            def keep_turned(b, g, then_invert=None):
                for t in range(ST):
                    if t == ST // 2 and then_invert is not None:
                        invert_totals(*then_invert)
                    r, before = turn_of(b, g, t)
                    if r == 1:
                        n = rows_of(t)
                        dve.wait_ge(t_filled[r], before + 1)
                        dve.wait_ge(t_used[r], before)
                        nc.vector.tensor_copy(PT[r][0:n, :], turn_bank[r][0:n, :]).then_inc(t_kept[r], 1)

            def keep_heads(b, g):
                r, before = turn_of(b, g, ST - 1)
                dve.wait_ge(t_used[r], before + 1)
                dve.wait_ge(ct_ready, 2 * b + g)
                nc.vector.tensor_tensor(picked[:, :], out_bank[g][:, :], headmask[:, :], ALU.mult).then_inc(out_read, 1)
                dve.wait_ge(out_read, 2 * b + g + 1)
                nc.vector.tensor_reduce(CT[:, g, bass.ds(b * LQ, LQ)], picked[:, :].rearrange("p (h q) -> p q h", h=HG),
                                        AX.X, ALU.add).then_inc(ct_ready, 1)

            def keep_v(b):
                for f in range(VF):
                    dve.wait_ge(v_filled, VF * b + f + 1)
                    if 2 * f + 1 < ST:
                        nc.vector.tensor_tensor(V[:, 2 * f:2 * f + 2, :],
                                                proj_bank[f % 2][:, :].rearrange("p (t n) -> p t n", t=2),
                                                bv[:, :].rearrange("p (a n) -> p a n", a=1).to_broadcast([P, 2, D]),
                                                ALU.add).then_inc(v_kept, 1)
                    else:
                        nc.vector.tensor_tensor(V[0:LAST, 2 * f, :], proj_bank[f % 2][0:LAST, 0:D], bv[0:LAST, :],
                                                ALU.add).then_inc(v_kept, 1)

            dve.wait_ge(w_loaded, 80)
            logits(0, 0, again=False)
            keep_v(0)
            invert_totals(0, 0)
            logits(0, 1, again=False)
            keep_turned(0, 0, (0, 1))
            keep_heads(0, 0)
            with dve.Fori(1, B) as b:
                logits(b, 0)
                keep_turned(b - 1, 1, (b, 0))
                keep_heads(b - 1, 1)
                keep_v(b)
                logits(b, 1)
                keep_turned(b, 0, (b, 1))
                keep_heads(b, 0)
            keep_turned(B - 1, 1)
            keep_heads(B - 1, 1)

        @block.scalar
        def _(act):
            def keep_k(b):
                for c in range(KC):
                    for j, (at, n) in enumerate(COLS):
                        i = c * NCOL + j
                        act.wait_ge(k_filled, nk * b + i + 1)
                        nc.scalar.activation(KT[:, c, at:at + n], proj_bank[i % 2][:, 0:n], ACT.Identity,
                                             bias=bk[:, c:c + 1]).then_inc(k_kept, 1)

            def exponentials(b, g):
                for i in range(PAIRS):
                    act.wait_ge(max_ready, (2 * b + g) * PAIRS + i + 1)
                    nc.scalar.activation(probs[g][:, i, :], probs[g][:, i, :], ACT.Exp, bias=neg_max[g][:, i:i + 1],
                                         accum_out=total[g][:, i:i + 1]).then_inc(exp_done, 1)

            def keep_turned(b, g):
                for t in range(ST):
                    r, before = turn_of(b, g, t)
                    if r == 0:
                        n = rows_of(t)
                        act.wait_ge(t_filled[r], before + 1)
                        act.wait_ge(t_used[r], before)
                        nc.scalar.copy(PT[r][0:n, :], turn_bank[r][0:n, :]).then_inc(t_kept[r], 1)

            act.wait_ge(w_loaded, 80)
            keep_k(0)
            exponentials(0, 0)
            with act.Fori(0, B - 1) as b:
                exponentials(b, 1)
                keep_turned(b, 0)
                keep_k(b + 1)
                exponentials(b + 1, 0)
                keep_turned(b, 1)
            exponentials(B - 1, 1)
            keep_turned(B - 1, 0)
            keep_turned(B - 1, 1)

        @block.gpsimd
        def _(pool):
            def spread_q(b, g):
                nc.gpsimd.tensor_tensor(QB[g][:, :].rearrange("p (h q) -> p h q", h=HG),
                                        QT[:, bass.ds(g, 1), bass.ds(b * LQ, LQ)].to_broadcast([P, HG, LQ]),
                                        headmask[:, :].rearrange("p (h q) -> p h q", h=HG), ALU.mult).then_inc(qb_ready[g], 1)

            def normalise(b, g):
                pool.wait_ge(scale_ready, 2 * b + g + 1)
                stand(pool, passed_pool)
                for i in range(PAIRS):
                    nc.gpsimd.tensor_scalar(probs[g][:, i, :], probs[g][:, i, :], total[g][:, i:i + 1], None,
                                            ALU.mult).then_inc(probs_ready, 1)

            spread_q(0, 0)
            spread_q(0, 1)
            normalise(0, 0)
            with pool.Fori(0, B - 1) as b:
                spread_q(b + 1, 0)
                normalise(b, 1)
                spread_q(b + 1, 1)
                normalise(b + 1, 0)
            normalise(B - 1, 1)


def gated_attention(nc, dram, keep):
    with ExitStack() as ctx:
        sb = lambda name, shape: ctx.enter_context(nc.sbuf_tensor(name, shape, F32))
        bank = lambda name: ctx.enter_context(nc.psum_tensor(name, [P, 512], F32))
        sem = lambda name: ctx.enter_context(nc.semaphore(name))
        wo_x, bo_x = sb("wo_x", [P, KC, D]), sb("bo_x", [P, D])
        wq, wk = sb("a_wq", [P, KC, NH * DH]), sb("a_wk", [P, KC, KV * 2 * DH])
        wv, wg, wo = sb("a_wv", [P, KC, KV * DH]), sb("a_wg", [P, KC, NH * 3]), sb("a_wo", [P, QC, D])
        causal, at_last = sb("causal", [P, GH * LQ]), sb("at_last", [P, 1])
        heads = sb("heads", [P, KC, GTOK])
        stats, mv, std = sb("a_stats", [P, GT, 6]), sb("a_mv", [P, GT, 2]), sb("a_std", [P, GT])
        xn, xnT = sb("a_xn", [P, GT, D]), sb("a_xnT", [P, KC, GTOK])
        xn_twice = sb("xn_twice", [P, KC * GB, 2, LQ])
        QT = sb("a_QT", [P, QC, GTOK])
        KB = sb("a_KB", [P, KV, GB, 2, LQ])
        VB = sb("a_VB", [P, GB, KV, 2, DH])
        gate = sb("gate", [P, GT, NH * 3])
        gate_near, gate_mean = sb("gate_near", [P, GT, NH]), sb("gate_mean", [P, GT, NH])
        A = [sb(f"A{r}", [P, GH, LQ]) for r in range(RING)]
        top = [sb(f"a_top{r}", [P, GH]) for r in range(RING)]
        total = [sb(f"a_total{r}", [P, GH]) for r in range(RING)]
        AT = [sb(f"AT{r}", [P, CH, 2, LQ]) for r in range(2)]
        OT = [sb(f"OT{r}", [P, QC, 2, LQ]) for r in range(2)]
        proj_bank = [bank(f"a_proj_bank{r}") for r in range(2)]
        score_bank = [bank(f"a_score_bank{r}") for r in range(2)]
        turn_bank = [bank(f"a_turn_bank{r}") for r in range(2)]
        out_bank = [bank(f"a_out_bank{r}") for r in range(2)]

        loaded, zeroed = sem("a_loaded"), sem("a_zeroed")
        heads_ready, bo_added = sem("heads_ready"), sem("bo_added")
        h_filled, h_added = sem("h_filled"), sem("h_added")
        chain, std_ready, normed = sem("a_chain"), sem("a_std_ready"), sem("a_normed")
        xT_filled, xT_kept, twice_ready = sem("a_xT_filled"), sem("a_xT_kept"), sem("twice_ready")
        p_filled, p_kept = sem("p_filled"), [sem(f"p_kept{r}") for r in range(2)]
        gate_step, gate_ready = sem("gate_step"), sem("gate_ready")
        s_filled, s_read = sem("a_s_filled"), sem("a_s_read")
        top_ready, moved, exp_done = sem("a_top_ready"), sem("a_moved"), sem("a_exp_done")
        sum_step, scale_ready, scaled, A_ready = sem("a_sum_step"), sem("a_scale_ready"), sem("a_scaled"), sem("A_ready")
        t_filled, t_kept, o_filled, o_kept = sem("a_t_filled"), sem("a_t_kept"), sem("o_filled"), sem("o_kept")
        w_filled, w_added = sem("w_filled"), sem("w_added")
        passed, passed_pool = sem("a_passed"), sem("a_passed_pool")
        x_all, CT, ident = keep["x_all"], keep["CT"], keep["ident"]
        N_LOAD = 9 * 16
        GATE_FILL = NP - 1
        block = ctx.enter_context(nc.Block())

        def since(g, per, n, ring):
            return g * per + max(n + 1 - ring, 0)

        @block.sync
        def _(sp):
            chunked = lambda ap: ap.rearrange("(k p) n -> p k n", p=P)
            sp.dma_start(wo_x[:, :, :], chunked(dram["wo_x"])).then_inc(loaded, 16)
            sp.dma_start(bo_x[:, :], dram["bo_x"]).then_inc(loaded, 16)
            sp.dma_start(wq[:, :, :], chunked(dram["a_wq"])).then_inc(loaded, 16)
            sp.dma_start(wk[:, :, :], chunked(dram["a_wk"])).then_inc(loaded, 16)
            sp.dma_start(wv[:, :, :], chunked(dram["a_wv"])).then_inc(loaded, 16)
            sp.dma_start(wg[:, :, :], chunked(dram["a_wg"])).then_inc(loaded, 16)
            sp.dma_start(wo[:, :, :], chunked(dram["a_wo"])).then_inc(loaded, 16)
            sp.dma_start(causal[:, :], dram["causal"]).then_inc(loaded, 16)
            sp.dma_start(at_last[:, :], dram["at_last"]).then_inc(loaded, 16)

        @block.tensor
        def _(pe):
            pe.wait_ge(loaded, N_LOAD)
            pe.wait_ge(zeroed, 2)
            with pe.Fori(0, NG) as g:
                pe.wait_ge(heads_ready, g + 1)
                pe.wait_ge(w_added, GT * g)
                for f in range(GT // 2):
                    for j in (2 * f, 2 * f + 1):
                        for k in range(KC):
                            last = nc.tensor.matmul(proj_bank[f][:, (j % 2) * D:(j % 2 + 1) * D], heads[:, k, j * P:(j + 1) * P],
                                                    wo_x[:, k, :], start=(k == 0), stop=(k == KC - 1))
                    last.then_inc(h_filled, 1)
                pe.wait_ge(normed, g + 1)
                for k in range(KC):
                    for j in range(GT):
                        last = nc.tensor.transpose(proj_bank[k][:, j * P:(j + 1) * P], xn[:, j, k * P:(k + 1) * P], ident[:, :])
                    last.then_inc(xT_filled, 1)
                pe.wait_ge(xT_kept, KC * (g + 1))
                for i in range(NP):
                    pe.wait_ge(p_kept[i % 2], g * NPR[i % 2] + i // 2)
                    to = proj_bank[i % 2]
                    if i < QC:
                        for k in range(KC):
                            last = nc.tensor.matmul(to[:, :], wq[:, k, i * P:(i + 1) * P], xnT[:, k, :],
                                                    start=(k == 0), stop=(k == KC - 1))
                    elif i < QC + KV:
                        n = i - QC
                        for k in range(KC):
                            last = nc.tensor.matmul(to[:, :], wk[:, k, n * P:(n + 1) * P], xnT[:, k, :],
                                                    start=(k == 0), stop=(k == KC - 1))
                    elif i < GATE_FILL:
                        pe.wait_ge(twice_ready, g + 1)
                        for half in range(2):
                            b = 2 * (i - QC - KV) + half
                            for k in range(KC):
                                last = nc.tensor.matmul(to[:, half * D:(half + 1) * D],
                                                        xn_twice[:, k * GB + b, :, :],
                                                        wv[:, k, :], start=(k == 0), stop=(k == KC - 1))
                    else:
                        for j in range(GT):
                            for k in range(KC):
                                last = nc.tensor.matmul(to[:, j * NH * 3:(j + 1) * NH * 3], xnT[:, k, j * P:(j + 1) * P],
                                                        wg[:, k, :], start=(k == 0), stop=(k == KC - 1))
                    last.then_inc(p_filled, 1)
                for r in range(2):
                    pe.wait_ge(p_kept[r], (g + 1) * NPR[r])
                for n in range(-AHEAD, UNITS + 2):
                    if n + AHEAD < UNITS:
                        m = n + AHEAD
                        j, kv = m // KV, m % KV
                        pe.wait_ge(s_read, since(g, UNITS, m, 2))
                        for half in range(2):
                            b = 2 * j + half
                            for c in range(CH):
                                last = nc.tensor.matmul(score_bank[m % 2][half * LQ:(half + 1) * LQ, c * P:(c + 1) * P],
                                                        QT[:, kv * CH + c, b * LQ:(b + 1) * LQ], KB[:, kv, b, :, :],
                                                        start=True, stop=True)
                        last.then_inc(s_filled, 1)
                    if 0 <= n < UNITS:
                        pe.wait_ge(A_ready, g * UNITS + n + 1)
                        pe.wait_ge(t_kept, since(g, UNITS, n, 2))
                        for c in range(CH):
                            last = nc.tensor.transpose(turn_bank[n % 2][:, c * P:(c + 1) * P],
                                                       A[n % RING][:, 2 * c:2 * c + 2, :], ident[:, :])
                        last.then_inc(t_filled, 1)
                    if 1 <= n <= UNITS:
                        m = n - 1
                        j, kv = m // KV, m % KV
                        pe.wait_ge(t_kept, g * UNITS + m + 1)
                        pe.wait_ge(o_kept, since(g, UNITS, m, 2))
                        for half in range(2):
                            last = nc.tensor.matmul(out_bank[m % 2][:, half * CH * LQ:(half + 1) * CH * LQ],
                                                    VB[:, 2 * j + half, kv, :, :], AT[m % 2][:, :, half, :],
                                                    start=True, stop=True)
                        last.then_inc(o_filled, 1)
                    if n >= KV + 1 and (n - 1) % KV == 0:
                        j = (n - 1) // KV - 1
                        pe.wait_ge(o_kept, g * UNITS + KV * (j + 1))
                        pe.wait_ge(w_added, since(g, GT, j, 2))
                        for c in range(QC):
                            last = nc.tensor.matmul(proj_bank[j % 2][:, 0:D], OT[j % 2][:, c, :, :], wo[:, c, :],
                                                    start=(c == 0), stop=(c == QC - 1))
                        last.then_inc(w_filled, 1)

        def keep_projection(eng, g, i, copy):
            eng.wait_ge(p_filled, g * NP + i + 1)
            src = proj_bank[i % 2]
            if i < QC:
                last = copy(QT[:, i, :], src[:, :], float(DH) ** -0.5)
            elif i < QC + KV:
                for half in range(2):
                    rows = slice(half * DH, (half + 1) * DH)
                    last = copy(KB[rows, i - QC, :, half, :], src[rows, :].rearrange("p (b s) -> p b s", b=GB), 1.0)
            elif i < GATE_FILL:
                b = 2 * (i - QC - KV)
                for half in range(2):
                    rows = slice(half * LQ, (half + 1) * LQ)
                    for one in range(2):
                        last = copy(VB[rows, b + one, :, half, :],
                                    src[rows, one * D:(one + 1) * D].rearrange("p (v d) -> p v d", v=KV), 1.0)
            last.then_inc(p_kept[i % 2], 1)

        @block.vector
        def _(dve):
            dve.wait_ge(loaded, N_LOAD)
            dve.wait_ge(zeroed, 2)
            with dve.Fori(0, NG) as g:
                for f in range(GT // 2):
                    dve.wait_ge(h_filled, GT // 2 * g + f + 1)
                    dve.wait_ge(bo_added, g + 1)
                    tiles = x_all[:, bass.ds(g * GT + 2 * f, 2), :]
                    nc.vector.tensor_tensor(tiles, proj_bank[f][:, :].rearrange("p (t n) -> p t n", t=2), tiles,
                                            ALU.add).then_inc(h_added, 1)
                dve.wait_ge(h_added, GT // 2 * (g + 1))
                layer_norm(dve, nc, lambda j: x_all[:, bass.ds(g * GT + j, 1), :].rearrange("p a d -> p (a d)"),
                           g, stats, mv, std, xn, chain, std_ready, passed).then_inc(normed, 1)
                for i in range(1, NP, 2):
                    keep_projection(dve, g, i, lambda o, s, f: nc.vector.tensor_scalar(o, s, f, None, ALU.mult))
                dve.wait_ge(p_kept[0], (g + 1) * NPR[0])
                nc.vector.tensor_scalar(gate[:, :, :], gate[:, :, :], 1.0, None, ALU.add).then_inc(gate_step, 1)
                dve.wait_ge(gate_step, 2 * g + 1)
                nc.vector.reciprocal(gate[:, :, :], gate[:, :, :]).then_inc(gate_step, 1)
                dve.wait_ge(gate_step, 2 * g + 2)
                by_kind = gate[:, :, :].rearrange("p t (h k) -> p t h k", k=3)
                nc.vector.tensor_tensor(gate_near[:, :, :], by_kind[:, :, :, 1], by_kind[:, :, :, 2], ALU.add)\
                    .then_inc(gate_ready, 1)
                nc.vector.tensor_scalar(gate_mean[:, :, :], by_kind[:, :, :, 0], at_last[:, 0:1], None, ALU.mult)\
                    .then_inc(gate_ready, 1)
                dve.wait_ge(gate_ready, 2 * g + 2)
                for n in range(-AHEAD, UNITS + 2):
                    if n + AHEAD < UNITS:
                        m = n + AHEAD
                        r = m % RING
                        dve.wait_ge(s_filled, g * UNITS + m + 1)
                        dve.wait_ge(t_filled, since(g, UNITS, m, RING))
                        nc.vector.tensor_tensor(A[r][:, :, :], score_bank[m % 2][:, :].rearrange("p (h s) -> p h s", h=GH),
                                                causal[:, :].rearrange("p (h s) -> p h s", h=GH), ALU.add).then_inc(s_read, 1)
                        dve.wait_ge(s_read, g * UNITS + m + 1)
                        nc.vector.tensor_reduce(top[r][:, :], A[r][:, :, :], AX.X, ALU.max).then_inc(top_ready, 1)
                    if 0 <= n + AHEAD - 1 < UNITS:
                        m = n + AHEAD - 1
                        r, j, kv = m % RING, m // KV, m % KV
                        dve.wait_ge(exp_done, g * UNITS + m + 1)
                        nc.vector.tensor_reduce(total[r][:, :], A[r][:, :, :], AX.X, ALU.add).then_inc(sum_step, 1)
                        dve.wait_ge(sum_step, 2 * (g * UNITS + m) + 1)
                        nc.vector.reciprocal(total[r][:, :], total[r][:, :]).then_inc(sum_step, 1)
                        dve.wait_ge(sum_step, 2 * (g * UNITS + m) + 2)
                        nc.vector.tensor_tensor(total[r][:, :], total[r][:, :], gate_near[:, j, kv * GH:(kv + 1) * GH],
                                                ALU.mult).then_inc(scale_ready, 1)
                    if n >= KV + 1 and (n - 1) % KV == 0:
                        j = (n - 1) // KV - 1
                        dve.wait_ge(w_filled, GT * g + j + 1)
                        tile = x_all[:, bass.ds(g * GT + j, 1), :]
                        nc.vector.tensor_tensor(tile, proj_bank[j % 2][:, 0:D].rearrange("p (a n) -> p a n", a=1), tile,
                                                ALU.add).then_inc(w_added, 1)

        @block.scalar
        def _(act):
            act.wait_ge(zeroed, 2)
            with act.Fori(0, NG) as g:
                layer_norm_root(act, nc, g, std, chain, std_ready)
                for k in range(KC):
                    act.wait_ge(xT_filled, KC * g + k + 1)
                    nc.scalar.copy(xnT[:, k, :], proj_bank[k][:, :]).then_inc(xT_kept, 1)
                for i in range(0, NP - 1, 2):
                    keep_projection(act, g, i, lambda o, s, f: nc.scalar.activation(o, s, ACT.Copy, scale=f))
                act.wait_ge(p_filled, g * NP + NP)
                act.wait_ge(A_ready, g * UNITS)
                nc.scalar.activation(gate[:, :, :], proj_bank[GATE_FILL % 2][:, 0:GT * NH * 3].rearrange("p (t n) -> p t n", t=GT),
                                     ACT.Exp, scale=-1.0).then_inc(p_kept[0], 1)
                for n in range(-AHEAD, UNITS + 2):
                    if 0 <= n < UNITS:
                        act.wait_ge(t_filled, g * UNITS + n + 1)
                        act.wait_ge(o_filled, since(g, UNITS, n, 2))
                        nc.scalar.copy(AT[n % 2][:, :, :, :], turn_bank[n % 2][:, :].rearrange("p (c b t) -> p c b t", c=CH, b=2))\
                            .then_inc(t_kept, 1)
                    if 1 <= n <= UNITS:
                        m = n - 1
                        j, kv = m // KV, m % KV
                        act.wait_ge(o_filled, g * UNITS + m + 1)
                        act.wait_ge(w_filled, since(g, GT, j, 2))
                        nc.scalar.copy(OT[j % 2][:, kv * CH:(kv + 1) * CH, :, :].rearrange("p c b t -> p b c t"),
                                       out_bank[m % 2][:, :].rearrange("p (b c t) -> p b c t", b=2, c=CH)).then_inc(o_kept, 1)
                    if n + AHEAD < UNITS:
                        m = n + AHEAD
                        act.wait_ge(moved, g * UNITS + m + 1)
                        nc.scalar.activation(A[m % RING][:, :, :], A[m % RING][:, :, :], ACT.Exp).then_inc(exp_done, 1)

        @block.gpsimd
        def _(pool):
            nc.gpsimd.memset(KB[:, :, :, :, :], 0.0).then_inc(zeroed, 1)
            nc.gpsimd.memset(VB[:, :, :, :, :], 0.0).then_inc(zeroed, 1)
            pool.wait_ge(loaded, N_LOAD)
            with pool.Fori(0, NG) as g:
                pool.wait_ge(h_filled, GT // 2 * g)
                nc.gpsimd.tensor_copy(heads[:, :, :], CT[:, :, bass.ds(g * GTOK, GTOK)]).then_inc(heads_ready, 1)
                tiles = x_all[:, bass.ds(g * GT, GT), :]
                nc.gpsimd.tensor_tensor(tiles, tiles, bo_x[:, :].rearrange("p (a n) -> p a n", a=1).to_broadcast([P, GT, D]),
                                        ALU.add).then_inc(bo_added, 1)
                pool.wait_ge(xT_kept, KC * (g + 1))
                stand(pool, passed_pool)
                for half in range(2):
                    last = nc.gpsimd.tensor_copy(xn_twice[:, :, half, :], xnT[:, :, :].rearrange("p k (b s) -> p (k b) s", s=LQ))
                last.then_inc(twice_ready, 1)
                pool.wait_ge(gate_ready, 2 * g + 2)
                for n in range(-AHEAD, UNITS):
                    if n + AHEAD < UNITS:
                        m = n + AHEAD
                        r = m % RING
                        pool.wait_ge(top_ready, g * UNITS + m + 1)
                        nc.gpsimd.tensor_tensor(A[r][:, :, :], A[r][:, :, :],
                                                top[r][:, :].rearrange("p (h a) -> p h a", a=1).to_broadcast([P, GH, LQ]),
                                                ALU.subtract).then_inc(moved, 1)
                    if 0 <= n + AHEAD - 1 < UNITS:
                        m = n + AHEAD - 1
                        r, j, kv = m % RING, m // KV, m % KV
                        pool.wait_ge(scale_ready, g * UNITS + m + 1)
                        nc.gpsimd.tensor_tensor(A[r][:, :, :], A[r][:, :, :],
                                                total[r][:, :].rearrange("p (h a) -> p h a", a=1).to_broadcast([P, GH, LQ]),
                                                ALU.mult).then_inc(scaled, 1)
                        pool.wait_ge(scaled, g * UNITS + m + 1)
                        nc.gpsimd.tensor_tensor(A[r][:, :, :], A[r][:, :, :],
                                                gate_mean[:, j, kv * GH:(kv + 1) * GH].rearrange("p (h a) -> p h a", a=1)
                                                .to_broadcast([P, GH, LQ]), ALU.add).then_inc(A_ready, 1)


def experts(nc, dram, keep, out):
    with ExitStack() as ctx:
        sb = lambda name, shape: ctx.enter_context(nc.sbuf_tensor(name, shape, F32))
        bank = lambda name: ctx.enter_context(nc.psum_tensor(name, [P, 512], F32))
        sem = lambda name: ctx.enter_context(nc.semaphore(name))
        w1 = [sb(f"w1_{r}", [P, KC, FF]) for r in range(2)]
        w2 = [sb(f"w2_{r}", [P, FC, D]) for r in range(2)]
        b1 = [sb(f"b1_{r}", [P, FC]) for r in range(2)]
        b2 = [sb(f"b2_{r}", [P, D]) for r in range(2)]
        wr, br = sb("wr", [P, KC, NE]), sb("br", [P, NE])
        which = sb("which", [P, NE])
        stats, mv, std = sb("f_stats", [P, GT, 6]), sb("f_mv", [P, GT, 2]), sb("f_std", [P, GT])
        xn, xnT = sb("f_xn", [P, GT, D]), sb("f_xnT", [P, KC, GTOK])
        allT = sb("allT", [P, KC, TOK])
        logit, best = sb("logit", [P, GT, NE]), sb("best", [P, GT, NE])
        place = ctx.enter_context(nc.sbuf_tensor("place", [P, GT, NE], mybir.dt.uint32))
        placef = sb("placef", [P, GT, NE])
        first, second = sb("first", [P, GT, NE]), sb("second", [P, GT, NE])
        total = sb("f_total", [P, GT])
        share = sb("share", [P, NE, NT])
        mine = [sb(f"mine{r}", [P, NT]) for r in range(2)]
        hT = [sb(f"hT{r}", [P, FC, GTOK]) for r in range(2)]
        yb = [sb(f"yb{r}", [P, D]) for r in range(2)]
        up_bank = [bank(f"up_bank{r}") for r in range(4)]
        down_bank = [bank(f"down_bank{r}") for r in range(4)]
        loaded = sem("f_loaded")
        w_loaded = [sem(f"f_w_loaded{r}") for r in range(2)]
        chain, std_ready, normed = sem("f_chain"), sem("f_std_ready"), sem("f_normed")
        xT_filled, xT_kept, all_kept = sem("f_xT_filled"), sem("f_xT_kept"), sem("all_kept")
        r_filled, r_step, r_exp, share_ready = sem("r_filled"), sem("r_step"), sem("r_exp"), sem("share_ready")
        mine_ready = sem("mine_ready")
        up_filled, up_kept = sem("up_filled"), sem("up_kept")
        down_filled, down_read, added = [sem(f"down_filled{r}") for r in range(2)], sem("down_read"), sem("added")
        stored = sem("stored")
        passed = sem("f_passed")
        x_all, ident = keep["x_all"], keep["ident"]
        R_STEPS = 2 * GT + 9
        block = ctx.enter_context(nc.Block())
        EU = NG
        PER = 2 * EU

        @block.sync
        def _(sp):
            sp.dma_start(wr[:, :, :], dram["wr"].rearrange("(k p) n -> p k n", p=P)).then_inc(loaded, 16)
            sp.dma_start(br[:, :], dram["br"]).then_inc(loaded, 16)
            sp.dma_start(which[:, :], dram["which"]).then_inc(loaded, 16)

            def load_expert(e, r):
                sp.dma_start(w1[r][:, :, :], dram["w1"][bass.ds(e, 1)].rearrange("a (k p) f -> p (a k) f", p=P)).then_inc(w_loaded[r], 16)
                sp.dma_start(b1[r][:, :], dram["b1"][bass.ds(e, 1)].rearrange("a p f -> p (a f)")).then_inc(w_loaded[r], 16)
                sp.dma_start(w2[r][:, :, :], dram["w2"][bass.ds(e, 1)].rearrange("a (k p) f -> p (a k) f", p=P)).then_inc(w_loaded[r], 16)
                sp.dma_start(b2[r][:, :], dram["b2"][bass.ds(e, 1)].rearrange("a p f -> p (a f)")).then_inc(w_loaded[r], 16)

            load_expert(0, 0)
            load_expert(1, 1)
            with sp.Fori(1, NE // 2) as i:
                for r in range(2):
                    sp.wait_ge(added, GT * (PER * i - PER + (r + 1) * EU))
                    load_expert(2 * i + r, r)
            sp.wait_ge(added, GT * EU * NE)
            sp.dma_start(out.rearrange("(t p) d -> p t d", p=P), x_all[:, :, :]).then_inc(stored, 16)
            sp.wait_ge(stored, 16)

        @block.tensor
        def _(pe):
            pe.wait_ge(loaded, 48)
            with pe.Fori(0, NG) as g:
                pe.wait_ge(normed, g + 1)
                pe.wait_ge(xT_kept, KC * g)
                for k in range(KC):
                    for j in range(GT):
                        last = nc.tensor.transpose(up_bank[k][:, j * P:(j + 1) * P], xn[:, j, k * P:(k + 1) * P], ident[:, :])
                    last.then_inc(xT_filled, 1)
                pe.wait_ge(xT_kept, KC * (g + 1))
                pe.wait_ge(r_step, R_STEPS * g + 1)
                for j in range(GT):
                    for k in range(KC):
                        last = nc.tensor.matmul(down_bank[0][:, j * NE:(j + 1) * NE], xnT[:, k, j * P:(j + 1) * P],
                                                wr[:, k, :], start=(k == 0), stop=(k == KC - 1))
                last.then_inc(r_filled, 1)

            def up(i, u, again=True):
                r, g = u // EU % 2, u % EU
                if g == 0:
                    pe.wait_ge(w_loaded[r], 64 * (i + 1 + u // PER))
                for f in range(FC):
                    m = (i * PER + u) * FC + f
                    to = up_bank[f % 4]
                    if again or f >= 4:
                        pe.wait_ge(up_kept, m - 3)
                    for k in range(KC):
                        last = nc.tensor.matmul(to[:, :], w1[r][:, k, f * P:(f + 1) * P],
                                                allT[:, k, g * GTOK:(g + 1) * GTOK], start=(k == 0), stop=(k == KC - 1))
                    last.then_inc(up_filled, 1)

            def down(i, u):
                r = u // EU % 2
                pe.wait_ge(up_kept, (i * PER + u + 1) * FC)
                pe.wait_ge(down_read, (i * PER + u) * GT)
                for j in range(GT):
                    for f in range(FC):
                        last = nc.tensor.matmul(down_bank[j][:, 0:D], hT[u % 2][:, f, j * P:(j + 1) * P], w2[r][:, f, :],
                                                start=(f == 0), stop=(f == FC - 1))
                    last.then_inc(down_filled[u % 2], 1)

            pe.wait_ge(all_kept, NG)
            pe.wait_ge(r_step, R_STEPS * NG + 1)
            up(0, 0, again=False)
            with pe.Fori(0, NE // 2 - 1) as i:
                for u in range(PER):
                    up(i, u + 1)
                    down(i, u)
            for u in range(PER):
                if u + 1 < PER:
                    up(NE // 2 - 1, u + 1)
                down(NE // 2 - 1, u)

        @block.scalar
        def _(act):
            with act.Fori(0, NG) as g:
                layer_norm_root(act, nc, g, std, chain, std_ready)
                act.wait_ge(all_kept, g)
                act.wait_ge(r_filled, g)
                for k in range(KC):
                    act.wait_ge(xT_filled, KC * g + k + 1)
                    nc.scalar.copy(xnT[:, k, :], up_bank[k][:, :]).then_inc(xT_kept, 1)
                act.wait_ge(r_step, R_STEPS * (g + 1) - 2)
                nc.scalar.activation(logit[:, :, :], logit[:, :, :], ACT.Exp).then_inc(r_exp, 1)

            def relu(i, u):
                r = u // EU % 2
                if u % EU == 0:
                    act.wait_ge(w_loaded[r], 64 * (i + 1 + u // PER))
                act.wait_ge(down_filled[u % 2], (i * (PER // 2) + u // 2) * GT)
                for f in range(FC):
                    act.wait_ge(up_filled, (i * PER + u) * FC + f + 1)
                    nc.scalar.activation(hT[u % 2][:, f, :], up_bank[f % 4][:, :], ACT.Relu, bias=b1[r][:, f:f + 1]).then_inc(up_kept, 1)

            with act.Fori(0, NE // 2) as i:
                for u in range(PER):
                    relu(i, u)

        @block.gpsimd
        def _(pool):
            with pool.Fori(0, NG) as g:
                pool.wait_ge(xT_kept, KC * (g + 1))
                nc.gpsimd.tensor_copy(allT[:, :, bass.ds(g * GTOK, GTOK)], xnT[:, :, :]).then_inc(all_kept, 1)
            pool.wait_ge(share_ready, NG)
            with pool.Fori(0, NE // 2) as i:
                for r in range(2):
                    pool.wait_ge(added, GT * (PER * i + r * EU) if r else GT * PER * i)
                    nc.gpsimd.tensor_copy(mine[r][:, :], share[:, bass.ds(2 * i + r, 1), :].rearrange("p a t -> p (a t)")).then_inc(mine_ready, 1)

        @block.vector
        def _(dve):
            dve.wait_ge(loaded, 48)
            nc.vector.memset(total[:, :], 0.0).then_inc(r_step, 1)
            with dve.Fori(0, NG) as g:
                dve.wait_ge(xT_filled, KC * g)
                layer_norm(dve, nc, lambda j: x_all[:, bass.ds(g * GT + j, 1), :].rearrange("p a d -> p (a d)"),
                           g, stats, mv, std, xn, chain, std_ready, passed).then_inc(normed, 1)
                at = R_STEPS * g + 1
                dve.wait_ge(r_filled, g + 1)
                nc.vector.tensor_tensor(logit[:, :, :], down_bank[0][:, 0:GT * NE].rearrange("p (t e) -> p t e", t=GT),
                                        br[:, :].rearrange("p (a e) -> p a e", a=1).to_broadcast([P, GT, NE]), ALU.add).then_inc(r_step, 1)
                dve.wait_ge(r_step, at + 1)
                stand(dve, passed)
                for j in range(GT):
                    nc.vector.max(best[:, j, :], logit[:, j, :]).then_inc(r_step, 1)
                for j in range(GT):
                    dve.wait_ge(r_step, at + 2 + j)
                    stand(dve, passed)
                    nc.vector.max_index(place[:, j, :], best[:, j, :], logit[:, j, :]).then_inc(r_step, 1)
                at = at + 1 + 2 * GT
                dve.wait_ge(r_step, at)
                nc.vector.tensor_copy(placef[:, :, :], place[:, :, :]).then_inc(r_step, 1)
                dve.wait_ge(r_step, at + 1)
                ids = which[:, :].rearrange("p (a e) -> p a e", a=1).to_broadcast([P, GT, NE])
                nc.vector.tensor_tensor(first[:, :, :], ids, placef[:, :, 0:1].to_broadcast([P, GT, NE]), ALU.is_equal).then_inc(r_step, 1)
                nc.vector.tensor_tensor(second[:, :, :], ids, placef[:, :, 1:2].to_broadcast([P, GT, NE]), ALU.is_equal).then_inc(r_step, 1)
                dve.wait_ge(r_step, at + 3)
                nc.vector.tensor_tensor(first[:, :, :], first[:, :, :], second[:, :, :], ALU.add).then_inc(r_step, 1)
                nc.vector.tensor_tensor(logit[:, :, :], logit[:, :, :], best[:, :, 0:1].to_broadcast([P, GT, NE]), ALU.subtract).then_inc(r_step, 1)
                dve.wait_ge(r_step, at + 5)
                dve.wait_ge(r_exp, g + 1)
                nc.vector.tensor_tensor(first[:, :, :], first[:, :, :], logit[:, :, :], ALU.mult).then_inc(r_step, 1)
                dve.wait_ge(r_step, at + 6)
                nc.vector.tensor_reduce(total[:, :], first[:, :, :], AX.X, ALU.add).then_inc(r_step, 1)
                dve.wait_ge(r_step, at + 7)
                nc.vector.reciprocal(total[:, :], total[:, :]).then_inc(r_step, 1)
                dve.wait_ge(r_step, at + 8)
                nc.vector.tensor_tensor(share[:, :, bass.ds(g * GT, GT)], first[:, :, :].rearrange("p t e -> p e t"),
                                        total[:, :].rearrange("p (a t) -> p a t", a=1).to_broadcast([P, NE, GT]),
                                        ALU.mult).then_inc(share_ready, 1)
            with dve.Fori(0, NE // 2) as i:
                for u in range(PER):
                    r, g = u // EU % 2, u % EU
                    if g == 0:
                        dve.wait_ge(w_loaded[r], 64 * (i + 1))
                        dve.wait_ge(mine_ready, 2 * i + r + 1)
                    for j in range(GT):
                        m = (i * PER + u) * GT + j
                        dve.wait_ge(down_filled[u % 2], (i * (PER // 2) + u // 2) * GT + j + 1)
                        nc.vector.tensor_tensor(yb[j % 2][:, :], down_bank[j][:, 0:D], b2[r][:, :], ALU.add).then_inc(down_read, 1)
                        dve.wait_ge(down_read, m + 1)
                        t = g * GT + j
                        nc.vector.scalar_tensor_tensor(x_all[:, t, :], yb[j % 2][:, :], mine[r][:, t:t + 1], x_all[:, t, :],
                                                       ALU.mult, ALU.add).then_inc(added, 1)


def build_program(nc, dram, out):
    with ExitStack() as ctx:
        keep = {
            "x_all": ctx.enter_context(nc.sbuf_tensor("x_all", [P, NT, D], F32)),
            "ident": ctx.enter_context(nc.sbuf_tensor("ident", [P, P], F32)),
        }
        with ExitStack() as middle:
            keep["CT"] = middle.enter_context(nc.sbuf_tensor("CT", [P, KC, TOK], F32))
            with ExitStack() as inner:
                keep["QT"] = inner.enter_context(nc.sbuf_tensor("QT", [P, KC, TOK], F32))
                keep["headmask"] = inner.enter_context(nc.sbuf_tensor("headmask", [P, HG * LQ], F32))
                project_queries(nc, dram, keep)
                cross_attention(nc, dram, keep)
            gated_attention(nc, dram, keep)
        experts(nc, dram, keep, out)


def laid_out(inputs):
    c = np.ascontiguousarray
    a = {k: np.asarray(v) for k, v in inputs.items()}
    repeated = lambda v: np.broadcast_to(v.reshape(1, -1), (P, v.size))
    rows = np.arange(P) // HD
    query = np.arange(P) % LQ
    f = np.float32
    r = {
        "x": a["x"].reshape(TOK, D),
        "ctxT": c(a["ctx_1024"].transpose(0, 2, 1)).reshape(B, KC, P, S),
        "bias": a["fside_1x16xSxS2_0"].reshape(KC * PAIRS, P, S),
        "wq": a["L0_xattn_wq"].reshape(D, D),
        "wk": a["L0_xattn_wk"].reshape(D, D),
        "wv": a["L0_xattn_wv"].reshape(D, D),
        "bq": a["L0_xattn_bq"].reshape(KC, P).T,
        "bk": a["L0_xattn_bk"].reshape(KC, P).T,
        "bv": repeated(a["L0_xattn_bv"]),
        "wo_x": a["L0_xattn_wo"].reshape(D, D),
        "bo_x": repeated(a["L0_xattn_bo"]),
        "a_wq": a["L0_attn_Wq"],
        "a_wk": np.repeat(a["L0_attn_Wk"].reshape(D, KV, 1, DH), 2, axis=2).reshape(D, KV * 2 * DH),
        "a_wv": a["L0_attn_Wv"],
        "a_wg": a["L0_attn_Wg"],
        "a_wo": a["L0_attn_Wo"],
        "wr": a["L0_ffn_W_router"],
        "br": repeated(a["L0_ffn_b_router"]),
        "w1": a["L0_ffn_W1"],
        "w2": a["L0_ffn_W2"],
        "b1": a["L0_ffn_b1"].reshape(NE, FC, P).transpose(0, 2, 1),
        "b2": np.broadcast_to(a["L0_ffn_b2"][:, None, :], (NE, P, D)),
        "ident": np.eye(P, dtype=f),
        "headmask": np.repeat((rows[:, None] == np.arange(HG)[None, :]).astype(f), LQ, axis=1),
        "causal": np.tile(np.where(query[:, None] >= np.arange(LQ)[None, :], f(0), f(MASKED)), (1, GH)),
        "at_last": np.where(query == LQ - 1, f(1 / LQ), f(0))[:, None],
        "which": np.tile(np.arange(NE, dtype=f), (P, 1)),
    }
    return {k: c(v) for k, v in r.items()}


def kernel(**inputs):
    import concourse.bacc as bacc
    from concourse.bass_utils import run_bass_kernel_spmd

    arrays = laid_out(inputs)
    nc = bacc.Bacc("TRN2", target_bir_lowering=False, num_devices=1)
    dram = {name: nc.dram_tensor("in_" + name, v.shape, mybir.dt.from_np(v.dtype), kind="ExternalInput").ap()
            for name, v in arrays.items()}
    out = nc.dram_tensor("out", (TOK, D), F32, kind="ExternalOutput").ap()
    build_program(nc, dram, out)
    result = run_bass_kernel_spmd(nc, [{"in_" + name: v for name, v in arrays.items()}], core_ids=[0])
    return result.results[0]["out"].reshape(B, LQ, D)
```

```python
from contextlib import ExitStack

import numpy as np

import concourse.bass as bass
from concourse import mybir

F32 = mybir.dt.float32
F32R = mybir.dt.float32r
ALU = mybir.AluOpType
ACT = mybir.ActivationFunctionType
AX = mybir.AxisListType

P = 128
B, LQ, D = 32, 64, 256
S = 1601
TOK = B * LQ
NT = TOK // P
KC = D // P
H, HD = 16, 16
HG = P // HD
NPAIR = H // 2
QH, NQ = 4, H // 4
SP = S + 1
COLS = [(0, 402), (402, 400), (802, 400), (1202, 400)]
HALVES = [(0, 802), (802, S)]
NCOL = len(COLS)
ST = -(-S // P)
LAST = S - (ST - 1) * P
TB = -(-ST // 2)
PIECES = 2 * NCOL
PIECES_AT = [2, 2, 2, 1, 1, 0, 0]
EXP_AT = {2: (0, 0), 3: (0, 1), 5: (1, 0)}
SECOND_AT = HALVES[1][0] // P // 2
SUMS_AT, FOLD_AT, CT_AT = 1, 2, 4
GT = 4
GTOK = GT * P
NG = TOK // GTOK
EPS = 1e-5
LOWEST = -3.0e38

NH, KV, DH = 32, 4, 64
GH = NH // KV
QC = NH * DH // P
CH = GH // 2
GB = GTOK // LQ
UNITS = GT * KV
AHEAD, RING = 3, 4
NP = QC + KV + GB // 2 + 1
NPR = [-(-NP // 2), NP // 2]
MASKED = -1.0e30

NE, FF = 8, 1024
FC = FF // P


def rows_of(t):
    return P if t < ST - 1 else LAST


def stand(eng, passed):
    eng.sem_inc(passed, 1)


def layer_norm(dve, nc, x_of, step, stats, mv, std, xn, chain, std_ready, passed):
    at = step * LN_STEPS
    stand(dve, passed)
    for j in range(GT):
        nc.vector.bn_stats(stats[:, j, :], x_of(j)).then_inc(chain, 1)
    for j in range(GT):
        dve.wait_ge(chain, at + j + 1)
        stand(dve, passed)
        nc.vector.bn_aggr(mv[:, j, :], stats[:, j, :]).then_inc(chain, 1)
    dve.wait_ge(chain, at + 2 * GT)
    nc.vector.tensor_scalar(std[:, :], mv[:, :, 1], EPS, None, ALU.add).then_inc(chain, 1)
    dve.wait_ge(std_ready, step + 1)
    nc.vector.reciprocal(std[:, :], std[:, :]).then_inc(chain, 1)
    dve.wait_ge(chain, at + LN_STEPS)
    for j in range(GT):
        last = nc.vector.tensor_scalar(xn[:, j, :], x_of(j), mv[:, j, 0:1], std[:, j:j + 1],
                                       ALU.subtract, ALU.mult)
    return last


LN_STEPS = 2 * GT + 2


def layer_norm_root(act, nc, step, std, chain, std_ready):
    act.wait_ge(chain, step * LN_STEPS + 2 * GT + 1)
    nc.scalar.activation(std[:, :], std[:, :], ACT.Sqrt).then_inc(std_ready, 1)


def project_queries(nc, dram, keep):
    with ExitStack() as ctx:
        sb = lambda name, shape: ctx.enter_context(nc.sbuf_tensor(name, shape, F32))
        sem = lambda name: ctx.enter_context(nc.semaphore(name))
        wq = sb("wq", [P, KC, D])
        bq = sb("bq", [P, KC])
        stats, mv, std = sb("q_stats", [P, GT, 6]), sb("q_mv", [P, GT, 2]), sb("q_std", [P, GT])
        xn = sb("q_xn", [P, GT, D])
        xnT = sb("q_xnT", [P, KC, GTOK])
        turned = [ctx.enter_context(nc.psum_tensor(f"q_turned{k}", [P, GTOK], F32)) for k in range(KC)]
        proj = [ctx.enter_context(nc.psum_tensor(f"q_proj{c}", [P, GTOK], F32)) for c in range(KC)]
        loaded, chain, std_ready, normed = sem("q_loaded"), sem("q_chain"), sem("q_std_ready"), sem("q_normed")
        xT_filled, xT_kept = sem("q_xT_filled"), sem("q_xT_kept")
        q_filled, q_kept = sem("q_filled"), sem("q_kept")
        passed = sem("q_passed")
        x_all = sb("q_x", [P, NT, D])
        QT, ident = keep["heads"], keep["ident"]
        block = ctx.enter_context(nc.Block())

        @block.sync
        def _(sp):
            sp.dma_start(x_all[:, :, :], dram["x"].rearrange("(t p) d -> p t d", p=P)).then_inc(loaded, 16)
            sp.dma_start(ident[:, :], dram["ident"]).then_inc(loaded, 16)
            sp.dma_start(wq[:, :, :], dram["wq"].rearrange("(k p) n -> p k n", p=P)).then_inc(loaded, 16)
            sp.dma_start(bq[:, :], dram["bq"]).then_inc(loaded, 16)
            sp.dma_start(keep["headmask"][:, :], dram["headmask"]).then_inc(loaded, 16)

        @block.vector
        def _(dve):
            dve.wait_ge(loaded, 80)
            with dve.Fori(0, NG) as g:
                dve.wait_ge(xT_filled, KC * g)
                layer_norm(dve, nc, lambda j: x_all[:, bass.ds(g * GT + j, 1), :].rearrange("p a d -> p (a d)"),
                           g, stats, mv, std, xn, chain, std_ready, passed).then_inc(normed, 1)
                for c in range(KC):
                    dve.wait_ge(q_filled, KC * g + c + 1)
                    nc.vector.tensor_scalar(QT[:, c, bass.ds(g * GTOK, GTOK)], proj[c][:, :], bq[:, c:c + 1],
                                            float(HD) ** -0.5, ALU.add, ALU.mult).then_inc(q_kept, 1)

        @block.scalar
        def _(act):
            with act.Fori(0, NG) as g:
                layer_norm_root(act, nc, g, std, chain, std_ready)
                for k in range(KC):
                    act.wait_ge(xT_filled, KC * g + k + 1)
                    act.wait_ge(q_filled, KC * g)
                    nc.scalar.copy(xnT[:, k, :], turned[k][:, :]).then_inc(xT_kept, 1)

        @block.tensor
        def _(pe):
            pe.wait_ge(loaded, 80)
            with pe.Fori(0, NG) as g:
                pe.wait_ge(normed, g + 1)
                for k in range(KC):
                    pe.wait_ge(xT_kept, KC * g)
                    for j in range(GT):
                        last = nc.tensor.transpose(turned[k][:, j * P:(j + 1) * P], xn[:, j, k * P:(k + 1) * P], ident[:, :])
                    last.then_inc(xT_filled, 1)
                pe.wait_ge(xT_kept, KC * (g + 1))
                for c in range(KC):
                    pe.wait_ge(q_kept, KC * g)
                    for k in range(KC):
                        last = nc.tensor.matmul(proj[c][:, :], wq[:, k, c * P:(c + 1) * P], xnT[:, k, :],
                                                start=(k == 0), stop=(k == KC - 1))
                    last.then_inc(q_filled, 1)


def cross_attention(nc, dram, keep):
    with ExitStack() as ctx:
        sb = lambda name, shape, dt=F32: ctx.enter_context(nc.sbuf_tensor(name, shape, dt))
        bank = lambda name: ctx.enter_context(nc.psum_tensor(name, [P, 512], F32))
        sem = lambda name: ctx.enter_context(nc.semaphore(name))
        pair = lambda name, shape: [sb(name + part, shape, F32R) for part in ("_high", "_low")]
        raw_w = sb("raw_w", [P, KC, D])
        wk, wv = pair("wk", [P, KC, D]), pair("wv", [P, KC, D])
        bk, bv = sb("bk", [P, KC]), sb("bv", [P, 2])
        fold = sb("fold", [P, QH, HD])
        bias = sb("bias", [P, NPAIR, S])
        raw_c = [sb(f"raw_c{r}", [P, SP // 2]) for r in range(2)]
        cT = pair("cT", [P, KC, SP])
        KT = pair("KT", [P, KC, SP])
        V = sb("V", [P, ST, NQ, 2, QH * HD], F32R)
        raw_q = sb("raw_q", [P, QH, LQ])
        QB = [pair(f"QB{r}", [P, QH, LQ]) for r in range(2)]
        probs = [sb(f"probs{r}", [P, 2, S]) for r in range(2)]
        PT = [pair(f"PT{r}", [P, 2, QH * LQ]) for r in range(2)]
        top = [sb(f"top{r}", [P, 2, NCOL]) for r in range(2)]
        neg_max = [sb(f"neg_max{r}", [P, 2]) for r in range(2)]
        total = [sb(f"total{r}", [P, 2, 2]) for r in range(2)]
        inverse = [sb(f"inverse{r}", [P, 2]) for r in range(2)]
        raw_out = [sb(f"raw_out{r}", [P, QH, LQ]) for r in range(2)]
        by_query = sb("by_query", [P, NPAIR, HD])
        score_bank = [bank(f"score_bank{r}") for r in range(2)]
        turn_bank = [bank(f"turn_bank{r}") for r in range(2)]
        proj_bank = [bank(f"proj_bank{r}") for r in range(2)]
        out_bank = [bank(f"out_bank{r}") for r in range(2)]

        wk_loaded, wv_loaded, loaded = sem("wk_loaded"), sem("wv_loaded"), sem("loaded")
        w_step = sem("w_step")
        c_loaded, c_ready = [sem(f"c_loaded{r}") for r in range(2)], sem("c_ready")
        c_high, q_high, q_raw = sem("c_high"), sem("q_high"), sem("q_raw")
        k_filled, k_high, k_kept = sem("k_filled"), sem("k_high"), sem("k_kept")
        v_filled, v_high, v_kept = sem("v_filled"), sem("v_high"), sem("v_kept")
        qb_ready = sem("qb_ready")
        s_filled, s_read = sem("s_filled"), sem("s_read")
        max_ready, exp_done = sem("max_ready"), sem("exp_done")
        sums_step, sums_taken = sem("sums_step"), sem("sums_taken")
        t_filled = [sem(f"t_filled{r}") for r in range(2)]
        t_high = [sem(f"t_high{r}") for r in range(2)]
        t_kept = [sem(f"t_kept{r}") for r in range(2)]
        t_used = [sem(f"t_used{r}") for r in range(2)]
        out_read, folded, scaled = sem("out_read"), sem("folded"), sem("scaled")
        ct_turned, ct_ready = sem("ct_turned"), sem("ct_ready")
        passed, passed_dve = sem("passed"), sem("passed_dve")
        heads, ident, headmask = keep["heads"], keep["ident"], keep["headmask"]
        nk = KC * NCOL
        vf = TB
        ONE, TWO = 1, 2
        block = ctx.enter_context(nc.Block())

        def turn_of(b, a, f):
            r = (a * TB + f) % 2
            before = sum((x % 2) == r for x in range(a * TB + f))
            return r, b * (NQ * TB // 2) + before

        def after(b, a):
            return (b, a + 1) if a + 1 < NQ else (b + 1, 0)

        def unit(b, a):
            return b * NQ + a

        def tiles_of(f):
            return range(2 * f, min(2 * f + 2, ST))

        @block.sync
        def _(sp):
            sp.dma_start(raw_w[:, :, :], dram["wk"].rearrange("(k p) n -> p k n", p=P)).then_inc(wk_loaded, 16)

            def load_context(b):
                for k in range(KC):
                    for half in range(2):
                        i = 2 * k + half
                        sp.wait_ge(c_ready, 4 * b + i - 1 + TWO)
                        sp.dma_start(raw_c[half][:, :], dram["ctxT"][bass.ds(b, 1), k, :, half * (SP // 2):(half + 1) * (SP // 2)]
                                     .rearrange("a p s -> p (a s)")).then_inc(c_loaded[half], 16)

            sp.sem_inc(c_ready, TWO)
            load_context(0)
            sp.wait_ge(w_step, 2)
            sp.dma_start(raw_w[:, :, :], dram["wv"].rearrange("(k p) n -> p k n", p=P)).then_inc(wv_loaded, 16)
            sp.dma_start(bk[:, :], dram["bk"]).then_inc(loaded, 16)
            sp.dma_start(bv[:, :], dram["bv"]).then_inc(loaded, 16)
            sp.dma_start(fold[:, :, :], dram["fold"]).then_inc(loaded, 16)
            sp.dma_start(bias[:, :, :], dram["bias"].rearrange("r p s -> p r s")).then_inc(loaded, 16)
            with sp.Fori(1, B) as b:
                load_context(b)

        @block.gpsimd
        def _(pool):
            def context_low(b, k):
                for half in range(2):
                    cols = slice(half * (SP // 2), (half + 1) * (SP // 2))
                    pool.wait_ge(c_high, 4 * b + 2 * k + half + 1)
                    nc.gpsimd.tensor_tensor(cT[1][:, k, cols], raw_c[half][:, :], cT[0][:, k, cols].bitcast(F32),
                                            ALU.subtract).then_inc(c_ready, 1)

            def spread_q(b, a, again=True):
                r, u = a % 2, unit(b, a)
                mask = headmask[:, :].rearrange("p (h q) -> p h q", h=HG)[:, r * QH:(r + 1) * QH, :]
                q = heads[:, a // 2:a // 2 + 1, bass.ds(b * LQ, LQ)].to_broadcast([P, QH, LQ])
                if again:
                    pool.wait_ge(s_filled, PIECES * (u - 1))
                    pool.wait_ge(qb_ready, u)
                    stand(pool, passed)
                elif a:
                    pool.wait_ge(qb_ready, u)
                nc.gpsimd.tensor_tensor(QB[r][0][:, :, :], q, mask, ALU.mult).then_inc(q_high, 1)
                nc.gpsimd.tensor_tensor(raw_q[:, :, :], q, mask, ALU.mult).then_inc(q_raw, 1)
                pool.wait_ge(q_high, u + 1)
                pool.wait_ge(q_raw, u + 1)
                nc.gpsimd.tensor_tensor(QB[r][1][:, :, :], raw_q[:, :, :], QB[r][0][:, :, :].bitcast(F32),
                                        ALU.subtract).then_inc(qb_ready, 1)

            context_low(0, 0)
            context_low(0, 1)
            spread_q(0, 0, again=False)
            spread_q(0, 1, again=False)
            with pool.Fori(0, B - 1) as b:
                spread_q(b, 2)
                context_low(b + 1, 0)
                spread_q(b, 3)
                context_low(b + 1, 1)
                spread_q(b + 1, 0)
                spread_q(b + 1, 1)
            spread_q(B - 1, 2)
            spread_q(B - 1, 3)

        @block.tensor
        def _(pe):
            def three(to, left, right, n_k=KC):
                todo = [(k, x, y) for k in range(n_k) for x, y in ((0, 0), (0, 1), (1, 0))]
                for i, (k, x, y) in enumerate(todo):
                    last = nc.tensor.matmul(to, left(k, x), right(k, y), start=(i == 0), stop=(i == len(todo) - 1))
                return last

            def project_k(b):
                pe.wait_ge(c_ready, 4 * b + 4 + TWO)
                pe.wait_ge(v_kept, vf * b + ONE)
                for c in range(KC):
                    for j, (at, n) in enumerate(COLS):
                        i = c * NCOL + j
                        if i >= 2:
                            pe.wait_ge(k_kept, nk * b + i - 1)
                        three(proj_bank[i % 2][:, 0:n], lambda k, x: wk[x][:, k, c * P:(c + 1) * P],
                              lambda k, y: cT[y][:, k, at:at + n]).then_inc(k_filled, 1)

            def project_v(b):
                pe.wait_ge(k_kept, nk * b + nk)
                for f in range(TB):
                    if f >= 2:
                        pe.wait_ge(v_kept, vf * b + f - 1 + ONE)
                    for t in tiles_of(f):
                        n = rows_of(t)
                        last = three(proj_bank[f % 2][0:n, (t % 2) * D:(t % 2 + 1) * D],
                                     lambda k, x: cT[x][:, k, t * P:t * P + n], lambda k, y: wv[y][:, k, :])
                    last.then_inc(v_filled, 1)

            def piece(b, a, m):
                u = unit(b, a)
                i, (at, n) = m // NCOL, COLS[m % NCOL]
                if m == 0:
                    pe.wait_ge(qb_ready, u + 1)
                    pe.wait_ge(k_kept, nk * b + (a // 2 + 1) * NCOL)
                pe.wait_ge(s_read, PIECES * u + m - 1 + TWO)
                three(score_bank[m % 2][:, 0:n], lambda k, x: QB[a % 2][x][:, 2 * i:2 * i + 2, :],
                      lambda k, y: KT[y][:, a // 2, at:at + n], 1).then_inc(s_filled, 1)

            def turn(b, a, f):
                u = unit(b, a)
                r, before = turn_of(b, a, f)
                if f == 0:
                    pe.wait_ge(exp_done, 4 * u + 3)
                if f == SECOND_AT:
                    pe.wait_ge(exp_done, 4 * u + 4)
                pe.wait_ge(t_kept[r], before + ONE)
                for t in tiles_of(f):
                    n = rows_of(t)
                    for i in range(2):
                        last = nc.tensor.transpose(turn_bank[r][0:n, (t % 2) * D + i * P:(t % 2) * D + (i + 1) * P],
                                                   probs[a % 2][:, i, t * P:t * P + n], ident[:, :])
                last.then_inc(t_filled[r], 1)

            def weigh(b, a, f):
                r, before = turn_of(b, a, f)
                if f == 0:
                    u = unit(b, a)
                    pe.wait_ge(v_kept, vf * b + vf + ONE)
                    pe.wait_ge(scaled, u - 1 + TWO)
                    if a % 2:
                        pe.wait_ge(ct_ready, b + ONE)
                pe.wait_ge(t_kept[r], before + 1 + ONE)
                for t in tiles_of(f):
                    n = rows_of(t)
                    for part in range(2):
                        last = nc.tensor.matmul(out_bank[a % 2][:, 0:D], V[0:n, t, a, :, :], PT[r][part][0:n, t % 2, :],
                                                start=(t == 0 and part == 0), stop=(t == ST - 1 and part == 1))
                last.then_inc(t_used[r], 1)

            def fold_heads(b, a):
                u = unit(b, a)
                pe.wait_ge(out_read, u + 1)
                for h in range(QH):
                    last = nc.tensor.matmul(out_bank[a % 2][(h % 2) * LQ:(h % 2 + 1) * LQ, D + (h // 2) * HD:D + (h // 2 + 1) * HD],
                                            raw_out[a % 2][:, h, :], fold[:, h, :], start=True, stop=True)
                last.then_inc(folded, 1)

            def turn_heads(b):
                pe.wait_ge(scaled, NQ * (b + 1) + TWO)
                nc.tensor.transpose(out_bank[1][:, 384:512], by_query[:, :, :], ident[:, :]).then_inc(ct_turned, 1)

            def step(b, a, scores=True, before=None):
                turn(b, a, 0)
                m = 0
                for f in range(TB):
                    for _ in range(PIECES_AT[f] if scores else 0):
                        piece(*after(b, a), m)
                        m += 1
                    if f + 1 < TB:
                        turn(b, a, f + 1)
                    weigh(b, a, f)
                    if f == FOLD_AT and before is not None:
                        fold_heads(*before)
                    if f == CT_AT and before is not None and a == 0:
                        turn_heads(before[0])

            pe.sem_inc(s_read, TWO)
            pe.sem_inc(v_kept, ONE)
            pe.sem_inc(scaled, TWO)
            pe.sem_inc(ct_ready, ONE)
            for r in range(2):
                pe.sem_inc(t_kept[r], ONE)
            pe.wait_ge(w_step, 4)
            project_k(0)
            pe.wait_ge(loaded, 64)
            for m in range(PIECES):
                piece(0, 0, m)
            project_v(0)
            step(0, 0)
            step(0, 1, before=(0, 0))
            step(0, 2, before=(0, 1))
            project_k(1)
            step(0, 3, before=(0, 2))
            project_v(1)
            with pe.Fori(1, B - 1) as b:
                step(b, 0, before=(b - 1, 3))
                step(b, 1, before=(b, 0))
                step(b, 2, before=(b, 1))
                project_k(b + 1)
                step(b, 3, before=(b, 2))
                project_v(b + 1)
            step(B - 1, 0, before=(B - 2, 3))
            step(B - 1, 1, before=(B - 1, 0))
            step(B - 1, 2, before=(B - 1, 1))
            step(B - 1, 3, scores=False, before=(B - 1, 2))
            fold_heads(B - 1, 3)
            turn_heads(B - 1)

        @block.scalar
        def _(act):
            def context_high(b, k):
                act.wait_ge(v_filled, vf * b + ONE)
                for half in range(2):
                    cols = slice(half * (SP // 2), (half + 1) * (SP // 2))
                    act.wait_ge(c_loaded[half], 32 * b + 16 * k + 16)
                    nc.scalar.copy(cT[0][:, k, cols], raw_c[half][:, :]).then_inc(c_high, 1)

            def keep_k(b):
                for c in range(KC):
                    for j, (at, n) in enumerate(COLS):
                        i = c * NCOL + j
                        act.wait_ge(k_filled, nk * b + i + 1)
                        nc.scalar.activation(KT[0][:, c, at:at + n], proj_bank[i % 2][:, 0:n], ACT.Identity,
                                             bias=bk[:, c:c + 1]).then_inc(k_high, 1)

            def keep_v(b):
                for f in range(TB):
                    act.wait_ge(v_filled, vf * b + f + 1 + ONE)
                    n, m = rows_of(2 * f), len(tiles_of(f))
                    nc.scalar.copy(V[0:n, 2 * f:2 * f + m, :, 0, :],
                                   proj_bank[f % 2][0:n, 0:m * D].rearrange("p (t a c) -> p t a c", t=m, a=NQ)).then_inc(v_high, 1)

            def exponentials(b, a, i, half):
                u, r = unit(b, a), a % 2
                at, to = HALVES[half]
                act.wait_ge(max_ready, 2 * u + i + 1)
                if i == 0 and half == 0:
                    act.wait_ge(sums_taken, u - 1 + TWO)
                nc.scalar.activation(probs[r][:, i, at:to], probs[r][:, i, at:to], ACT.Exp, bias=neg_max[r][:, i:i + 1],
                                     accum_out=total[r][:, i, half:half + 1]).then_inc(exp_done, 1)

            def keep_turned(b, a, f):
                r, before = turn_of(b, a, f)
                n, m = rows_of(2 * f), len(tiles_of(f))
                act.wait_ge(t_filled[r], before + 1)
                act.wait_ge(t_used[r], before + ONE)
                nc.scalar.copy(PT[r][0][0:n, 0:m, :], turn_bank[r][0:n, 0:m * D].rearrange("p (t c) -> p t c", t=m))\
                    .then_inc(t_high[r], 1)

            def keep_product(b, a):
                u = unit(b, a)
                r, before = turn_of(b, a, TB - 1)
                act.wait_ge(t_used[r], before + 1 + ONE)
                act.wait_ge(folded, u - 1 + TWO)
                nc.scalar.copy(raw_out[a % 2][:, :, :], out_bank[a % 2][:, 0:D].rearrange("p (h q) -> p h q", h=QH))\
                    .then_inc(out_read, 1)

            def step(b, a, scores=True, before=None):
                for f in range(TB):
                    if f == 0 and before is not None:
                        keep_product(*before)
                    keep_turned(b, a, f)
                    if f == 0:
                        exponentials(b, a, 1, 1)
                    if scores and f in EXP_AT:
                        exponentials(*after(b, a), *EXP_AT[f])

            act.sem_inc(v_filled, ONE)
            act.sem_inc(sums_taken, TWO)
            act.sem_inc(folded, TWO)
            for r in range(2):
                act.sem_inc(t_used[r], ONE)
            context_high(0, 0)
            context_high(0, 1)
            act.wait_ge(loaded, 64)
            keep_k(0)
            for i, half in EXP_AT.values():
                exponentials(0, 0, i, half)
            keep_v(0)
            step(0, 0)
            context_high(1, 0)
            step(0, 1, before=(0, 0))
            context_high(1, 1)
            step(0, 2, before=(0, 1))
            keep_k(1)
            step(0, 3, before=(0, 2))
            keep_v(1)
            with act.Fori(1, B - 1) as b:
                step(b, 0, before=(b - 1, 3))
                context_high(b + 1, 0)
                step(b, 1, before=(b, 0))
                context_high(b + 1, 1)
                step(b, 2, before=(b, 1))
                keep_k(b + 1)
                step(b, 3, before=(b, 2))
                keep_v(b + 1)
            step(B - 1, 0, before=(B - 2, 3))
            step(B - 1, 1, before=(B - 1, 0))
            step(B - 1, 2, before=(B - 1, 1))
            step(B - 1, 3, scores=False, before=(B - 1, 2))
            keep_product(B - 1, 3)

        @block.vector
        def _(dve):
            def keep_k(b):
                for c in range(KC):
                    for j, (at, n) in enumerate(COLS):
                        i = c * NCOL + j
                        dve.wait_ge(k_high, nk * b + i + 1)
                        nc.vector.scalar_tensor_tensor(KT[1][:, c, at:at + n], proj_bank[i % 2][:, 0:n], bk[:, c:c + 1],
                                                       KT[0][:, c, at:at + n].bitcast(F32), ALU.add, ALU.subtract).then_inc(k_kept, 1)

            def keep_v(b):
                for f in range(TB):
                    dve.wait_ge(v_high, vf * b + f + 1)
                    n, m = rows_of(2 * f), len(tiles_of(f))
                    nc.vector.tensor_tensor(V[0:n, 2 * f:2 * f + m, :, 1, :],
                                            proj_bank[f % 2][0:n, 0:m * D].rearrange("p (t a c) -> p t a c", t=m, a=NQ),
                                            V[0:n, 2 * f:2 * f + m, :, 0, :].bitcast(F32), ALU.subtract).then_inc(v_kept, 1)

            def logits(b, a, m):
                u, r = unit(b, a), a % 2
                i, j = m // NCOL, m % NCOL
                at = COLS[j][0]
                n = min(COLS[j][1], S - at)
                dve.wait_ge(s_filled, PIECES * u + m + 1)
                stand(dve, passed_dve)
                nc.vector.tensor_tensor_reduce(probs[r][:, i, at:at + n], score_bank[m % 2][:, 0:n],
                                               bias[:, 2 * a + i, at:at + n], 1.0, LOWEST,
                                               ALU.add, ALU.max, top[r][:, i, j:j + 1]).then_inc(s_read, 1)
                if j == NCOL - 1:
                    dve.wait_ge(s_read, PIECES * u + m + 1 + TWO)
                    nc.vector.tensor_reduce(neg_max[r][:, i:i + 1], top[r][:, i, :], AX.X, ALU.max,
                                            negate=True).then_inc(max_ready, 1)

            def keep_turned(b, a, f):
                r, before = turn_of(b, a, f)
                n, m = rows_of(2 * f), len(tiles_of(f))
                dve.wait_ge(t_high[r], before + 1)
                nc.vector.tensor_tensor(PT[r][1][0:n, 0:m, :], turn_bank[r][0:n, 0:m * D].rearrange("p (t c) -> p t c", t=m),
                                        PT[r][0][0:n, 0:m, :].bitcast(F32), ALU.subtract).then_inc(t_kept[r], 1)

            def invert_sums(b, a):
                u, r = unit(b, a), a % 2
                dve.wait_ge(exp_done, 4 * u + 4)
                nc.vector.tensor_tensor(inverse[r][:, :], total[r][:, :, 0], total[r][:, :, 1], ALU.add).then_inc(sums_taken, 1)
                dve.wait_ge(sums_taken, u + 1 + TWO)
                nc.vector.reciprocal(inverse[r][:, :], inverse[r][:, :]).then_inc(sums_step, 1)

            def scale_heads(b, a):
                u, r = unit(b, a), a % 2
                dve.wait_ge(folded, u + 1 + TWO)
                dve.wait_ge(sums_step, u + 1)
                nc.vector.tensor_tensor(by_query[:, 2 * a:2 * a + 2, :], out_bank[r][:, D:D + 2 * HD].rearrange("p (i d) -> p i d", i=2),
                                        inverse[r][:, :].rearrange("p (i x) -> p i x", x=1).to_broadcast([P, 2, HD]),
                                        ALU.mult).then_inc(scaled, 1)

            def keep_heads(b):
                dve.wait_ge(ct_turned, b + 1)
                nc.vector.tensor_tensor(heads[:, :, bass.ds(b * LQ, LQ)], out_bank[1][:, 384:512].rearrange("p (h q) -> p h q", h=2),
                                        bv[:, :].rearrange("p (h x) -> p h x", x=1).to_broadcast([P, 2, LQ]), ALU.add).then_inc(ct_ready, 1)

            def step(b, a, scores=True, before=None):
                m = 0
                for f in range(TB):
                    keep_turned(b, a, f)
                    for _ in range(PIECES_AT[f] if scores else 0):
                        logits(*after(b, a), m)
                        m += 1
                    if f == SUMS_AT:
                        invert_sums(b, a)
                    if f == FOLD_AT + 1 and before is not None:
                        scale_heads(*before)
                    if f == CT_AT + 1 and before is not None and a == 0:
                        keep_heads(before[0])

            for i, (w, arrived) in enumerate(((wk, wk_loaded), (wv, wv_loaded))):
                dve.wait_ge(arrived, 16)
                nc.vector.tensor_copy(w[0][:, :, :], raw_w[:, :, :]).then_inc(w_step, 1)
                dve.wait_ge(w_step, 2 * i + 1)
                nc.vector.tensor_tensor(w[1][:, :, :], raw_w[:, :, :], w[0][:, :, :].bitcast(F32), ALU.subtract).then_inc(w_step, 1)
            dve.wait_ge(loaded, 64)
            keep_k(0)
            for m in range(PIECES):
                logits(0, 0, m)
            keep_v(0)
            step(0, 0)
            step(0, 1, before=(0, 0))
            step(0, 2, before=(0, 1))
            keep_k(1)
            step(0, 3, before=(0, 2))
            keep_v(1)
            with dve.Fori(1, B - 1) as b:
                step(b, 0, before=(b - 1, 3))
                step(b, 1, before=(b, 0))
                step(b, 2, before=(b, 1))
                keep_k(b + 1)
                step(b, 3, before=(b, 2))
                keep_v(b + 1)
            step(B - 1, 0, before=(B - 2, 3))
            step(B - 1, 1, before=(B - 1, 0))
            step(B - 1, 2, before=(B - 1, 1))
            step(B - 1, 3, scores=False, before=(B - 1, 2))
            scale_heads(B - 1, 3)
            keep_heads(B - 1)


def gated_attention(nc, dram, keep):
    with ExitStack() as ctx:
        sb = lambda name, shape: ctx.enter_context(nc.sbuf_tensor(name, shape, F32))
        bank = lambda name: ctx.enter_context(nc.psum_tensor(name, [P, 512], F32))
        sem = lambda name: ctx.enter_context(nc.semaphore(name))
        wo_x, bo_x = sb("wo_x", [P, KC, D]), sb("bo_x", [P, D])
        wq, wk = sb("a_wq", [P, KC, NH * DH]), sb("a_wk", [P, KC, KV * 2 * DH])
        wv, wg, wo = sb("a_wv", [P, KC, KV * DH]), sb("a_wg", [P, KC, NH * 3]), sb("a_wo", [P, QC, D])
        causal, at_last = sb("causal", [P, GH * LQ]), sb("at_last", [P, 1])
        heads = sb("heads", [P, KC, GTOK])
        stats, mv, std = sb("a_stats", [P, GT, 6]), sb("a_mv", [P, GT, 2]), sb("a_std", [P, GT])
        xn, xnT = sb("a_xn", [P, GT, D]), sb("a_xnT", [P, KC, GTOK])
        xn_twice = sb("xn_twice", [P, KC * GB, 2, LQ])
        QT = sb("a_QT", [P, QC, GTOK])
        KB = sb("a_KB", [P, KV, GB, 2, LQ])
        VB = sb("a_VB", [P, GB, KV, 2, DH])
        gate = sb("gate", [P, GT, NH * 3])
        gate_near, gate_mean = sb("gate_near", [P, GT, NH]), sb("gate_mean", [P, GT, NH])
        A = [sb(f"A{r}", [P, GH, LQ]) for r in range(RING)]
        top = [sb(f"a_top{r}", [P, GH]) for r in range(RING)]
        total = [sb(f"a_total{r}", [P, GH]) for r in range(RING)]
        AT = [sb(f"AT{r}", [P, CH, 2, LQ]) for r in range(2)]
        OT = [sb(f"OT{r}", [P, QC, 2, LQ]) for r in range(2)]
        proj_bank = [bank(f"a_proj_bank{r}") for r in range(2)]
        score_bank = [bank(f"a_score_bank{r}") for r in range(2)]
        turn_bank = [bank(f"a_turn_bank{r}") for r in range(2)]
        out_bank = [bank(f"a_out_bank{r}") for r in range(2)]

        loaded, zeroed = sem("a_loaded"), sem("a_zeroed")
        heads_ready, bo_added = sem("heads_ready"), sem("bo_added")
        h_filled, h_added = sem("h_filled"), sem("h_added")
        chain, std_ready, normed = sem("a_chain"), sem("a_std_ready"), sem("a_normed")
        xT_filled, xT_kept, twice_ready = sem("a_xT_filled"), sem("a_xT_kept"), sem("twice_ready")
        p_filled, p_kept = sem("p_filled"), [sem(f"p_kept{r}") for r in range(2)]
        gate_step, gate_ready = sem("gate_step"), sem("gate_ready")
        s_filled, s_read = sem("a_s_filled"), sem("a_s_read")
        top_ready, moved, exp_done = sem("a_top_ready"), sem("a_moved"), sem("a_exp_done")
        sum_step, scale_ready, scaled, A_ready = sem("a_sum_step"), sem("a_scale_ready"), sem("a_scaled"), sem("A_ready")
        t_filled, t_kept, o_filled, o_kept = sem("a_t_filled"), sem("a_t_kept"), sem("o_filled"), sem("o_kept")
        w_filled, w_added = sem("w_filled"), sem("w_added")
        passed, passed_pool = sem("a_passed"), sem("a_passed_pool")
        x_all, CT, ident = keep["x_all"], keep["heads"], keep["ident"]
        N_LOAD = 10 * 16
        GATE_FILL = NP - 1
        block = ctx.enter_context(nc.Block())

        def since(g, per, n, ring):
            return g * per + max(n + 1 - ring, 0)

        @block.sync
        def _(sp):
            chunked = lambda ap: ap.rearrange("(k p) n -> p k n", p=P)
            sp.dma_start(x_all[:, :, :], dram["x"].rearrange("(t p) d -> p t d", p=P)).then_inc(loaded, 16)
            sp.dma_start(wo_x[:, :, :], chunked(dram["wo_x"])).then_inc(loaded, 16)
            sp.dma_start(bo_x[:, :], dram["bo_x"]).then_inc(loaded, 16)
            sp.dma_start(wq[:, :, :], chunked(dram["a_wq"])).then_inc(loaded, 16)
            sp.dma_start(wk[:, :, :], chunked(dram["a_wk"])).then_inc(loaded, 16)
            sp.dma_start(wv[:, :, :], chunked(dram["a_wv"])).then_inc(loaded, 16)
            sp.dma_start(wg[:, :, :], chunked(dram["a_wg"])).then_inc(loaded, 16)
            sp.dma_start(wo[:, :, :], chunked(dram["a_wo"])).then_inc(loaded, 16)
            sp.dma_start(causal[:, :], dram["causal"]).then_inc(loaded, 16)
            sp.dma_start(at_last[:, :], dram["at_last"]).then_inc(loaded, 16)

        @block.tensor
        def _(pe):
            pe.wait_ge(loaded, N_LOAD)
            pe.wait_ge(zeroed, 2)
            with pe.Fori(0, NG) as g:
                pe.wait_ge(heads_ready, g + 1)
                pe.wait_ge(w_added, GT * g)
                for f in range(GT // 2):
                    for j in (2 * f, 2 * f + 1):
                        for k in range(KC):
                            last = nc.tensor.matmul(proj_bank[f][:, (j % 2) * D:(j % 2 + 1) * D], heads[:, k, j * P:(j + 1) * P],
                                                    wo_x[:, k, :], start=(k == 0), stop=(k == KC - 1))
                    last.then_inc(h_filled, 1)
                pe.wait_ge(normed, g + 1)
                for k in range(KC):
                    for j in range(GT):
                        last = nc.tensor.transpose(proj_bank[k][:, j * P:(j + 1) * P], xn[:, j, k * P:(k + 1) * P], ident[:, :])
                    last.then_inc(xT_filled, 1)
                pe.wait_ge(xT_kept, KC * (g + 1))
                for i in range(NP):
                    pe.wait_ge(p_kept[i % 2], g * NPR[i % 2] + i // 2)
                    to = proj_bank[i % 2]
                    if i < QC:
                        for k in range(KC):
                            last = nc.tensor.matmul(to[:, :], wq[:, k, i * P:(i + 1) * P], xnT[:, k, :],
                                                    start=(k == 0), stop=(k == KC - 1))
                    elif i < QC + KV:
                        n = i - QC
                        for k in range(KC):
                            last = nc.tensor.matmul(to[:, :], wk[:, k, n * P:(n + 1) * P], xnT[:, k, :],
                                                    start=(k == 0), stop=(k == KC - 1))
                    elif i < GATE_FILL:
                        pe.wait_ge(twice_ready, g + 1)
                        for half in range(2):
                            b = 2 * (i - QC - KV) + half
                            for k in range(KC):
                                last = nc.tensor.matmul(to[:, half * D:(half + 1) * D],
                                                        xn_twice[:, k * GB + b, :, :],
                                                        wv[:, k, :], start=(k == 0), stop=(k == KC - 1))
                    else:
                        for j in range(GT):
                            for k in range(KC):
                                last = nc.tensor.matmul(to[:, j * NH * 3:(j + 1) * NH * 3], xnT[:, k, j * P:(j + 1) * P],
                                                        wg[:, k, :], start=(k == 0), stop=(k == KC - 1))
                    last.then_inc(p_filled, 1)
                for r in range(2):
                    pe.wait_ge(p_kept[r], (g + 1) * NPR[r])
                for n in range(-AHEAD, UNITS + 2):
                    if n + AHEAD < UNITS:
                        m = n + AHEAD
                        j, kv = m // KV, m % KV
                        pe.wait_ge(s_read, since(g, UNITS, m, 2))
                        for half in range(2):
                            b = 2 * j + half
                            for c in range(CH):
                                last = nc.tensor.matmul(score_bank[m % 2][half * LQ:(half + 1) * LQ, c * P:(c + 1) * P],
                                                        QT[:, kv * CH + c, b * LQ:(b + 1) * LQ], KB[:, kv, b, :, :],
                                                        start=True, stop=True)
                        last.then_inc(s_filled, 1)
                    if 0 <= n < UNITS:
                        pe.wait_ge(A_ready, g * UNITS + n + 1)
                        pe.wait_ge(t_kept, since(g, UNITS, n, 2))
                        for c in range(CH):
                            last = nc.tensor.transpose(turn_bank[n % 2][:, c * P:(c + 1) * P],
                                                       A[n % RING][:, 2 * c:2 * c + 2, :], ident[:, :])
                        last.then_inc(t_filled, 1)
                    if 1 <= n <= UNITS:
                        m = n - 1
                        j, kv = m // KV, m % KV
                        pe.wait_ge(t_kept, g * UNITS + m + 1)
                        pe.wait_ge(o_kept, since(g, UNITS, m, 2))
                        for half in range(2):
                            last = nc.tensor.matmul(out_bank[m % 2][:, half * CH * LQ:(half + 1) * CH * LQ],
                                                    VB[:, 2 * j + half, kv, :, :], AT[m % 2][:, :, half, :],
                                                    start=True, stop=True)
                        last.then_inc(o_filled, 1)
                    if n >= KV + 1 and (n - 1) % KV == 0:
                        j = (n - 1) // KV - 1
                        pe.wait_ge(o_kept, g * UNITS + KV * (j + 1))
                        pe.wait_ge(w_added, since(g, GT, j, 2))
                        for c in range(QC):
                            last = nc.tensor.matmul(proj_bank[j % 2][:, 0:D], OT[j % 2][:, c, :, :], wo[:, c, :],
                                                    start=(c == 0), stop=(c == QC - 1))
                        last.then_inc(w_filled, 1)

        def keep_projection(eng, g, i, copy):
            eng.wait_ge(p_filled, g * NP + i + 1)
            src = proj_bank[i % 2]
            if i < QC:
                last = copy(QT[:, i, :], src[:, :], float(DH) ** -0.5)
            elif i < QC + KV:
                for half in range(2):
                    rows = slice(half * DH, (half + 1) * DH)
                    last = copy(KB[rows, i - QC, :, half, :], src[rows, :].rearrange("p (b s) -> p b s", b=GB), 1.0)
            elif i < GATE_FILL:
                b = 2 * (i - QC - KV)
                for half in range(2):
                    rows = slice(half * LQ, (half + 1) * LQ)
                    for one in range(2):
                        last = copy(VB[rows, b + one, :, half, :],
                                    src[rows, one * D:(one + 1) * D].rearrange("p (v d) -> p v d", v=KV), 1.0)
            last.then_inc(p_kept[i % 2], 1)

        @block.vector
        def _(dve):
            dve.wait_ge(loaded, N_LOAD)
            dve.wait_ge(zeroed, 2)
            with dve.Fori(0, NG) as g:
                for f in range(GT // 2):
                    dve.wait_ge(h_filled, GT // 2 * g + f + 1)
                    dve.wait_ge(bo_added, g + 1)
                    tiles = x_all[:, bass.ds(g * GT + 2 * f, 2), :]
                    nc.vector.tensor_tensor(tiles, proj_bank[f][:, :].rearrange("p (t n) -> p t n", t=2), tiles,
                                            ALU.add).then_inc(h_added, 1)
                dve.wait_ge(h_added, GT // 2 * (g + 1))
                layer_norm(dve, nc, lambda j: x_all[:, bass.ds(g * GT + j, 1), :].rearrange("p a d -> p (a d)"),
                           g, stats, mv, std, xn, chain, std_ready, passed).then_inc(normed, 1)
                for i in range(1, NP, 2):
                    keep_projection(dve, g, i, lambda o, s, f: nc.vector.tensor_scalar(o, s, f, None, ALU.mult))
                dve.wait_ge(p_kept[0], (g + 1) * NPR[0])
                nc.vector.tensor_scalar(gate[:, :, :], gate[:, :, :], 1.0, None, ALU.add).then_inc(gate_step, 1)
                dve.wait_ge(gate_step, 2 * g + 1)
                nc.vector.reciprocal(gate[:, :, :], gate[:, :, :]).then_inc(gate_step, 1)
                dve.wait_ge(gate_step, 2 * g + 2)
                by_kind = gate[:, :, :].rearrange("p t (h k) -> p t h k", k=3)
                nc.vector.tensor_tensor(gate_near[:, :, :], by_kind[:, :, :, 1], by_kind[:, :, :, 2], ALU.add)\
                    .then_inc(gate_ready, 1)
                nc.vector.tensor_scalar(gate_mean[:, :, :], by_kind[:, :, :, 0], at_last[:, 0:1], None, ALU.mult)\
                    .then_inc(gate_ready, 1)
                dve.wait_ge(gate_ready, 2 * g + 2)
                for n in range(-AHEAD, UNITS + 2):
                    if n + AHEAD < UNITS:
                        m = n + AHEAD
                        r = m % RING
                        dve.wait_ge(s_filled, g * UNITS + m + 1)
                        dve.wait_ge(t_filled, since(g, UNITS, m, RING))
                        nc.vector.tensor_tensor(A[r][:, :, :], score_bank[m % 2][:, :].rearrange("p (h s) -> p h s", h=GH),
                                                causal[:, :].rearrange("p (h s) -> p h s", h=GH), ALU.add).then_inc(s_read, 1)
                        dve.wait_ge(s_read, g * UNITS + m + 1)
                        nc.vector.tensor_reduce(top[r][:, :], A[r][:, :, :], AX.X, ALU.max).then_inc(top_ready, 1)
                    if 0 <= n + AHEAD - 1 < UNITS:
                        m = n + AHEAD - 1
                        r, j, kv = m % RING, m // KV, m % KV
                        dve.wait_ge(exp_done, g * UNITS + m + 1)
                        nc.vector.tensor_reduce(total[r][:, :], A[r][:, :, :], AX.X, ALU.add).then_inc(sum_step, 1)
                        dve.wait_ge(sum_step, 2 * (g * UNITS + m) + 1)
                        nc.vector.reciprocal(total[r][:, :], total[r][:, :]).then_inc(sum_step, 1)
                        dve.wait_ge(sum_step, 2 * (g * UNITS + m) + 2)
                        nc.vector.tensor_tensor(total[r][:, :], total[r][:, :], gate_near[:, j, kv * GH:(kv + 1) * GH],
                                                ALU.mult).then_inc(scale_ready, 1)
                    if n >= KV + 1 and (n - 1) % KV == 0:
                        j = (n - 1) // KV - 1
                        dve.wait_ge(w_filled, GT * g + j + 1)
                        tile = x_all[:, bass.ds(g * GT + j, 1), :]
                        nc.vector.tensor_tensor(tile, proj_bank[j % 2][:, 0:D].rearrange("p (a n) -> p a n", a=1), tile,
                                                ALU.add).then_inc(w_added, 1)

        @block.scalar
        def _(act):
            act.wait_ge(zeroed, 2)
            with act.Fori(0, NG) as g:
                layer_norm_root(act, nc, g, std, chain, std_ready)
                for k in range(KC):
                    act.wait_ge(xT_filled, KC * g + k + 1)
                    nc.scalar.copy(xnT[:, k, :], proj_bank[k][:, :]).then_inc(xT_kept, 1)
                for i in range(0, NP - 1, 2):
                    keep_projection(act, g, i, lambda o, s, f: nc.scalar.activation(o, s, ACT.Copy, scale=f))
                act.wait_ge(p_filled, g * NP + NP)
                act.wait_ge(A_ready, g * UNITS)
                nc.scalar.activation(gate[:, :, :], proj_bank[GATE_FILL % 2][:, 0:GT * NH * 3].rearrange("p (t n) -> p t n", t=GT),
                                     ACT.Exp, scale=-1.0).then_inc(p_kept[0], 1)
                for n in range(-AHEAD, UNITS + 2):
                    if 0 <= n < UNITS:
                        act.wait_ge(t_filled, g * UNITS + n + 1)
                        act.wait_ge(o_filled, since(g, UNITS, n, 2))
                        nc.scalar.copy(AT[n % 2][:, :, :, :], turn_bank[n % 2][:, :].rearrange("p (c b t) -> p c b t", c=CH, b=2))\
                            .then_inc(t_kept, 1)
                    if 1 <= n <= UNITS:
                        m = n - 1
                        j, kv = m // KV, m % KV
                        act.wait_ge(o_filled, g * UNITS + m + 1)
                        act.wait_ge(w_filled, since(g, GT, j, 2))
                        nc.scalar.copy(OT[j % 2][:, kv * CH:(kv + 1) * CH, :, :].rearrange("p c b t -> p b c t"),
                                       out_bank[m % 2][:, :].rearrange("p (b c t) -> p b c t", b=2, c=CH)).then_inc(o_kept, 1)
                    if n + AHEAD < UNITS:
                        m = n + AHEAD
                        act.wait_ge(moved, g * UNITS + m + 1)
                        nc.scalar.activation(A[m % RING][:, :, :], A[m % RING][:, :, :], ACT.Exp).then_inc(exp_done, 1)

        @block.gpsimd
        def _(pool):
            nc.gpsimd.memset(KB[:, :, :, :, :], 0.0).then_inc(zeroed, 1)
            nc.gpsimd.memset(VB[:, :, :, :, :], 0.0).then_inc(zeroed, 1)
            pool.wait_ge(loaded, N_LOAD)
            with pool.Fori(0, NG) as g:
                pool.wait_ge(h_filled, GT // 2 * g)
                nc.gpsimd.tensor_copy(heads[:, :, :], CT[:, :, bass.ds(g * GTOK, GTOK)]).then_inc(heads_ready, 1)
                tiles = x_all[:, bass.ds(g * GT, GT), :]
                nc.gpsimd.tensor_tensor(tiles, tiles, bo_x[:, :].rearrange("p (a n) -> p a n", a=1).to_broadcast([P, GT, D]),
                                        ALU.add).then_inc(bo_added, 1)
                pool.wait_ge(xT_kept, KC * (g + 1))
                stand(pool, passed_pool)
                for half in range(2):
                    last = nc.gpsimd.tensor_copy(xn_twice[:, :, half, :], xnT[:, :, :].rearrange("p k (b s) -> p (k b) s", s=LQ))
                last.then_inc(twice_ready, 1)
                pool.wait_ge(gate_ready, 2 * g + 2)
                for n in range(-AHEAD, UNITS):
                    if n + AHEAD < UNITS:
                        m = n + AHEAD
                        r = m % RING
                        pool.wait_ge(top_ready, g * UNITS + m + 1)
                        nc.gpsimd.tensor_tensor(A[r][:, :, :], A[r][:, :, :],
                                                top[r][:, :].rearrange("p (h a) -> p h a", a=1).to_broadcast([P, GH, LQ]),
                                                ALU.subtract).then_inc(moved, 1)
                    if 0 <= n + AHEAD - 1 < UNITS:
                        m = n + AHEAD - 1
                        r, j, kv = m % RING, m // KV, m % KV
                        pool.wait_ge(scale_ready, g * UNITS + m + 1)
                        nc.gpsimd.tensor_tensor(A[r][:, :, :], A[r][:, :, :],
                                                total[r][:, :].rearrange("p (h a) -> p h a", a=1).to_broadcast([P, GH, LQ]),
                                                ALU.mult).then_inc(scaled, 1)
                        pool.wait_ge(scaled, g * UNITS + m + 1)
                        nc.gpsimd.tensor_tensor(A[r][:, :, :], A[r][:, :, :],
                                                gate_mean[:, j, kv * GH:(kv + 1) * GH].rearrange("p (h a) -> p h a", a=1)
                                                .to_broadcast([P, GH, LQ]), ALU.add).then_inc(A_ready, 1)


def experts(nc, dram, keep, out):
    with ExitStack() as ctx:
        sb = lambda name, shape: ctx.enter_context(nc.sbuf_tensor(name, shape, F32))
        bank = lambda name: ctx.enter_context(nc.psum_tensor(name, [P, 512], F32))
        sem = lambda name: ctx.enter_context(nc.semaphore(name))
        w1 = [sb(f"w1_{r}", [P, KC, FF]) for r in range(2)]
        w2 = [sb(f"w2_{r}", [P, FC, D]) for r in range(2)]
        b1 = [sb(f"b1_{r}", [P, FC]) for r in range(2)]
        b2 = [sb(f"b2_{r}", [P, D]) for r in range(2)]
        wr, br = sb("wr", [P, KC, NE]), sb("br", [P, NE])
        which = sb("which", [P, NE])
        stats, mv, std = sb("f_stats", [P, GT, 6]), sb("f_mv", [P, GT, 2]), sb("f_std", [P, GT])
        xn, xnT = sb("f_xn", [P, GT, D]), sb("f_xnT", [P, KC, GTOK])
        allT = sb("allT", [P, KC, TOK])
        logit, best = sb("logit", [P, GT, NE]), sb("best", [P, GT, NE])
        place = ctx.enter_context(nc.sbuf_tensor("place", [P, GT, NE], mybir.dt.uint32))
        placef = sb("placef", [P, GT, NE])
        first, second = sb("first", [P, GT, NE]), sb("second", [P, GT, NE])
        total = sb("f_total", [P, GT])
        share = sb("share", [P, NE, NT])
        mine = [sb(f"mine{r}", [P, NT]) for r in range(2)]
        hT = [sb(f"hT{r}", [P, FC, GTOK]) for r in range(2)]
        yb = [sb(f"yb{r}", [P, D]) for r in range(2)]
        up_bank = [bank(f"up_bank{r}") for r in range(4)]
        down_bank = [bank(f"down_bank{r}") for r in range(4)]
        loaded = sem("f_loaded")
        w_loaded = [sem(f"f_w_loaded{r}") for r in range(2)]
        chain, std_ready, normed = sem("f_chain"), sem("f_std_ready"), sem("f_normed")
        xT_filled, xT_kept, all_kept = sem("f_xT_filled"), sem("f_xT_kept"), sem("all_kept")
        r_filled, r_step, r_exp, share_ready = sem("r_filled"), sem("r_step"), sem("r_exp"), sem("share_ready")
        mine_ready = sem("mine_ready")
        up_filled, up_kept = sem("up_filled"), sem("up_kept")
        down_filled, down_read, added = [sem(f"down_filled{r}") for r in range(2)], sem("down_read"), sem("added")
        stored = sem("stored")
        passed = sem("f_passed")
        x_all, ident = keep["x_all"], keep["ident"]
        R_STEPS = 2 * GT + 9
        block = ctx.enter_context(nc.Block())
        EU = NG
        PER = 2 * EU

        @block.sync
        def _(sp):
            sp.dma_start(wr[:, :, :], dram["wr"].rearrange("(k p) n -> p k n", p=P)).then_inc(loaded, 16)
            sp.dma_start(br[:, :], dram["br"]).then_inc(loaded, 16)
            sp.dma_start(which[:, :], dram["which"]).then_inc(loaded, 16)

            def load_expert(e, r):
                sp.dma_start(w1[r][:, :, :], dram["w1"][bass.ds(e, 1)].rearrange("a (k p) f -> p (a k) f", p=P)).then_inc(w_loaded[r], 16)
                sp.dma_start(b1[r][:, :], dram["b1"][bass.ds(e, 1)].rearrange("a p f -> p (a f)")).then_inc(w_loaded[r], 16)
                sp.dma_start(w2[r][:, :, :], dram["w2"][bass.ds(e, 1)].rearrange("a (k p) f -> p (a k) f", p=P)).then_inc(w_loaded[r], 16)
                sp.dma_start(b2[r][:, :], dram["b2"][bass.ds(e, 1)].rearrange("a p f -> p (a f)")).then_inc(w_loaded[r], 16)

            load_expert(0, 0)
            load_expert(1, 1)
            with sp.Fori(1, NE // 2) as i:
                for r in range(2):
                    sp.wait_ge(added, GT * (PER * i - PER + (r + 1) * EU))
                    load_expert(2 * i + r, r)
            sp.wait_ge(added, GT * EU * NE)
            sp.dma_start(out.rearrange("(t p) d -> p t d", p=P), x_all[:, :, :]).then_inc(stored, 16)
            sp.wait_ge(stored, 16)

        @block.tensor
        def _(pe):
            pe.wait_ge(loaded, 48)
            with pe.Fori(0, NG) as g:
                pe.wait_ge(normed, g + 1)
                pe.wait_ge(xT_kept, KC * g)
                for k in range(KC):
                    for j in range(GT):
                        last = nc.tensor.transpose(up_bank[k][:, j * P:(j + 1) * P], xn[:, j, k * P:(k + 1) * P], ident[:, :])
                    last.then_inc(xT_filled, 1)
                pe.wait_ge(xT_kept, KC * (g + 1))
                pe.wait_ge(r_step, R_STEPS * g + 1)
                for j in range(GT):
                    for k in range(KC):
                        last = nc.tensor.matmul(down_bank[0][:, j * NE:(j + 1) * NE], xnT[:, k, j * P:(j + 1) * P],
                                                wr[:, k, :], start=(k == 0), stop=(k == KC - 1))
                last.then_inc(r_filled, 1)

            def up(i, u, again=True):
                r, g = u // EU % 2, u % EU
                if g == 0:
                    pe.wait_ge(w_loaded[r], 64 * (i + 1 + u // PER))
                for f in range(FC):
                    m = (i * PER + u) * FC + f
                    to = up_bank[f % 4]
                    if again or f >= 4:
                        pe.wait_ge(up_kept, m - 3)
                    for k in range(KC):
                        last = nc.tensor.matmul(to[:, :], w1[r][:, k, f * P:(f + 1) * P],
                                                allT[:, k, g * GTOK:(g + 1) * GTOK], start=(k == 0), stop=(k == KC - 1))
                    last.then_inc(up_filled, 1)

            def down(i, u):
                r = u // EU % 2
                pe.wait_ge(up_kept, (i * PER + u + 1) * FC)
                pe.wait_ge(down_read, (i * PER + u) * GT)
                for j in range(GT):
                    for f in range(FC):
                        last = nc.tensor.matmul(down_bank[j][:, 0:D], hT[u % 2][:, f, j * P:(j + 1) * P], w2[r][:, f, :],
                                                start=(f == 0), stop=(f == FC - 1))
                    last.then_inc(down_filled[u % 2], 1)

            pe.wait_ge(all_kept, NG)
            pe.wait_ge(r_step, R_STEPS * NG + 1)
            up(0, 0, again=False)
            with pe.Fori(0, NE // 2 - 1) as i:
                for u in range(PER):
                    up(i, u + 1)
                    down(i, u)
            for u in range(PER):
                if u + 1 < PER:
                    up(NE // 2 - 1, u + 1)
                down(NE // 2 - 1, u)

        @block.scalar
        def _(act):
            with act.Fori(0, NG) as g:
                layer_norm_root(act, nc, g, std, chain, std_ready)
                act.wait_ge(all_kept, g)
                act.wait_ge(r_filled, g)
                for k in range(KC):
                    act.wait_ge(xT_filled, KC * g + k + 1)
                    nc.scalar.copy(xnT[:, k, :], up_bank[k][:, :]).then_inc(xT_kept, 1)
                act.wait_ge(r_step, R_STEPS * (g + 1) - 2)
                nc.scalar.activation(logit[:, :, :], logit[:, :, :], ACT.Exp).then_inc(r_exp, 1)

            def relu(i, u):
                r = u // EU % 2
                if u % EU == 0:
                    act.wait_ge(w_loaded[r], 64 * (i + 1 + u // PER))
                act.wait_ge(down_filled[u % 2], (i * (PER // 2) + u // 2) * GT)
                for f in range(FC):
                    act.wait_ge(up_filled, (i * PER + u) * FC + f + 1)
                    nc.scalar.activation(hT[u % 2][:, f, :], up_bank[f % 4][:, :], ACT.Relu, bias=b1[r][:, f:f + 1]).then_inc(up_kept, 1)

            with act.Fori(0, NE // 2) as i:
                for u in range(PER):
                    relu(i, u)

        @block.gpsimd
        def _(pool):
            with pool.Fori(0, NG) as g:
                pool.wait_ge(xT_kept, KC * (g + 1))
                nc.gpsimd.tensor_copy(allT[:, :, bass.ds(g * GTOK, GTOK)], xnT[:, :, :]).then_inc(all_kept, 1)
            pool.wait_ge(share_ready, NG)
            with pool.Fori(0, NE // 2) as i:
                for r in range(2):
                    pool.wait_ge(added, GT * (PER * i + r * EU) if r else GT * PER * i)
                    nc.gpsimd.tensor_copy(mine[r][:, :], share[:, bass.ds(2 * i + r, 1), :].rearrange("p a t -> p (a t)")).then_inc(mine_ready, 1)

        @block.vector
        def _(dve):
            dve.wait_ge(loaded, 48)
            nc.vector.memset(total[:, :], 0.0).then_inc(r_step, 1)
            with dve.Fori(0, NG) as g:
                dve.wait_ge(xT_filled, KC * g)
                layer_norm(dve, nc, lambda j: x_all[:, bass.ds(g * GT + j, 1), :].rearrange("p a d -> p (a d)"),
                           g, stats, mv, std, xn, chain, std_ready, passed).then_inc(normed, 1)
                at = R_STEPS * g + 1
                dve.wait_ge(r_filled, g + 1)
                nc.vector.tensor_tensor(logit[:, :, :], down_bank[0][:, 0:GT * NE].rearrange("p (t e) -> p t e", t=GT),
                                        br[:, :].rearrange("p (a e) -> p a e", a=1).to_broadcast([P, GT, NE]), ALU.add).then_inc(r_step, 1)
                dve.wait_ge(r_step, at + 1)
                stand(dve, passed)
                for j in range(GT):
                    nc.vector.max(best[:, j, :], logit[:, j, :]).then_inc(r_step, 1)
                for j in range(GT):
                    dve.wait_ge(r_step, at + 2 + j)
                    stand(dve, passed)
                    nc.vector.max_index(place[:, j, :], best[:, j, :], logit[:, j, :]).then_inc(r_step, 1)
                at = at + 1 + 2 * GT
                dve.wait_ge(r_step, at)
                nc.vector.tensor_copy(placef[:, :, :], place[:, :, :]).then_inc(r_step, 1)
                dve.wait_ge(r_step, at + 1)
                ids = which[:, :].rearrange("p (a e) -> p a e", a=1).to_broadcast([P, GT, NE])
                nc.vector.tensor_tensor(first[:, :, :], ids, placef[:, :, 0:1].to_broadcast([P, GT, NE]), ALU.is_equal).then_inc(r_step, 1)
                nc.vector.tensor_tensor(second[:, :, :], ids, placef[:, :, 1:2].to_broadcast([P, GT, NE]), ALU.is_equal).then_inc(r_step, 1)
                dve.wait_ge(r_step, at + 3)
                nc.vector.tensor_tensor(first[:, :, :], first[:, :, :], second[:, :, :], ALU.add).then_inc(r_step, 1)
                nc.vector.tensor_tensor(logit[:, :, :], logit[:, :, :], best[:, :, 0:1].to_broadcast([P, GT, NE]), ALU.subtract).then_inc(r_step, 1)
                dve.wait_ge(r_step, at + 5)
                dve.wait_ge(r_exp, g + 1)
                nc.vector.tensor_tensor(first[:, :, :], first[:, :, :], logit[:, :, :], ALU.mult).then_inc(r_step, 1)
                dve.wait_ge(r_step, at + 6)
                nc.vector.tensor_reduce(total[:, :], first[:, :, :], AX.X, ALU.add).then_inc(r_step, 1)
                dve.wait_ge(r_step, at + 7)
                nc.vector.reciprocal(total[:, :], total[:, :]).then_inc(r_step, 1)
                dve.wait_ge(r_step, at + 8)
                nc.vector.tensor_tensor(share[:, :, bass.ds(g * GT, GT)], first[:, :, :].rearrange("p t e -> p e t"),
                                        total[:, :].rearrange("p (a t) -> p a t", a=1).to_broadcast([P, NE, GT]),
                                        ALU.mult).then_inc(share_ready, 1)
            with dve.Fori(0, NE // 2) as i:
                for u in range(PER):
                    r, g = u // EU % 2, u % EU
                    if g == 0:
                        dve.wait_ge(w_loaded[r], 64 * (i + 1))
                        dve.wait_ge(mine_ready, 2 * i + r + 1)
                    for j in range(GT):
                        m = (i * PER + u) * GT + j
                        dve.wait_ge(down_filled[u % 2], (i * (PER // 2) + u // 2) * GT + j + 1)
                        nc.vector.tensor_tensor(yb[j % 2][:, :], down_bank[j][:, 0:D], b2[r][:, :], ALU.add).then_inc(down_read, 1)
                        dve.wait_ge(down_read, m + 1)
                        t = g * GT + j
                        nc.vector.scalar_tensor_tensor(x_all[:, t, :], yb[j % 2][:, :], mine[r][:, t:t + 1], x_all[:, t, :],
                                                       ALU.mult, ALU.add).then_inc(added, 1)


def build_program(nc, dram, out):
    with ExitStack() as ctx:
        sb = lambda where, name, shape: where.enter_context(nc.sbuf_tensor(name, shape, F32))
        keep = {"ident": sb(ctx, "ident", [P, P])}
        with ExitStack() as middle:
            keep["heads"] = sb(middle, "heads_all", [P, KC, TOK])
            with ExitStack() as inner:
                keep["headmask"] = sb(inner, "headmask", [P, HG * LQ])
                project_queries(nc, dram, keep)
                cross_attention(nc, dram, keep)
            keep["x_all"] = sb(middle, "x_all", [P, NT, D])
            gated_attention(nc, dram, keep)
            experts(nc, dram, keep, out)


def laid_out(inputs):
    c = np.ascontiguousarray
    a = {k: np.asarray(v) for k, v in inputs.items()}
    repeated = lambda v: np.broadcast_to(v.reshape(1, -1), (P, v.size))
    rows = np.arange(P) // HD
    query = np.arange(P) % LQ
    f = np.float32
    r = {
        "x": a["x"].reshape(TOK, D),
        "ctxT": np.pad(a["ctx_1024"].transpose(0, 2, 1), ((0, 0), (0, 0), (0, 1))).reshape(B, KC, P, SP),
        "bias": a["fside_1x16xSxS2_0"].reshape(NPAIR, P, S),
        "wq": a["L0_xattn_wq"].reshape(D, D),
        "wk": a["L0_xattn_wk"].reshape(D, D),
        "wv": a["L0_xattn_wv"].reshape(D, D),
        "bq": a["L0_xattn_bq"].reshape(KC, P).T,
        "bk": a["L0_xattn_bk"].reshape(KC, P).T,
        "bv": a["L0_xattn_bv"].reshape(NPAIR, 2, HD).transpose(0, 2, 1).reshape(P, 2),
        "wo_x": a["L0_xattn_wo"].reshape(NPAIR, 2, HD, D).transpose(1, 0, 2, 3).reshape(D, D),
        "bo_x": repeated(a["L0_xattn_bo"]),
        "a_wq": a["L0_attn_Wq"],
        "a_wk": np.repeat(a["L0_attn_Wk"].reshape(D, KV, 1, DH), 2, axis=2).reshape(D, KV * 2 * DH),
        "a_wv": a["L0_attn_Wv"],
        "a_wg": a["L0_attn_Wg"],
        "a_wo": a["L0_attn_Wo"],
        "wr": a["L0_ffn_W_router"],
        "br": repeated(a["L0_ffn_b_router"]),
        "w1": a["L0_ffn_W1"],
        "w2": a["L0_ffn_W2"],
        "b1": a["L0_ffn_b1"].reshape(NE, FC, P).transpose(0, 2, 1),
        "b2": np.broadcast_to(a["L0_ffn_b2"][:, None, :], (NE, P, D)),
        "fold": ((np.arange(P)[:, None, None] // HD % QH == np.arange(QH)[None, :, None])
                 & (np.arange(P)[:, None, None] % HD == np.arange(HD)[None, None, :])).astype(f),
        "ident": np.eye(P, dtype=f),
        "headmask": np.repeat((rows[:, None] == np.arange(HG)[None, :]).astype(f), LQ, axis=1),
        "causal": np.tile(np.where(query[:, None] >= np.arange(LQ)[None, :], f(0), f(MASKED)), (1, GH)),
        "at_last": np.where(query == LQ - 1, f(1 / LQ), f(0))[:, None],
        "which": np.tile(np.arange(NE, dtype=f), (P, 1)),
    }
    return {k: c(v) for k, v in r.items()}


def kernel(**inputs):
    import concourse.bacc as bacc
    from concourse.bass_utils import run_bass_kernel_spmd

    arrays = laid_out(inputs)
    nc = bacc.Bacc("TRN2", target_bir_lowering=False, num_devices=1)
    dram = {name: nc.dram_tensor("in_" + name, v.shape, mybir.dt.from_np(v.dtype), kind="ExternalInput").ap()
            for name, v in arrays.items()}
    out = nc.dram_tensor("out", (TOK, D), F32, kind="ExternalOutput").ap()
    build_program(nc, dram, out)
    result = run_bass_kernel_spmd(nc, [{"in_" + name: v for name, v in arrays.items()}], core_ids=[0])
    return result.results[0]["out"].reshape(B, LQ, D)
```

```python
from contextlib import ExitStack

import numpy as np

import concourse.bass as bass
from concourse import mybir

F32 = mybir.dt.float32
F32R = mybir.dt.float32r
ALU = mybir.AluOpType
ACT = mybir.ActivationFunctionType
AX = mybir.AxisListType

P = 128
B, LQ, D = 32, 64, 256
S = 1601
TOK = B * LQ
NT = TOK // P
KC = D // P
H, HD = 16, 16
HG = P // HD
NPAIR = H // 2
QH, NQ = 4, H // 4
SP = S + 1
COLS = [(0, 402), (402, 400), (802, 400), (1202, 400)]
HALVES = [(0, 802), (802, S)]
NCOL = len(COLS)
ST = -(-S // P)
LAST = S - (ST - 1) * P
TB = -(-ST // 2)
PIECES = 2 * NCOL
NEAR = {0: [3], 1: [4], 2: [5], 3: [6], 4: [7]}
FAR = {5: [0, 1], 6: [2]}
EXP_AT = {1: (0, 0), 3: (0, 1), 5: (1, 0), 6: (1, 1)}
K_SLOT = 2
C_AT = {(0, 0): 0, (0, 2): 1, (0, 4): 2, (1, 0): 3}
SECOND_AT = HALVES[1][0] // P // 2
SUMS_AT, FOLD_AT, CT_AT = 1, 4, 5
GT = 4
GTOK = GT * P
NG = TOK // GTOK
EPS = 1e-5
LOWEST = -3.0e38

NH, KV, DH = 32, 4, 64
GH = NH // KV
QC = NH * DH // P
CH = GH // 2
GB = GTOK // LQ
UNITS = GT * KV
AHEAD, RING = 3, 4
NP = QC + KV + GB // 2 + 1
NPR = [-(-NP // 2), NP // 2]
MASKED = -1.0e30

NE, FF = 8, 1024
FC = FF // P
UT = 2
UTOK = UT * P
EU = NT // UT
UPB = FC // 2
Y_STEPS, Y_READ = 2, 1


def rows_of(t):
    return P if t < ST - 1 else LAST


def stand(eng, passed):
    eng.sem_inc(passed, 1)


def layer_norm(dve, nc, x_of, step, stats, mv, std, xn, chain, std_ready, passed):
    at = step * LN_STEPS
    stand(dve, passed)
    for j in range(GT):
        nc.vector.bn_stats(stats[:, j, :], x_of(j)).then_inc(chain, 1)
    for j in range(GT):
        dve.wait_ge(chain, at + j + 1)
        stand(dve, passed)
        nc.vector.bn_aggr(mv[:, j, :], stats[:, j, :]).then_inc(chain, 1)
    dve.wait_ge(chain, at + 2 * GT)
    nc.vector.tensor_scalar(std[:, :], mv[:, :, 1], EPS, None, ALU.add).then_inc(chain, 1)
    dve.wait_ge(std_ready, step + 1)
    nc.vector.reciprocal(std[:, :], std[:, :]).then_inc(chain, 1)
    dve.wait_ge(chain, at + LN_STEPS)
    for j in range(GT):
        last = nc.vector.tensor_scalar(xn[:, j, :], x_of(j), mv[:, j, 0:1], std[:, j:j + 1],
                                       ALU.subtract, ALU.mult)
    return last


LN_STEPS = 2 * GT + 2


def layer_norm_root(act, nc, step, std, chain, std_ready):
    act.wait_ge(chain, step * LN_STEPS + 2 * GT + 1)
    nc.scalar.activation(std[:, :], std[:, :], ACT.Sqrt).then_inc(std_ready, 1)


def project_queries(nc, dram, keep):
    with ExitStack() as ctx:
        sb = lambda name, shape: ctx.enter_context(nc.sbuf_tensor(name, shape, F32))
        sem = lambda name: ctx.enter_context(nc.semaphore(name))
        wq = sb("wq", [P, KC, D])
        bq = sb("bq", [P, KC])
        stats, mv, std = sb("q_stats", [P, GT, 6]), sb("q_mv", [P, GT, 2]), sb("q_std", [P, GT])
        xn = sb("q_xn", [P, GT, D])
        xnT = sb("q_xnT", [P, KC, GTOK])
        turned = [ctx.enter_context(nc.psum_tensor(f"q_turned{k}", [P, GTOK], F32)) for k in range(KC)]
        proj = [ctx.enter_context(nc.psum_tensor(f"q_proj{c}", [P, GTOK], F32)) for c in range(KC)]
        loaded, chain, std_ready, normed = sem("q_loaded"), sem("q_chain"), sem("q_std_ready"), sem("q_normed")
        xT_filled, xT_kept = sem("q_xT_filled"), sem("q_xT_kept")
        q_filled, q_kept, bq_ready = sem("q_filled"), sem("q_kept"), sem("bq_ready")
        passed = sem("q_passed")
        x_all = sb("q_x", [P, NT, D])
        QT, ident = keep["heads"], keep["ident"]
        ONE = 1
        block = ctx.enter_context(nc.Block())

        @block.sync
        def _(sp):
            sp.dma_start(x_all[:, :, :], dram["x"].rearrange("(t p) d -> p t d", p=P)).then_inc(loaded, 16)
            sp.dma_start(ident[:, :], dram["ident"]).then_inc(loaded, 16)
            sp.dma_start(wq[:, :, :], dram["wq"].rearrange("(k p) n -> p k n", p=P)).then_inc(loaded, 16)
            sp.dma_start(bq[:, :], dram["bq"]).then_inc(loaded, 16)
            sp.dma_start(keep["headmask"][:, :], dram["headmask"]).then_inc(loaded, 16)

        @block.vector
        def _(dve):
            dve.wait_ge(loaded, 80)
            nc.vector.tensor_scalar(bq[:, :], bq[:, :], float(HD) ** -0.5, None, ALU.mult).then_inc(bq_ready, 1)
            with dve.Fori(0, NG) as g:
                dve.wait_ge(xT_filled, KC * g + ONE)
                layer_norm(dve, nc, lambda j: x_all[:, bass.ds(g * GT + j, 1), :].rearrange("p a d -> p (a d)"),
                           g, stats, mv, std, xn, chain, std_ready, passed).then_inc(normed, 1)

        @block.scalar
        def _(act):
            act.sem_inc(xT_kept, ONE)
            act.sem_inc(q_kept, ONE)
            act.wait_ge(bq_ready, 1)
            with act.Fori(0, NG) as g:
                layer_norm_root(act, nc, g, std, chain, std_ready)
                for k in range(KC):
                    act.wait_ge(xT_filled, KC * g + k + 1 + ONE)
                    act.wait_ge(q_filled, KC * g + ONE)
                    nc.scalar.copy(xnT[:, k, :], turned[k][:, :]).then_inc(xT_kept, 1)
                for c in range(KC):
                    act.wait_ge(q_filled, KC * g + c + 1 + ONE)
                    nc.scalar.activation(QT[:, c, bass.ds(g * GTOK, GTOK)], proj[c][:, :], ACT.Identity,
                                         bias=bq[:, c:c + 1], scale=float(HD) ** -0.5).then_inc(q_kept, 1)

        @block.tensor
        def _(pe):
            pe.sem_inc(xT_filled, ONE)
            pe.sem_inc(q_filled, ONE)
            pe.wait_ge(loaded, 80)
            with pe.Fori(0, NG) as g:
                pe.wait_ge(normed, g + 1)
                for k in range(KC):
                    pe.wait_ge(xT_kept, KC * g + ONE)
                    for j in range(GT):
                        last = nc.tensor.transpose(turned[k][:, j * P:(j + 1) * P], xn[:, j, k * P:(k + 1) * P], ident[:, :])
                    last.then_inc(xT_filled, 1)
                pe.wait_ge(xT_kept, KC * (g + 1) + ONE)
                for c in range(KC):
                    pe.wait_ge(q_kept, KC * g + ONE)
                    for k in range(KC):
                        last = nc.tensor.matmul(proj[c][:, :], wq[:, k, c * P:(c + 1) * P], xnT[:, k, :],
                                                start=(k == 0), stop=(k == KC - 1))
                    last.then_inc(q_filled, 1)


def cross_attention(nc, dram, keep):
    with ExitStack() as ctx:
        sb = lambda name, shape, dt=F32: ctx.enter_context(nc.sbuf_tensor(name, shape, dt))
        bank = lambda name: ctx.enter_context(nc.psum_tensor(name, [P, 512], F32))
        sem = lambda name: ctx.enter_context(nc.semaphore(name))
        pair = lambda name, shape: [sb(name + part, shape, F32R) for part in ("_high", "_low")]
        raw_w = sb("raw_w", [P, KC, D])
        wk, wv = pair("wk", [P, KC, D]), pair("wv", [P, KC, D])
        bk, bv = sb("bk", [P, KC]), sb("bv", [P, 2])
        fold = sb("fold", [P, QH, HD])
        bias = sb("bias", [P, NPAIR, S])
        raw_c = [sb(f"raw_c{r}", [P, SP // 2]) for r in range(2)]
        cT = pair("cT", [P, KC, SP])
        KT = pair("KT", [P, KC, SP])
        V = sb("V", [P, ST, NQ, 2, QH * HD], F32R)
        raw_q = sb("raw_q", [P, QH, LQ])
        QB = [pair(f"QB{r}", [P, QH, LQ]) for r in range(2)]
        probs = [sb(f"probs{r}", [P, 2, S]) for r in range(2)]
        PT = [pair(f"PT{r}", [P, 2, QH * LQ]) for r in range(2)]
        top = [sb(f"top{r}", [P, 2, NCOL]) for r in range(2)]
        neg_max = [sb(f"neg_max{r}", [P, 2]) for r in range(2)]
        total = [sb(f"total{r}", [P, 2, 2]) for r in range(2)]
        inverse = [sb(f"inverse{r}", [P, 2]) for r in range(2)]
        raw_out = [sb(f"raw_out{r}", [P, QH, LQ]) for r in range(2)]
        by_query = sb("by_query", [P, NPAIR, HD])
        score_bank = [bank(f"score_bank{r}") for r in range(2)]
        turn_bank = [bank(f"turn_bank{r}") for r in range(2)]
        proj_bank = [bank(f"proj_bank{r}") for r in range(2)]
        out_bank = [bank(f"out_bank{r}") for r in range(2)]

        wk_loaded, wv_loaded, loaded = sem("wk_loaded"), sem("wv_loaded"), sem("loaded")
        w_step = sem("w_step")
        c_loaded, c_ready = [sem(f"c_loaded{r}") for r in range(2)], sem("c_ready")
        c_high, q_high, q_raw = sem("c_high"), sem("q_high"), sem("q_raw")
        k_filled, k_high, k_kept = sem("k_filled"), sem("k_high"), sem("k_kept")
        v_filled, v_high, v_kept = sem("v_filled"), sem("v_high"), sem("v_kept")
        qb_ready = sem("qb_ready")
        s_filled, s_read = sem("s_filled"), sem("s_read")
        max_ready, exp_done = sem("max_ready"), sem("exp_done")
        sums_step, sums_taken = sem("sums_step"), sem("sums_taken")
        t_filled = [sem(f"t_filled{r}") for r in range(2)]
        t_high = [sem(f"t_high{r}") for r in range(2)]
        t_kept = [sem(f"t_kept{r}") for r in range(2)]
        t_used = [sem(f"t_used{r}") for r in range(2)]
        out_read, folded, scaled = sem("out_read"), sem("folded"), sem("scaled")
        ct_turned, ct_ready = sem("ct_turned"), sem("ct_ready")
        passed, passed_dve = sem("passed"), sem("passed_dve")
        heads, ident, headmask = keep["heads"], keep["ident"], keep["headmask"]
        ONE, TWO = 1, 2
        block = ctx.enter_context(nc.Block())

        def turn_of(b, a, f):
            r = (a * TB + f) % 2
            before = sum((x % 2) == r for x in range(a * TB + f))
            return r, b * (NQ * TB // 2) + before

        def k_bank(c, j):
            return 1 if c else j % 2

        def v_bank(f):
            return f % 2 if f > NCOL else 0

        def k_before(b, c, j):
            return b * KC * NCOL + c * NCOL + j

        def after(b, a):
            return (b, a + 1) if a + 1 < NQ else (b + 1, 0)

        def unit(b, a):
            return b * NQ + a

        def tiles_of(f):
            return range(2 * f, min(2 * f + 2, ST))

        @block.sync
        def _(sp):
            sp.dma_start(raw_w[:, :, :], dram["wk"].rearrange("(k p) n -> p k n", p=P)).then_inc(wk_loaded, 16)

            def load_context(b):
                for k in range(KC):
                    for half in range(2):
                        i = 2 * k + half
                        sp.wait_ge(c_ready, 4 * b + i - 1 + TWO)
                        sp.dma_start(raw_c[half][:, :], dram["ctxT"][bass.ds(b, 1), k, :, half * (SP // 2):(half + 1) * (SP // 2)]
                                     .rearrange("a p s -> p (a s)")).then_inc(c_loaded[half], 16)

            sp.sem_inc(c_ready, TWO)
            load_context(0)
            sp.wait_ge(w_step, 2)
            sp.dma_start(raw_w[:, :, :], dram["wv"].rearrange("(k p) n -> p k n", p=P)).then_inc(wv_loaded, 16)
            sp.dma_start(bk[:, :], dram["bk"]).then_inc(loaded, 16)
            sp.dma_start(bv[:, :], dram["bv"]).then_inc(loaded, 16)
            sp.dma_start(fold[:, :, :], dram["fold"]).then_inc(loaded, 16)
            sp.dma_start(bias[:, :, :], dram["bias"].rearrange("r p s -> p r s")).then_inc(loaded, 16)
            with sp.Fori(1, B) as b:
                load_context(b)

        @block.gpsimd
        def _(pool):
            def context_low(b):
                for i in range(2 * KC):
                    k, half = i // 2, i % 2
                    cols = slice(half * (SP // 2), (half + 1) * (SP // 2))
                    pool.wait_ge(c_high, 2 * KC * b + i + 1)
                    nc.gpsimd.tensor_tensor(cT[1][:, k, cols], raw_c[half][:, :], cT[0][:, k, cols].bitcast(F32),
                                            ALU.subtract).then_inc(c_ready, 1)

            def spread_q(b, a, again=True):
                r, u = a % 2, unit(b, a)
                mask = headmask[:, :].rearrange("p (h q) -> p h q", h=HG)[:, r * QH:(r + 1) * QH, :]
                q = heads[:, a // 2:a // 2 + 1, bass.ds(b * LQ, LQ)].to_broadcast([P, QH, LQ])
                if again:
                    pool.wait_ge(s_filled, PIECES * (u - 1))
                    pool.wait_ge(qb_ready, u)
                    stand(pool, passed)
                elif a:
                    pool.wait_ge(qb_ready, u)
                nc.gpsimd.tensor_tensor(QB[r][0][:, :, :], q, mask, ALU.mult).then_inc(q_high, 1)
                nc.gpsimd.tensor_tensor(raw_q[:, :, :], q, mask, ALU.mult).then_inc(q_raw, 1)
                pool.wait_ge(q_high, u + 1)
                pool.wait_ge(q_raw, u + 1)
                nc.gpsimd.tensor_tensor(QB[r][1][:, :, :], raw_q[:, :, :], QB[r][0][:, :, :].bitcast(F32),
                                        ALU.subtract).then_inc(qb_ready, 1)

            context_low(0)
            spread_q(0, 0, again=False)
            spread_q(0, 1, again=False)
            with pool.Fori(0, B - 1) as b:
                spread_q(b, 2)
                context_low(b + 1)
                spread_q(b, 3)
                spread_q(b + 1, 0)
                spread_q(b + 1, 1)
            spread_q(B - 1, 2)
            spread_q(B - 1, 3)

        @block.tensor
        def _(pe):
            def three(to, left, right, n_k=KC):
                todo = [(k, x, y) for k in range(n_k) for x, y in ((0, 0), (0, 1), (1, 0))]
                for i, (k, x, y) in enumerate(todo):
                    last = nc.tensor.matmul(to, left(k, x), right(k, y), start=(i == 0), stop=(i == len(todo) - 1))
                return last

            def project_k(b, c, j):
                if c == 0 and j == 0:
                    pe.wait_ge(c_ready, 2 * KC * b + 2 * KC + TWO)
                if c == 0 and j < 2:
                    pe.wait_ge(v_kept, TB * b + ONE)
                elif j > 0:
                    pe.wait_ge(k_kept, k_before(b, c, j - 1) + int(c > 0))
                at, n = COLS[j]
                three(proj_bank[k_bank(c, j)][:, 0:n], lambda k, x: wk[x][:, k, c * P:(c + 1) * P],
                      lambda k, y: cT[y][:, k, at:at + n]).then_inc(k_filled, 1)

            def project_v(b, f):
                if f == 0:
                    pe.wait_ge(k_kept, k_before(b, 1, 0))
                elif f == NCOL + 1:
                    pe.wait_ge(k_kept, k_before(b + 1, 0, 0))
                else:
                    pe.wait_ge(v_kept, TB * b + f - int(f > NCOL + 1) + ONE)
                for t in tiles_of(f):
                    n = rows_of(t)
                    last = three(proj_bank[v_bank(f)][0:n, (t % 2) * D:(t % 2 + 1) * D],
                                 lambda k, x: cT[x][:, k, t * P:t * P + n], lambda k, y: wv[y][:, k, :])
                last.then_inc(v_filled, 1)

            def piece(b, a, m):
                u = unit(b, a)
                i, (at, n) = m // NCOL, COLS[m % NCOL]
                if m == 0:
                    pe.wait_ge(qb_ready, u + 1)
                    pe.wait_ge(k_kept, k_before(b, a // 2 + 1, 0))
                pe.wait_ge(s_read, PIECES * u + m - 1 + TWO)
                three(score_bank[m % 2][:, 0:n], lambda k, x: QB[a % 2][x][:, 2 * i:2 * i + 2, :],
                      lambda k, y: KT[y][:, a // 2, at:at + n], 1).then_inc(s_filled, 1)

            def turn(b, a, f):
                u = unit(b, a)
                r, before = turn_of(b, a, f)
                if f == 0:
                    pe.wait_ge(exp_done, 4 * u + 3)
                if f == SECOND_AT:
                    pe.wait_ge(exp_done, 4 * u + 4)
                pe.wait_ge(t_kept[r], before + ONE)
                for t in tiles_of(f):
                    n = rows_of(t)
                    for i in range(2):
                        last = nc.tensor.transpose(turn_bank[r][0:n, (t % 2) * D + i * P:(t % 2) * D + (i + 1) * P],
                                                   probs[a % 2][:, i, t * P:t * P + n], ident[:, :])
                last.then_inc(t_filled[r], 1)

            def weigh(b, a, f):
                r, before = turn_of(b, a, f)
                if a == 0:
                    pe.wait_ge(v_kept, TB * b + f + 1 + ONE)
                if f == 0:
                    u = unit(b, a)
                    pe.wait_ge(scaled, u - 1 + TWO)
                    if a % 2:
                        pe.wait_ge(ct_ready, b + ONE)
                pe.wait_ge(t_kept[r], before + 1 + ONE)
                for t in tiles_of(f):
                    n = rows_of(t)
                    for part in range(2):
                        last = nc.tensor.matmul(out_bank[a % 2][:, 0:D], V[0:n, t, a, :, :], PT[r][part][0:n, t % 2, :],
                                                start=(t == 0 and part == 0), stop=(t == ST - 1 and part == 1))
                last.then_inc(t_used[r], 1)

            def fold_heads(b, a):
                u = unit(b, a)
                pe.wait_ge(out_read, u + 1)
                for h in range(QH):
                    last = nc.tensor.matmul(out_bank[a % 2][(h % 2) * LQ:(h % 2 + 1) * LQ, D + (h // 2) * HD:D + (h // 2 + 1) * HD],
                                            raw_out[a % 2][:, h, :], fold[:, h, :], start=True, stop=True)
                last.then_inc(folded, 1)

            def turn_heads(b):
                pe.wait_ge(scaled, NQ * (b + 1) + TWO)
                nc.tensor.transpose(out_bank[1][:, 384:512], by_query[:, :, :], ident[:, :]).then_inc(ct_turned, 1)

            def step(b, a, before=None, near=True, far=True, fill=True):
                for f in range(TB):
                    for m in NEAR.get(f, []) if near else []:
                        piece(*after(b, a), m)
                    for m in FAR.get(f, []) if far else []:
                        piece(*after(*after(b, a)), m)
                    weigh(b, a, f)
                    if f + 2 < TB:
                        turn(b, a, f + 2)
                    elif near:
                        turn(*after(b, a), f + 2 - TB)
                    if f == FOLD_AT and before is not None:
                        fold_heads(*before)
                    if f == CT_AT and before is not None and a == 0:
                        turn_heads(before[0])
                    if fill and a == 1 and 0 <= f - K_SLOT < NCOL:
                        project_k(b + 1, 0, f - K_SLOT)
                    if fill and a == NQ - 1:
                        project_v(b + 1, f)
                        if f < NCOL:
                            project_k(b + 1, 1, f)

            pe.sem_inc(s_read, TWO)
            pe.sem_inc(v_kept, ONE)
            pe.sem_inc(scaled, TWO)
            pe.sem_inc(ct_ready, ONE)
            for r in range(2):
                pe.sem_inc(t_kept[r], ONE)
            pe.wait_ge(w_step, 4)
            for j in range(NCOL):
                project_k(0, 0, j)
            pe.wait_ge(loaded, 64)
            for m in range(PIECES):
                piece(0, 0, m)
            for f in range(TB):
                project_v(0, f)
                if f < NCOL:
                    project_k(0, 1, f)
            for m in sum(FAR.values(), []):
                piece(0, 1, m)
            turn(0, 0, 0)
            turn(0, 0, 1)
            for a in range(NQ):
                step(0, a, before=(0, a - 1) if a else None)
            with pe.Fori(1, B - 1) as b:
                for a in range(NQ):
                    step(b, a, before=(b, a - 1) if a else (b - 1, NQ - 1))
            for a in range(NQ):
                step(B - 1, a, before=(B - 1, a - 1) if a else (B - 2, NQ - 1),
                     near=a < NQ - 1, far=a < NQ - 2, fill=False)
            fold_heads(B - 1, NQ - 1)
            turn_heads(B - 1)

        @block.scalar
        def _(act):
            def context_high(b, i):
                k, half = i // 2, i % 2
                cols = slice(half * (SP // 2), (half + 1) * (SP // 2))
                act.wait_ge(v_filled, TB * b + ONE)
                act.wait_ge(c_loaded[half], 32 * b + 16 * k + 16)
                nc.scalar.copy(cT[0][:, k, cols], raw_c[half][:, :]).then_inc(c_high, 1)

            def keep_k(b, c, j):
                at, n = COLS[j]
                act.wait_ge(k_filled, k_before(b, c, j) + 1)
                nc.scalar.activation(KT[0][:, c, at:at + n], proj_bank[k_bank(c, j)][:, 0:n], ACT.Identity,
                                     bias=bk[:, c:c + 1]).then_inc(k_high, 1)

            def keep_v(b, f):
                act.wait_ge(v_filled, TB * b + f + 1 + ONE)
                n, m = rows_of(2 * f), len(tiles_of(f))
                nc.scalar.copy(V[0:n, 2 * f:2 * f + m, :, 0, :],
                               proj_bank[v_bank(f)][0:n, 0:m * D].rearrange("p (t a c) -> p t a c", t=m, a=NQ)).then_inc(v_high, 1)

            def exponentials(b, a, i, half):
                u, r = unit(b, a), a % 2
                at, to = HALVES[half]
                act.wait_ge(max_ready, 2 * u + i + 1)
                if i == 0 and half == 0:
                    act.wait_ge(sums_taken, u - 1 + TWO)
                nc.scalar.activation(probs[r][:, i, at:to], probs[r][:, i, at:to], ACT.Exp, bias=neg_max[r][:, i:i + 1],
                                     accum_out=total[r][:, i, half:half + 1]).then_inc(exp_done, 1)

            def keep_turned(b, a, f):
                r, before = turn_of(b, a, f)
                n, m = rows_of(2 * f), len(tiles_of(f))
                act.wait_ge(t_filled[r], before + 1)
                act.wait_ge(t_used[r], before + ONE)
                nc.scalar.copy(PT[r][0][0:n, 0:m, :], turn_bank[r][0:n, 0:m * D].rearrange("p (t c) -> p t c", t=m))\
                    .then_inc(t_high[r], 1)

            def keep_product(b, a):
                u = unit(b, a)
                r, before = turn_of(b, a, TB - 1)
                act.wait_ge(t_used[r], before + 1 + ONE)
                act.wait_ge(folded, u - 1 + TWO)
                nc.scalar.copy(raw_out[a % 2][:, :, :], out_bank[a % 2][:, 0:D].rearrange("p (h q) -> p h q", h=QH))\
                    .then_inc(out_read, 1)

            def step(b, a, before=None, near=True, far=True, fill=True):
                for f in range(TB):
                    if f + 1 < TB:
                        keep_turned(b, a, f + 1)
                    elif near:
                        keep_turned(*after(b, a), 0)
                    if f == 0 and before is not None:
                        keep_product(*before)
                    if near and f in EXP_AT:
                        exponentials(*after(b, a), *EXP_AT[f])
                    if fill and (a, f) in C_AT:
                        context_high(b + 1, C_AT[a, f])
                    if fill and a == 1 and 0 <= f - K_SLOT < NCOL:
                        keep_k(b + 1, 0, f - K_SLOT)
                    if fill and a == NQ - 1:
                        keep_v(b + 1, f)
                        if f < NCOL:
                            keep_k(b + 1, 1, f)

            act.sem_inc(v_filled, ONE)
            act.sem_inc(sums_taken, TWO)
            act.sem_inc(folded, TWO)
            for r in range(2):
                act.sem_inc(t_used[r], ONE)
            for i in range(2 * KC):
                context_high(0, i)
            act.wait_ge(loaded, 64)
            for j in range(NCOL):
                keep_k(0, 0, j)
            for i, half in EXP_AT.values():
                exponentials(0, 0, i, half)
            for f in range(TB):
                keep_v(0, f)
                if f < NCOL:
                    keep_k(0, 1, f)
            keep_turned(0, 0, 0)
            for a in range(NQ):
                step(0, a, before=(0, a - 1) if a else None)
            with act.Fori(1, B - 1) as b:
                for a in range(NQ):
                    step(b, a, before=(b, a - 1) if a else (b - 1, NQ - 1))
            for a in range(NQ):
                step(B - 1, a, before=(B - 1, a - 1) if a else (B - 2, NQ - 1),
                     near=a < NQ - 1, far=a < NQ - 2, fill=False)
            keep_product(B - 1, NQ - 1)

        @block.vector
        def _(dve):
            def keep_k(b, c, j):
                at, n = COLS[j]
                dve.wait_ge(k_high, k_before(b, c, j) + 1)
                nc.vector.scalar_tensor_tensor(KT[1][:, c, at:at + n], proj_bank[k_bank(c, j)][:, 0:n], bk[:, c:c + 1],
                                               KT[0][:, c, at:at + n].bitcast(F32), ALU.add, ALU.subtract).then_inc(k_kept, 1)

            def keep_v(b, f):
                dve.wait_ge(v_high, TB * b + f + 1)
                n, m = rows_of(2 * f), len(tiles_of(f))
                nc.vector.tensor_tensor(V[0:n, 2 * f:2 * f + m, :, 1, :],
                                        proj_bank[v_bank(f)][0:n, 0:m * D].rearrange("p (t a c) -> p t a c", t=m, a=NQ),
                                        V[0:n, 2 * f:2 * f + m, :, 0, :].bitcast(F32), ALU.subtract).then_inc(v_kept, 1)

            def logits(b, a, m):
                u, r = unit(b, a), a % 2
                i, j = m // NCOL, m % NCOL
                at = COLS[j][0]
                n = min(COLS[j][1], S - at)
                dve.wait_ge(s_filled, PIECES * u + m + 1)
                stand(dve, passed_dve)
                nc.vector.tensor_tensor_reduce(probs[r][:, i, at:at + n], score_bank[m % 2][:, 0:n],
                                               bias[:, 2 * a + i, at:at + n], 1.0, LOWEST,
                                               ALU.add, ALU.max, top[r][:, i, j:j + 1]).then_inc(s_read, 1)
                if j == NCOL - 1:
                    dve.wait_ge(s_read, PIECES * u + m + 1 + TWO)
                    nc.vector.tensor_reduce(neg_max[r][:, i:i + 1], top[r][:, i, :], AX.X, ALU.max,
                                            negate=True).then_inc(max_ready, 1)

            def keep_turned(b, a, f):
                r, before = turn_of(b, a, f)
                n, m = rows_of(2 * f), len(tiles_of(f))
                dve.wait_ge(t_high[r], before + 1)
                nc.vector.tensor_tensor(PT[r][1][0:n, 0:m, :], turn_bank[r][0:n, 0:m * D].rearrange("p (t c) -> p t c", t=m),
                                        PT[r][0][0:n, 0:m, :].bitcast(F32), ALU.subtract).then_inc(t_kept[r], 1)

            def invert_sums(b, a):
                u, r = unit(b, a), a % 2
                dve.wait_ge(exp_done, 4 * u + 4)
                nc.vector.tensor_tensor(inverse[r][:, :], total[r][:, :, 0], total[r][:, :, 1], ALU.add).then_inc(sums_taken, 1)
                dve.wait_ge(sums_taken, u + 1 + TWO)
                nc.vector.reciprocal(inverse[r][:, :], inverse[r][:, :]).then_inc(sums_step, 1)

            def scale_heads(b, a):
                u, r = unit(b, a), a % 2
                dve.wait_ge(folded, u + 1 + TWO)
                dve.wait_ge(sums_step, u + 1)
                nc.vector.tensor_tensor(by_query[:, 2 * a:2 * a + 2, :], out_bank[r][:, D:D + 2 * HD].rearrange("p (i d) -> p i d", i=2),
                                        inverse[r][:, :].rearrange("p (i x) -> p i x", x=1).to_broadcast([P, 2, HD]),
                                        ALU.mult).then_inc(scaled, 1)

            def keep_heads(b):
                dve.wait_ge(ct_turned, b + 1)
                nc.vector.tensor_tensor(heads[:, :, bass.ds(b * LQ, LQ)], out_bank[1][:, 384:512].rearrange("p (h q) -> p h q", h=2),
                                        bv[:, :].rearrange("p (h x) -> p h x", x=1).to_broadcast([P, 2, LQ]), ALU.add).then_inc(ct_ready, 1)

            def step(b, a, before=None, near=True, far=True, fill=True):
                for f in range(TB):
                    if f + 1 < TB:
                        keep_turned(b, a, f + 1)
                    elif near:
                        keep_turned(*after(b, a), 0)
                    for m in NEAR.get(f, []) if near else []:
                        logits(*after(b, a), m)
                    for m in FAR.get(f, []) if far else []:
                        logits(*after(*after(b, a)), m)
                    if f == SUMS_AT:
                        invert_sums(b, a)
                    if f == FOLD_AT + 1 and before is not None:
                        scale_heads(*before)
                    if f == CT_AT + 1 and before is not None and a == 0:
                        keep_heads(before[0])
                    if fill and a == 1 and 0 <= f - K_SLOT < NCOL:
                        keep_k(b + 1, 0, f - K_SLOT)
                    if fill and a == NQ - 1:
                        keep_v(b + 1, f)
                        if f < NCOL:
                            keep_k(b + 1, 1, f)

            for i, (w, arrived) in enumerate(((wk, wk_loaded), (wv, wv_loaded))):
                dve.wait_ge(arrived, 16)
                nc.vector.tensor_copy(w[0][:, :, :], raw_w[:, :, :]).then_inc(w_step, 1)
                dve.wait_ge(w_step, 2 * i + 1)
                nc.vector.tensor_tensor(w[1][:, :, :], raw_w[:, :, :], w[0][:, :, :].bitcast(F32), ALU.subtract).then_inc(w_step, 1)
            dve.wait_ge(loaded, 64)
            for j in range(NCOL):
                keep_k(0, 0, j)
            for m in range(PIECES):
                logits(0, 0, m)
            for f in range(TB):
                keep_v(0, f)
                if f < NCOL:
                    keep_k(0, 1, f)
            for m in sum(FAR.values(), []):
                logits(0, 1, m)
            keep_turned(0, 0, 0)
            for a in range(NQ):
                step(0, a, before=(0, a - 1) if a else None)
            with dve.Fori(1, B - 1) as b:
                for a in range(NQ):
                    step(b, a, before=(b, a - 1) if a else (b - 1, NQ - 1))
            for a in range(NQ):
                step(B - 1, a, before=(B - 1, a - 1) if a else (B - 2, NQ - 1),
                     near=a < NQ - 1, far=a < NQ - 2, fill=False)
            scale_heads(B - 1, 3)
            keep_heads(B - 1)


def gated_attention(nc, dram, keep):
    with ExitStack() as ctx:
        sb = lambda name, shape: ctx.enter_context(nc.sbuf_tensor(name, shape, F32))
        bank = lambda name: ctx.enter_context(nc.psum_tensor(name, [P, 512], F32))
        sem = lambda name: ctx.enter_context(nc.semaphore(name))
        wo_x, bo_x = sb("wo_x", [P, KC, D]), sb("bo_x", [P, D])
        wq, wk = sb("a_wq", [P, KC, NH * DH]), sb("a_wk", [P, KC, KV * 2 * DH])
        wv, wg, wo = sb("a_wv", [P, KC, KV * DH]), sb("a_wg", [P, KC, NH * 3]), sb("a_wo", [P, QC, D])
        causal, at_last = sb("causal", [P, GH * LQ]), sb("at_last", [P, 1])
        heads = sb("heads", [P, KC, GTOK])
        stats, mv, std = sb("a_stats", [P, GT, 6]), sb("a_mv", [P, GT, 2]), sb("a_std", [P, GT])
        xn, xnT = sb("a_xn", [P, GT, D]), sb("a_xnT", [P, KC, GTOK])
        xn_twice = sb("xn_twice", [P, KC * GB, 2, LQ])
        QT = sb("a_QT", [P, QC, GTOK])
        KB = sb("a_KB", [P, KV, GB, 2, LQ])
        VB = sb("a_VB", [P, GB, KV, 2, DH])
        gate = sb("gate", [P, GT, NH * 3])
        gate_near, gate_mean = sb("gate_near", [P, GT, NH]), sb("gate_mean", [P, GT, NH])
        A = [sb(f"A{r}", [P, GH, LQ]) for r in range(RING)]
        top = [sb(f"a_top{r}", [P, GH]) for r in range(RING)]
        total = [sb(f"a_total{r}", [P, GH]) for r in range(RING)]
        AT = [sb(f"AT{r}", [P, CH, 2, LQ]) for r in range(2)]
        OT = [sb(f"OT{r}", [P, QC, 2, LQ]) for r in range(2)]
        proj_bank = [bank(f"a_proj_bank{r}") for r in range(2)]
        score_bank = [bank(f"a_score_bank{r}") for r in range(2)]
        turn_bank = [bank(f"a_turn_bank{r}") for r in range(2)]
        out_bank = [bank(f"a_out_bank{r}") for r in range(2)]

        loaded, w_loaded, late_loaded = sem("a_loaded"), sem("a_w_loaded"), sem("a_late_loaded")
        zeroed = sem("a_zeroed")
        heads_ready, bo_added = sem("heads_ready"), sem("bo_added")
        h_filled, h_added = sem("h_filled"), sem("h_added")
        chain, std_ready, normed = sem("a_chain"), sem("a_std_ready"), sem("a_normed")
        xT_filled, xT_kept, twice_ready = sem("a_xT_filled"), sem("a_xT_kept"), sem("twice_ready")
        p_filled, p_kept = sem("p_filled"), [sem(f"p_kept{r}") for r in range(2)]
        gate_step, gate_ready = sem("gate_step"), sem("gate_ready")
        s_filled, s_read = sem("a_s_filled"), sem("a_s_read")
        top_ready, moved, exp_done = sem("a_top_ready"), sem("a_moved"), sem("a_exp_done")
        sum_step, scale_ready, scaled, A_ready = sem("a_sum_step"), sem("a_scale_ready"), sem("a_scaled"), sem("A_ready")
        t_filled, t_kept, o_filled, o_kept = sem("a_t_filled"), sem("a_t_kept"), sem("o_filled"), sem("o_kept")
        w_filled, w_added = sem("w_filled"), sem("w_added")
        passed, passed_pool = sem("a_passed"), sem("a_passed_pool")
        x_all, CT, ident = keep["x_all"], keep["heads"], keep["ident"]
        N_LOAD, N_W, N_LATE = 3 * 16, 4 * 16, 3 * 16
        GATE_FILL = NP - 1
        block = ctx.enter_context(nc.Block())

        ONE = 1

        def since(g, per, n, ring):
            return g * per + max(n + 1 - ring, 0) + ONE

        @block.sync
        def _(sp):
            chunked = lambda ap: ap.rearrange("(k p) n -> p k n", p=P)

            sp.dma_start(wo_x[:, :, :], chunked(dram["wo_x"])).then_inc(loaded, 16)
            sp.dma_start(bo_x[:, :], dram["bo_x"]).then_inc(loaded, 16)
            sp.dma_start(x_all[:, :, :], dram["x"].rearrange("(t p) d -> p t d", p=P)).then_inc(loaded, 16)
            sp.dma_start(wq[:, :, :], chunked(dram["a_wq"])).then_inc(w_loaded, 16)
            sp.dma_start(wk[:, :, :], chunked(dram["a_wk"])).then_inc(w_loaded, 16)
            sp.dma_start(wv[:, :, :], chunked(dram["a_wv"])).then_inc(w_loaded, 16)
            sp.dma_start(wg[:, :, :], chunked(dram["a_wg"])).then_inc(w_loaded, 16)
            sp.dma_start(causal[:, :], dram["causal"]).then_inc(late_loaded, 16)
            sp.dma_start(at_last[:, :], dram["at_last"]).then_inc(late_loaded, 16)
            sp.dma_start(wo[:, :, :], chunked(dram["a_wo"])).then_inc(late_loaded, 16)

        @block.tensor
        def _(pe):
            pe.sem_inc(t_filled, ONE)
            pe.sem_inc(o_filled, ONE)
            pe.sem_inc(w_filled, ONE)
            pe.sem_inc(h_filled, ONE)
            pe.wait_ge(loaded, N_LOAD)
            pe.wait_ge(zeroed, 2)
            with pe.Fori(0, NG) as g:
                pe.wait_ge(heads_ready, g + 1)
                pe.wait_ge(w_added, GT * g + ONE)
                for f in range(GT // 2):
                    for j in (2 * f, 2 * f + 1):
                        for k in range(KC):
                            last = nc.tensor.matmul(proj_bank[f][:, (j % 2) * D:(j % 2 + 1) * D], heads[:, k, j * P:(j + 1) * P],
                                                    wo_x[:, k, :], start=(k == 0), stop=(k == KC - 1))
                    last.then_inc(h_filled, 1)
                pe.wait_ge(normed, g + 1)
                for k in range(KC):
                    for j in range(GT):
                        last = nc.tensor.transpose(proj_bank[k][:, j * P:(j + 1) * P], xn[:, j, k * P:(k + 1) * P], ident[:, :])
                    last.then_inc(xT_filled, 1)
                pe.wait_ge(xT_kept, KC * (g + 1))
                pe.wait_ge(w_loaded, N_W)
                for i in range(NP):
                    pe.wait_ge(p_kept[i % 2], g * NPR[i % 2] + i // 2 + ONE)
                    to = proj_bank[i % 2]
                    if i < QC:
                        for k in range(KC):
                            last = nc.tensor.matmul(to[:, :], wq[:, k, i * P:(i + 1) * P], xnT[:, k, :],
                                                    start=(k == 0), stop=(k == KC - 1))
                    elif i < QC + KV:
                        n = i - QC
                        for k in range(KC):
                            last = nc.tensor.matmul(to[:, :], wk[:, k, n * P:(n + 1) * P], xnT[:, k, :],
                                                    start=(k == 0), stop=(k == KC - 1))
                    elif i < GATE_FILL:
                        pe.wait_ge(twice_ready, g + 1)
                        for half in range(2):
                            b = 2 * (i - QC - KV) + half
                            for k in range(KC):
                                last = nc.tensor.matmul(to[:, half * D:(half + 1) * D],
                                                        xn_twice[:, k * GB + b, :, :],
                                                        wv[:, k, :], start=(k == 0), stop=(k == KC - 1))
                    else:
                        for j in range(GT):
                            for k in range(KC):
                                last = nc.tensor.matmul(to[:, j * NH * 3:(j + 1) * NH * 3], xnT[:, k, j * P:(j + 1) * P],
                                                        wg[:, k, :], start=(k == 0), stop=(k == KC - 1))
                    last.then_inc(p_filled, 1)
                pe.wait_ge(late_loaded, N_LATE)
                for r in range(2):
                    pe.wait_ge(p_kept[r], (g + 1) * NPR[r] + ONE)
                for n in range(-AHEAD, UNITS + 2):
                    if n + AHEAD < UNITS:
                        m = n + AHEAD
                        j, kv = m // KV, m % KV
                        pe.wait_ge(s_read, since(g, UNITS, m, 2))
                        for half in range(2):
                            b = 2 * j + half
                            for c in range(CH):
                                last = nc.tensor.matmul(score_bank[m % 2][half * LQ:(half + 1) * LQ, c * P:(c + 1) * P],
                                                        QT[:, kv * CH + c, b * LQ:(b + 1) * LQ], KB[:, kv, b, :, :],
                                                        start=True, stop=True)
                        last.then_inc(s_filled, 1)
                    if 0 <= n < UNITS:
                        pe.wait_ge(A_ready, g * UNITS + n + 1 + ONE)
                        pe.wait_ge(t_kept, since(g, UNITS, n, 2))
                        for c in range(CH):
                            last = nc.tensor.transpose(turn_bank[n % 2][:, c * P:(c + 1) * P],
                                                       A[n % RING][:, 2 * c:2 * c + 2, :], ident[:, :])
                        last.then_inc(t_filled, 1)
                    if 1 <= n <= UNITS:
                        m = n - 1
                        j, kv = m // KV, m % KV
                        pe.wait_ge(t_kept, g * UNITS + m + 1 + ONE)
                        pe.wait_ge(o_kept, since(g, UNITS, m, 2))
                        for half in range(2):
                            last = nc.tensor.matmul(out_bank[m % 2][:, half * CH * LQ:(half + 1) * CH * LQ],
                                                    VB[:, 2 * j + half, kv, :, :], AT[m % 2][:, :, half, :],
                                                    start=True, stop=True)
                        last.then_inc(o_filled, 1)
                    if n >= KV + 1 and (n - 1) % KV == 0:
                        j = (n - 1) // KV - 1
                        pe.wait_ge(o_kept, g * UNITS + KV * (j + 1) + ONE)
                        pe.wait_ge(w_added, since(g, GT, j, 2))
                        for c in range(QC):
                            last = nc.tensor.matmul(proj_bank[j % 2][:, 0:D], OT[j % 2][:, c, :, :], wo[:, c, :],
                                                    start=(c == 0), stop=(c == QC - 1))
                        last.then_inc(w_filled, 1)

        def keep_projection(eng, g, i, copy):
            eng.wait_ge(p_filled, g * NP + i + 1)
            src = proj_bank[i % 2]
            if i < QC:
                last = copy(QT[:, i, :], src[:, :], float(DH) ** -0.5)
            elif i < QC + KV:
                for half in range(2):
                    rows = slice(half * DH, (half + 1) * DH)
                    last = copy(KB[rows, i - QC, :, half, :], src[rows, :].rearrange("p (b s) -> p b s", b=GB), 1.0)
            elif i < GATE_FILL:
                b = 2 * (i - QC - KV)
                for half in range(2):
                    rows = slice(half * LQ, (half + 1) * LQ)
                    for one in range(2):
                        last = copy(VB[rows, b + one, :, half, :],
                                    src[rows, one * D:(one + 1) * D].rearrange("p (v d) -> p v d", v=KV), 1.0)
            last.then_inc(p_kept[i % 2], 1)

        @block.vector
        def _(dve):
            dve.sem_inc(s_read, ONE)
            dve.sem_inc(w_added, ONE)
            dve.wait_ge(zeroed, 2)
            with dve.Fori(0, NG) as g:
                for f in range(GT // 2):
                    dve.wait_ge(h_filled, GT // 2 * g + f + 1 + ONE)
                    dve.wait_ge(bo_added, g + 1)
                    tiles = x_all[:, bass.ds(g * GT + 2 * f, 2), :]
                    nc.vector.tensor_tensor(tiles, proj_bank[f][:, :].rearrange("p (t n) -> p t n", t=2), tiles,
                                            ALU.add).then_inc(h_added, 1)
                dve.wait_ge(h_added, GT // 2 * (g + 1))
                layer_norm(dve, nc, lambda j: x_all[:, bass.ds(g * GT + j, 1), :].rearrange("p a d -> p (a d)"),
                           g, stats, mv, std, xn, chain, std_ready, passed).then_inc(normed, 1)
                for i in range(1, NP, 2):
                    keep_projection(dve, g, i, lambda o, s, f: nc.vector.tensor_scalar(o, s, f, None, ALU.mult))
                dve.wait_ge(late_loaded, N_LATE)
                dve.wait_ge(p_kept[0], (g + 1) * NPR[0] + ONE)
                nc.vector.tensor_scalar(gate[:, :, :], gate[:, :, :], 1.0, None, ALU.add).then_inc(gate_step, 1)
                dve.wait_ge(gate_step, 2 * g + 1)
                nc.vector.reciprocal(gate[:, :, :], gate[:, :, :]).then_inc(gate_step, 1)
                dve.wait_ge(gate_step, 2 * g + 2)
                by_kind = gate[:, :, :].rearrange("p t (h k) -> p t h k", k=3)
                nc.vector.tensor_tensor(gate_near[:, :, :], by_kind[:, :, :, 1], by_kind[:, :, :, 2], ALU.add)\
                    .then_inc(gate_ready, 1)
                nc.vector.tensor_scalar(gate_mean[:, :, :], by_kind[:, :, :, 0], at_last[:, 0:1], None, ALU.mult)\
                    .then_inc(gate_ready, 1)
                dve.wait_ge(gate_ready, 2 * g + 2)
                for n in range(-AHEAD, UNITS + 2):
                    if n + AHEAD < UNITS:
                        m = n + AHEAD
                        r = m % RING
                        dve.wait_ge(s_filled, g * UNITS + m + 1)
                        dve.wait_ge(t_filled, since(g, UNITS, m, RING))
                        nc.vector.tensor_tensor(A[r][:, :, :], score_bank[m % 2][:, :].rearrange("p (h s) -> p h s", h=GH),
                                                causal[:, :].rearrange("p (h s) -> p h s", h=GH), ALU.add).then_inc(s_read, 1)
                        dve.wait_ge(s_read, g * UNITS + m + 1 + ONE)
                        nc.vector.tensor_reduce(top[r][:, :], A[r][:, :, :], AX.X, ALU.max).then_inc(top_ready, 1)
                    if 0 <= n + AHEAD - 1 < UNITS:
                        m = n + AHEAD - 1
                        r, j, kv = m % RING, m // KV, m % KV
                        dve.wait_ge(exp_done, g * UNITS + m + 1)
                        nc.vector.tensor_reduce(total[r][:, :], A[r][:, :, :], AX.X, ALU.add).then_inc(sum_step, 1)
                        dve.wait_ge(sum_step, 2 * (g * UNITS + m) + 1)
                        nc.vector.reciprocal(total[r][:, :], total[r][:, :]).then_inc(sum_step, 1)
                        dve.wait_ge(sum_step, 2 * (g * UNITS + m) + 2)
                        nc.vector.tensor_tensor(total[r][:, :], total[r][:, :], gate_near[:, j, kv * GH:(kv + 1) * GH],
                                                ALU.mult).then_inc(scale_ready, 1)
                    if n >= KV + 1 and (n - 1) % KV == 0:
                        j = (n - 1) // KV - 1
                        dve.wait_ge(w_filled, GT * g + j + 1 + ONE)
                        tile = x_all[:, bass.ds(g * GT + j, 1), :]
                        nc.vector.tensor_tensor(tile, proj_bank[j % 2][:, 0:D].rearrange("p (a n) -> p a n", a=1), tile,
                                                ALU.add).then_inc(w_added, 1)

        @block.scalar
        def _(act):
            act.sem_inc(t_kept, ONE)
            act.sem_inc(o_kept, ONE)
            act.sem_inc(p_kept[0], ONE)
            act.sem_inc(p_kept[1], ONE)
            act.wait_ge(zeroed, 2)
            with act.Fori(0, NG) as g:
                layer_norm_root(act, nc, g, std, chain, std_ready)
                for k in range(KC):
                    act.wait_ge(xT_filled, KC * g + k + 1)
                    nc.scalar.copy(xnT[:, k, :], proj_bank[k][:, :]).then_inc(xT_kept, 1)
                for i in range(0, NP - 1, 2):
                    keep_projection(act, g, i, lambda o, s, f: nc.scalar.activation(o, s, ACT.Copy, scale=f))
                act.wait_ge(p_filled, g * NP + NP)
                act.wait_ge(A_ready, g * UNITS + ONE)
                nc.scalar.activation(gate[:, :, :], proj_bank[GATE_FILL % 2][:, 0:GT * NH * 3].rearrange("p (t n) -> p t n", t=GT),
                                     ACT.Exp, scale=-1.0).then_inc(p_kept[0], 1)
                for n in range(-AHEAD, UNITS + 2):
                    if 0 <= n < UNITS:
                        act.wait_ge(t_filled, g * UNITS + n + 1 + ONE)
                        act.wait_ge(o_filled, since(g, UNITS, n, 2))
                        nc.scalar.copy(AT[n % 2][:, :, :, :], turn_bank[n % 2][:, :].rearrange("p (c b t) -> p c b t", c=CH, b=2))\
                            .then_inc(t_kept, 1)
                    if 1 <= n <= UNITS:
                        m = n - 1
                        j, kv = m // KV, m % KV
                        act.wait_ge(o_filled, g * UNITS + m + 1 + ONE)
                        act.wait_ge(w_filled, since(g, GT, j, 2))
                        nc.scalar.copy(OT[j % 2][:, kv * CH:(kv + 1) * CH, :, :].rearrange("p c b t -> p b c t"),
                                       out_bank[m % 2][:, :].rearrange("p (b c t) -> p b c t", b=2, c=CH)).then_inc(o_kept, 1)
                    if n + AHEAD < UNITS:
                        m = n + AHEAD
                        act.wait_ge(moved, g * UNITS + m + 1)
                        nc.scalar.activation(A[m % RING][:, :, :], A[m % RING][:, :, :], ACT.Exp).then_inc(exp_done, 1)

        @block.gpsimd
        def _(pool):
            pool.sem_inc(A_ready, ONE)
            nc.gpsimd.memset(KB[:, :, :, :, :], 0.0).then_inc(zeroed, 1)
            nc.gpsimd.memset(VB[:, :, :, :, :], 0.0).then_inc(zeroed, 1)
            pool.wait_ge(loaded, N_LOAD)
            with pool.Fori(0, NG) as g:
                pool.wait_ge(h_filled, GT // 2 * g + ONE)
                nc.gpsimd.tensor_copy(heads[:, :, :], CT[:, :, bass.ds(g * GTOK, GTOK)]).then_inc(heads_ready, 1)
                tiles = x_all[:, bass.ds(g * GT, GT), :]
                nc.gpsimd.tensor_tensor(tiles, tiles, bo_x[:, :].rearrange("p (a n) -> p a n", a=1).to_broadcast([P, GT, D]),
                                        ALU.add).then_inc(bo_added, 1)
                pool.wait_ge(xT_kept, KC * (g + 1))
                stand(pool, passed_pool)
                for half in range(2):
                    last = nc.gpsimd.tensor_copy(xn_twice[:, :, half, :], xnT[:, :, :].rearrange("p k (b s) -> p (k b) s", s=LQ))
                last.then_inc(twice_ready, 1)
                pool.wait_ge(gate_ready, 2 * g + 2)
                for n in range(-AHEAD, UNITS):
                    if n + AHEAD < UNITS:
                        m = n + AHEAD
                        r = m % RING
                        pool.wait_ge(top_ready, g * UNITS + m + 1)
                        nc.gpsimd.tensor_tensor(A[r][:, :, :], A[r][:, :, :],
                                                top[r][:, :].rearrange("p (h a) -> p h a", a=1).to_broadcast([P, GH, LQ]),
                                                ALU.subtract).then_inc(moved, 1)
                    if 0 <= n + AHEAD - 1 < UNITS:
                        m = n + AHEAD - 1
                        r, j, kv = m % RING, m // KV, m % KV
                        pool.wait_ge(scale_ready, g * UNITS + m + 1)
                        nc.gpsimd.tensor_tensor(A[r][:, :, :], A[r][:, :, :],
                                                total[r][:, :].rearrange("p (h a) -> p h a", a=1).to_broadcast([P, GH, LQ]),
                                                ALU.mult).then_inc(scaled, 1)
                        pool.wait_ge(scaled, g * UNITS + m + 1)
                        nc.gpsimd.tensor_tensor(A[r][:, :, :], A[r][:, :, :],
                                                gate_mean[:, j, kv * GH:(kv + 1) * GH].rearrange("p (h a) -> p h a", a=1)
                                                .to_broadcast([P, GH, LQ]), ALU.add).then_inc(A_ready, 1)


def experts(nc, dram, keep, out):
    with ExitStack() as ctx:
        sb = lambda name, shape, dt=F32: ctx.enter_context(nc.sbuf_tensor(name, shape, dt))
        bank = lambda name: ctx.enter_context(nc.psum_tensor(name, [P, 512], F32))
        sem = lambda name: ctx.enter_context(nc.semaphore(name))
        pair = lambda name, shape: [sb(name + part, shape, F32R) for part in ("_high", "_low")]
        raw_w1, raw_w2 = sb("raw_w1", [P, KC, FF]), sb("raw_w2", [P, FC, D])
        w1 = [pair(f"w1_{r}", [P, KC, FF]) for r in range(2)]
        w2 = [pair(f"w2_{r}", [P, FC, D]) for r in range(2)]
        b1 = [sb(f"b1_{r}", [P, FC]) for r in range(2)]
        b2 = [sb(f"b2_{r}", [P, D]) for r in range(2)]
        wr, br = sb("wr", [P, KC, NE]), sb("br", [P, NE])
        which = sb("which", [P, NE])
        stats, mv, std = sb("f_stats", [P, GT, 6]), sb("f_mv", [P, GT, 2]), sb("f_std", [P, GT])
        xn, xnT = sb("f_xn", [P, GT, D]), sb("f_xnT", [P, KC, GTOK])
        allT = pair("allT", [P, KC, TOK])
        logit, best = sb("logit", [P, NT, NE]), sb("best", [P, NT, NE])
        place = sb("place", [P, NT, NE], mybir.dt.uint32)
        placef = sb("placef", [P, NT, NE])
        first, second = sb("first", [P, NT, NE]), sb("second", [P, NT, NE])
        total = sb("f_total", [P, NT])
        share = sb("share", [P, NE * NT])
        h_raw = [sb(f"h_raw{r}", [P, 2, UTOK]) for r in range(2)]
        hT = [pair(f"hT{r}", [P, FC, UTOK]) for r in range(2)]
        y = [sb(f"y{r}", [P, UT, D]) for r in range(2)]
        up_bank = [bank(f"up_bank{r}") for r in range(UPB)]
        down_bank = [bank(f"down_bank{r}") for r in range(2)]

        loaded, raw_loaded = sem("f_loaded"), sem("raw_loaded")
        b_loaded = [sem(f"b_loaded{r}") for r in range(2)]
        w_high, w_low = sem("w_high"), sem("w_low")
        chain, std_ready, normed = sem("f_chain"), sem("f_std_ready"), sem("f_normed")
        xT_filled, xT_kept, all_kept = sem("f_xT_filled"), sem("f_xT_kept"), sem("all_kept")
        r_filled, r_step, r_exp = sem("r_filled"), sem("r_step"), sem("r_exp")
        up_filled, up_read, h_kept = sem("up_filled"), sem("up_read"), sem("h_kept")
        down_filled, y_step, added = sem("down_filled"), sem("y_step"), sem("added")
        stored = sem("stored")
        passed, passed_pe, passed_act = [sem("f_passed" + x) for x in ("", "_pe", "_act")]
        x_all, ident = keep["x_all"], keep["ident"]
        R_LESS = 2 * NT + 2
        ONE, TWO = 1, 2
        FREE = 2 * EU
        block = ctx.enter_context(nc.Block())

        @block.sync
        def _(sp):
            sp.dma_start(wr[:, :, :], dram["wr"].rearrange("(k p) n -> p k n", p=P)).then_inc(loaded, 16)
            sp.dma_start(br[:, :], dram["br"]).then_inc(loaded, 16)
            sp.dma_start(which[:, :], dram["which"]).then_inc(loaded, 16)

            def load_weights(e):
                sp.dma_start(raw_w1[:, :, :], dram["w1"][bass.ds(e, 1)].rearrange("a (k p) f -> p (a k) f", p=P)).then_inc(raw_loaded, 16)
                sp.dma_start(raw_w2[:, :, :], dram["w2"][bass.ds(e, 1)].rearrange("a (k p) f -> p (a k) f", p=P)).then_inc(raw_loaded, 16)

            def load_biases(e, r):
                sp.dma_start(b1[r][:, :], dram["b1"][bass.ds(e, 1)].rearrange("a p f -> p (a f)")).then_inc(b_loaded[r], 16)
                sp.dma_start(b2[r][:, :], dram["b2"][bass.ds(e, 1)].rearrange("a p f -> p (a f)")).then_inc(b_loaded[r], 16)

            load_weights(0)
            load_biases(0, 0)
            load_biases(1, 1)
            sp.wait_ge(w_low, 2)
            load_weights(1)
            with sp.Fori(1, NE // 2) as i:
                for r in range(2):
                    sp.wait_ge(w_low, 2 * (2 * i + r))
                    load_weights(2 * i + r)
                    sp.wait_ge(added, EU * (2 * i + r - 1))
                    load_biases(2 * i + r, r)
            sp.wait_ge(added, EU * NE)
            sp.dma_start(out.rearrange("(t p) d -> p t d", p=P), x_all[:, :, :]).then_inc(stored, 16)
            sp.wait_ge(stored, 16)

        @block.gpsimd
        def _(pool):
            def weights_low(e, r):
                for i, (raw, w) in enumerate(((raw_w1, w1[r]), (raw_w2, w2[r]))):
                    pool.wait_ge(w_high, 2 * e + i + 1)
                    nc.gpsimd.tensor_tensor(w[1][:, :, :], raw[:, :, :], w[0][:, :, :].bitcast(F32),
                                            ALU.subtract).then_inc(w_low, 1)

            pool.wait_ge(raw_loaded, 32)
            for raw, w in ((raw_w1, w1[0]), (raw_w2, w2[0])):
                nc.gpsimd.tensor_copy(w[0][:, :, :], raw[:, :, :]).then_inc(w_high, 1)
            weights_low(0, 0)
            weights_low(1, 1)
            with pool.Fori(1, NE // 2) as i:
                for r in range(2):
                    weights_low(2 * i + r, r)

        @block.tensor
        def _(pe):
            pe.sem_inc(down_filled, FREE)
            pe.sem_inc(xT_filled, ONE)
            pe.sem_inc(r_filled, ONE)
            pe.wait_ge(loaded, 48)
            with pe.Fori(0, NG) as g:
                pe.wait_ge(normed, g + 1)
                pe.wait_ge(xT_kept, 2 * KC * g + ONE)
                for k in range(KC):
                    for j in range(GT):
                        last = nc.tensor.transpose(up_bank[k][:, j * P:(j + 1) * P], xn[:, j, k * P:(k + 1) * P], ident[:, :])
                    last.then_inc(xT_filled, 1)
                pe.wait_ge(xT_kept, 2 * KC * (g + 1) + ONE)
                for j in range(GT):
                    for k in range(KC):
                        last = nc.tensor.matmul(down_bank[0][:, bass.ds((g * GT + j) * NE, NE)], xnT[:, k, j * P:(j + 1) * P],
                                                wr[:, k, :], start=(k == 0), stop=(k == KC - 1))
                last.then_inc(r_filled, 1)

            def three(to, left, right, n_k):
                todo = [(k, x, y) for k in range(n_k) for x, y in ((0, 0), (0, 1), (1, 0))]
                for i, (k, x, y) in enumerate(todo):
                    last = nc.tensor.matmul(to, left(k, x), right(k, y), start=(i == 0), stop=(i == len(todo) - 1))
                return last

            def up(e, r, g):
                u = e * EU + g
                for q in range(UPB):
                    pe.wait_ge(up_read, UPB * (u - 1) + q + 1 + UPB)
                    for half in range(2):
                        f = 2 * q + half
                        last = three(up_bank[q][:, half * UTOK:(half + 1) * UTOK], lambda k, x: w1[r][x][:, k, f * P:(f + 1) * P],
                                     lambda k, y: allT[y][:, k, bass.ds(g * UTOK, UTOK)], KC)
                    last.then_inc(up_filled, 1)

            def down(e, r, g, s):
                u = e * EU + g
                pe.wait_ge(h_kept, UPB * (u + 1) + TWO)
                pe.wait_ge(y_step, Y_STEPS * (u - 1) + Y_READ + FREE)
                for j in range(UT):
                    last = three(down_bank[s][:, j * D:(j + 1) * D], lambda f, x: hT[s][x][:, f, j * P:(j + 1) * P],
                                 lambda f, y: w2[r][y][:, f, :], FC)
                last.then_inc(down_filled, 1)

            pe.wait_ge(all_kept, NG + ONE)
            pe.wait_ge(r_step, 1)
            with pe.Fori(0, NE // 2) as i:
                for r in range(2):
                    pe.wait_ge(w_low, 2 * (2 * i + r + 1))
                    stand(pe, passed_pe)
                    with pe.Fori(0, EU // 2) as g:
                        for s in range(2):
                            up(2 * i + r, r, 2 * g + s)
                        for s in range(2):
                            down(2 * i + r, r, 2 * g + s, s)

        @block.scalar
        def _(act):
            act.sem_inc(xT_kept, ONE)
            act.sem_inc(up_read, UPB)
            with act.Fori(0, NG) as g:
                layer_norm_root(act, nc, g, std, chain, std_ready)
                act.wait_ge(all_kept, g + ONE)
                act.wait_ge(r_filled, g + ONE)
                for k in range(KC):
                    act.wait_ge(xT_filled, KC * g + k + 1 + ONE)
                    nc.scalar.copy(xnT[:, k, :], up_bank[k][:, :]).then_inc(xT_kept, 1)
                    nc.scalar.copy(allT[0][:, k, bass.ds(g * GTOK, GTOK)], up_bank[k][:, :]).then_inc(xT_kept, 1)

            act.wait_ge(r_step, R_LESS)
            nc.scalar.activation(logit[:, :, :], logit[:, :, :], ACT.Exp).then_inc(r_exp, 1)

            def weights_high(e, r):
                act.wait_ge(raw_loaded, 32 * (e + 1))
                act.wait_ge(down_filled, EU * (e - 1) + FREE)
                for raw, w in ((raw_w1, w1[r]), (raw_w2, w2[r])):
                    nc.scalar.copy(w[0][:, :, :], raw[:, :, :]).then_inc(w_high, 1)

            def relu(e, r, g, s):
                u = e * EU + g
                act.wait_ge(down_filled, u - 1 + FREE)
                for q in range(UPB):
                    act.wait_ge(up_filled, UPB * u + q + 1)
                    act.wait_ge(h_kept, UPB * u + q - 1 + TWO)
                    for to in (h_raw[q % 2][:, :, :], hT[s][0][:, 2 * q:2 * q + 2, :]):
                        for half in range(2):
                            last = nc.scalar.activation(to[:, half, :], up_bank[q][:, half * UTOK:(half + 1) * UTOK], ACT.Relu,
                                                        bias=b1[r][:, 2 * q + half:2 * q + half + 1])
                    last.then_inc(up_read, 1)

            def expert(i, r, following=True):
                act.wait_ge(b_loaded[r], 32 * (i + 1))
                if following:
                    weights_high(2 * i + r + 1, 1 - r)
                stand(act, passed_act)
                with act.Fori(0, EU // 2) as g:
                    for s in range(2):
                        relu(2 * i + r, r, 2 * g + s, s)

            with act.Fori(0, NE // 2 - 1) as i:
                for r in range(2):
                    expert(i, r)
            expert(NE // 2 - 1, 0)
            expert(NE // 2 - 1, 1, following=False)

        @block.vector
        def _(dve):
            dve.sem_inc(h_kept, TWO)
            dve.sem_inc(y_step, FREE)
            dve.sem_inc(all_kept, ONE)
            dve.wait_ge(loaded, 48)
            with dve.Fori(0, NG) as g:
                dve.wait_ge(xT_filled, KC * g + ONE)
                layer_norm(dve, nc, lambda j: x_all[:, bass.ds(g * GT + j, 1), :].rearrange("p a d -> p (a d)"),
                           g, stats, mv, std, xn, chain, std_ready, passed).then_inc(normed, 1)
                dve.wait_ge(xT_kept, 2 * KC * (g + 1) + ONE)
                stand(dve, passed)
                nc.vector.tensor_tensor(allT[1][:, :, bass.ds(g * GTOK, GTOK)], xnT[:, :, :],
                                        allT[0][:, :, bass.ds(g * GTOK, GTOK)].bitcast(F32), ALU.subtract).then_inc(all_kept, 1)
            dve.wait_ge(r_filled, NG + ONE)
            nc.vector.tensor_tensor(logit[:, :, :], down_bank[0][:, 0:NT * NE].rearrange("p (t e) -> p t e", t=NT),
                                    br[:, :].rearrange("p (a e) -> p a e", a=1).to_broadcast([P, NT, NE]), ALU.add).then_inc(r_step, 1)
            dve.wait_ge(r_step, 1)
            for t in range(NT):
                nc.vector.max(best[:, t, :], logit[:, t, :]).then_inc(r_step, 1)
            dve.wait_ge(r_step, 1 + NT)
            for t in range(NT):
                nc.vector.max_index(place[:, t, :], best[:, t, :], logit[:, t, :]).then_inc(r_step, 1)
            at = 1 + 2 * NT
            dve.wait_ge(r_step, at)
            nc.vector.tensor_tensor(logit[:, :, :], logit[:, :, :], best[:, :, 0:1].to_broadcast([P, NT, NE]), ALU.subtract).then_inc(r_step, 1)
            nc.vector.tensor_copy(placef[:, :, :], place[:, :, :]).then_inc(r_step, 1)
            dve.wait_ge(r_step, at + 2)
            ids = which[:, :].rearrange("p (a e) -> p a e", a=1).to_broadcast([P, NT, NE])
            nc.vector.tensor_tensor(first[:, :, :], ids, placef[:, :, 0:1].to_broadcast([P, NT, NE]), ALU.is_equal).then_inc(r_step, 1)
            nc.vector.tensor_tensor(second[:, :, :], ids, placef[:, :, 1:2].to_broadcast([P, NT, NE]), ALU.is_equal).then_inc(r_step, 1)
            dve.wait_ge(r_step, at + 4)
            nc.vector.tensor_tensor(first[:, :, :], first[:, :, :], second[:, :, :], ALU.add).then_inc(r_step, 1)
            dve.wait_ge(r_step, at + 5)
            dve.wait_ge(r_exp, 1)
            nc.vector.tensor_tensor(first[:, :, :], first[:, :, :], logit[:, :, :], ALU.mult).then_inc(r_step, 1)
            dve.wait_ge(r_step, at + 6)
            nc.vector.tensor_reduce(total[:, :], first[:, :, :], AX.X, ALU.add).then_inc(r_step, 1)
            dve.wait_ge(r_step, at + 7)
            nc.vector.reciprocal(total[:, :], total[:, :]).then_inc(r_step, 1)
            dve.wait_ge(r_step, at + 8)
            nc.vector.tensor_tensor(share[:, :].rearrange("p (e t) -> p e t", e=NE), first[:, :, :].rearrange("p t e -> p e t"),
                                    total[:, :].rearrange("p (a t) -> p a t", a=1).to_broadcast([P, NE, NT]),
                                    ALU.mult).then_inc(r_step, 1)
            dve.wait_ge(r_step, at + 9)

            def h_low(e, r, g, s):
                u = e * EU + g
                for q in range(UPB):
                    dve.wait_ge(up_read, UPB * u + q + 1 + UPB)
                    nc.vector.tensor_tensor(hT[s][1][:, 2 * q:2 * q + 2, :], h_raw[q % 2][:, :, :],
                                            hT[s][0][:, 2 * q:2 * q + 2, :].bitcast(F32), ALU.subtract).then_inc(h_kept, 1)

            def add_share(e, r, g, s):
                u = e * EU + g
                tiles = x_all[:, bass.ds(g * UT, UT), :]
                dve.wait_ge(down_filled, u + 1 + FREE)
                nc.vector.tensor_tensor(y[s][:, :, :], down_bank[s][:, :].rearrange("p (t n) -> p t n", t=UT),
                                        b2[r][:, :].rearrange("p (t n) -> p t n", t=1).to_broadcast([P, UT, D]), ALU.add).then_inc(y_step, 1)
                dve.wait_ge(y_step, Y_STEPS * u + 1 + FREE)
                nc.vector.tensor_tensor(y[s][:, :, :], y[s][:, :, :],
                                        share[:, bass.ds(e * NT + g * UT, UT)].rearrange("p (t n) -> p t n", n=1)
                                        .to_broadcast([P, UT, D]), ALU.mult).then_inc(y_step, 1)
                dve.wait_ge(y_step, Y_STEPS * u + 2 + FREE)
                nc.vector.tensor_tensor(tiles, tiles, y[s][:, :, :], ALU.add).then_inc(added, 1)

            with dve.Fori(0, NE // 2) as i:
                for r in range(2):
                    dve.wait_ge(b_loaded[r], 32 * (i + 1))
                    stand(dve, passed)
                    with dve.Fori(0, EU // 2) as g:
                        for s in range(2):
                            h_low(2 * i + r, r, 2 * g + s, s)
                        for s in range(2):
                            add_share(2 * i + r, r, 2 * g + s, s)


def build_program(nc, dram, out):
    with ExitStack() as ctx:
        sb = lambda where, name, shape: where.enter_context(nc.sbuf_tensor(name, shape, F32))
        keep = {"ident": sb(ctx, "ident", [P, P]),
                "heads": sb(ctx, "heads_all", [P, KC, TOK])}
        with ExitStack() as inner:
            keep["headmask"] = sb(inner, "headmask", [P, HG * LQ])
            project_queries(nc, dram, keep)
            cross_attention(nc, dram, keep)
        keep["x_all"] = sb(ctx, "x_all", [P, NT, D])
        gated_attention(nc, dram, keep)
        experts(nc, dram, keep, out)


def laid_out(inputs):
    c = np.ascontiguousarray
    a = {k: np.asarray(v) for k, v in inputs.items()}
    repeated = lambda v: np.broadcast_to(v.reshape(1, -1), (P, v.size))
    rows = np.arange(P) // HD
    query = np.arange(P) % LQ
    f = np.float32
    r = {
        "x": a["x"].reshape(TOK, D),
        "ctxT": np.pad(a["ctx_1024"].transpose(0, 2, 1), ((0, 0), (0, 0), (0, 1))).reshape(B, KC, P, SP),
        "bias": a["fside_1x16xSxS2_0"].reshape(NPAIR, P, S),
        "wq": a["L0_xattn_wq"].reshape(D, D),
        "wk": a["L0_xattn_wk"].reshape(D, D),
        "wv": a["L0_xattn_wv"].reshape(D, D),
        "bq": a["L0_xattn_bq"].reshape(KC, P).T,
        "bk": a["L0_xattn_bk"].reshape(KC, P).T,
        "bv": a["L0_xattn_bv"].reshape(NPAIR, 2, HD).transpose(0, 2, 1).reshape(P, 2),
        "wo_x": a["L0_xattn_wo"].reshape(NPAIR, 2, HD, D).transpose(1, 0, 2, 3).reshape(D, D),
        "bo_x": repeated(a["L0_xattn_bo"]),
        "a_wq": a["L0_attn_Wq"],
        "a_wk": np.repeat(a["L0_attn_Wk"].reshape(D, KV, 1, DH), 2, axis=2).reshape(D, KV * 2 * DH),
        "a_wv": a["L0_attn_Wv"],
        "a_wg": a["L0_attn_Wg"],
        "a_wo": a["L0_attn_Wo"],
        "wr": a["L0_ffn_W_router"],
        "br": repeated(a["L0_ffn_b_router"]),
        "w1": a["L0_ffn_W1"],
        "w2": a["L0_ffn_W2"],
        "b1": a["L0_ffn_b1"].reshape(NE, FC, P).transpose(0, 2, 1),
        "b2": np.broadcast_to(a["L0_ffn_b2"][:, None, :], (NE, P, D)),
        "fold": ((np.arange(P)[:, None, None] // HD % QH == np.arange(QH)[None, :, None])
                 & (np.arange(P)[:, None, None] % HD == np.arange(HD)[None, None, :])).astype(f),
        "ident": np.eye(P, dtype=f),
        "headmask": np.repeat((rows[:, None] == np.arange(HG)[None, :]).astype(f), LQ, axis=1),
        "causal": np.tile(np.where(query[:, None] >= np.arange(LQ)[None, :], f(0), f(MASKED)), (1, GH)),
        "at_last": np.where(query == LQ - 1, f(1 / LQ), f(0))[:, None],
        "which": np.tile(np.arange(NE, dtype=f), (P, 1)),
    }
    return {k: c(v) for k, v in r.items()}


def kernel(**inputs):
    import concourse.bacc as bacc
    from concourse.bass_utils import run_bass_kernel_spmd

    arrays = laid_out(inputs)
    nc = bacc.Bacc("TRN2", target_bir_lowering=False, num_devices=1)
    dram = {name: nc.dram_tensor("in_" + name, v.shape, mybir.dt.from_np(v.dtype), kind="ExternalInput").ap()
            for name, v in arrays.items()}
    out = nc.dram_tensor("out", (TOK, D), F32, kind="ExternalOutput").ap()
    build_program(nc, dram, out)
    result = run_bass_kernel_spmd(nc, [{"in_" + name: v for name, v in arrays.items()}], core_ids=[0])
    return result.results[0]["out"].reshape(B, LQ, D)
```
